# Optimizing a Trainium2 kernel written in Bass

```python
import numpy as np
import jax
import jax.numpy as jnp

def _softmax(x, axis=-1):
    return jax.nn.softmax(x, axis=axis)

def _gelu(x):
    return jax.nn.gelu(x, approximate=True)

def _silu(x):
    return jax.nn.silu(x)

def _sigmoid(x):
    return jax.nn.sigmoid(x)

def _layernorm(x, axis=-1, eps=1e-05):
    m = jnp.mean(x, axis=axis, keepdims=True)
    v = jnp.var(x, axis=axis, keepdims=True)
    return (x - m) / jnp.sqrt(v + eps)

def _scatter_add(tgt, idx, src, axis=0):
    return tgt.at[idx].add(src)

def _segment_sum(src, seg, n):
    return jax.ops.segment_sum(src, seg, n)
kernel_name = 'mk_adaln_d2_jaxref_r8_ed875f'

def setup_inputs(seed: int=0):
    np.random.seed(seed)
    _w = jnp.asarray

    def _L0_attn_setup():
        import jax, jax.numpy as jnp
        import numpy as np
        HID = 128
        HEADS = 16
        HEAD_DIM = HID // HEADS
        key = jax.random.key(seed)
        ks = jax.random.split(key, 6)
        N, S = (4, 512)
        scale = 1.0 / np.sqrt(HID)
        return {'x': jax.random.normal(ks[0], (N, S, HID), dtype=jnp.float32), 'Wq': jax.random.normal(ks[1], (HID, HID), dtype=jnp.float32) * scale, 'Wk': jax.random.normal(ks[2], (HID, HID), dtype=jnp.float32) * scale, 'Wv': jax.random.normal(ks[3], (HID, HID), dtype=jnp.float32) * scale, 'Wo': jax.random.normal(ks[4], (HID, HID), dtype=jnp.float32) * scale, 'bo': jnp.zeros((HID,), dtype=jnp.float32)}
    _L0_attn_in = _L0_attn_setup()

    def _L0_ffn_setup():
        import jax, jax.numpy as jnp
        import numpy as np
        D = 128
        H = 16
        HD = D // H
        L = 64
        E = 8
        B, T = (4, 256)
        EPS = 1e-06

        def _glorot(k, shape):
            fan_in, fan_out = (shape[-2], shape[-1])
            lim = np.sqrt(6.0 / (fan_in + fan_out)).astype(np.float32)
            return jax.random.uniform(k, shape, jnp.float32, -lim, lim)

        def _rmsnorm(x, gamma):
            return gamma * x * jax.lax.rsqrt(jnp.mean(x * x, axis=-1, keepdims=True) + EPS)
        key = jax.random.key(seed)
        ks = jax.random.split(key, 8)
        return {'x': jax.random.normal(ks[0], (B, T, D), jnp.float32), 'gamma1': jnp.ones((D,), jnp.float32), 'Wq': _glorot(ks[1], (D, D)), 'bq': jnp.zeros((D,), jnp.float32), 'Wdown': _glorot(ks[2], (D, L)), 'bdown': jnp.zeros((L,), jnp.float32), 'Wup': _glorot(ks[3], (L, 2 * D)), 'bup': jnp.zeros((2 * D,), jnp.float32), 'Wo': _glorot(ks[4], (D, D)), 'bo': jnp.zeros((D,), jnp.float32), 'gamma2': jnp.ones((D,), jnp.float32), 'Wg': _glorot(ks[5], (D, E)), 'bg': jnp.zeros((E,), jnp.float32), 'We': _glorot(ks[6], (E, D, D))}
    _L0_ffn_in = _L0_ffn_setup()
    _L0_c = _w((lambda *s: np.random.randn(*s).astype(np.float32) * 0.05)(1, 128))
    _L0_wmod = _w((lambda *s: np.random.randn(*s).astype(np.float32) * 0.05)(128, 6 * 128) * 128 ** (-0.5))

    def _L1_attn_setup():
        import jax, jax.numpy as jnp
        import numpy as np
        import math
        B, N, D, K = (4, 512, 128, 8)
        key = jax.random.key(seed)
        ks = jax.random.split(key, 9)
        s = 0.02
        return {'summaries': jax.random.normal(ks[0], (B, N, D), dtype=jnp.float32), 'Wq': jax.random.normal(ks[1], (D, D), dtype=jnp.float32) * s, 'bq': jnp.zeros((D,), dtype=jnp.float32), 'Wk': jax.random.normal(ks[2], (D, D), dtype=jnp.float32) * s, 'bk': jnp.zeros((D,), dtype=jnp.float32), 'Wv': jax.random.normal(ks[3], (D, D), dtype=jnp.float32) * s, 'bv': jnp.zeros((D,), dtype=jnp.float32), 'Wo': jax.random.normal(ks[4], (D, D), dtype=jnp.float32) * s, 'bo': jnp.zeros((D,), dtype=jnp.float32)}
    _L1_attn_in = _L1_attn_setup()

    def _L1_ffn_setup():
        import jax, jax.numpy as jnp
        import numpy as np
        B, S, H = (4, 256, 128)
        D = 256
        E = 8
        K = 2
        key = jax.random.key(seed)
        ks = jax.random.split(key, 8)
        w = lambda k, shape: jax.random.normal(k, shape, jnp.float32) * 0.02
        return {'hidden_states': jax.random.normal(ks[0], (B, S, H), jnp.float32), 'gate_w': w(ks[1], (H, E)), 'w_gate': w(ks[2], (E, H, D)), 'w_up': w(ks[3], (E, H, D)), 'w_down': w(ks[4], (E, D, H)), 'ws_gate': w(ks[5], (H, D)), 'ws_up': w(ks[6], (H, D)), 'ws_down': w(ks[7], (D, H))}
    _L1_ffn_in = _L1_ffn_setup()
    _L1_c = _w((lambda *s: np.random.randn(*s).astype(np.float32) * 0.05)(1, 128))
    _L1_wmod = _w((lambda *s: np.random.randn(*s).astype(np.float32) * 0.05)(128, 6 * 128) * 128 ** (-0.5))
    _d = {'L0_attn_x': _L0_attn_in['x'], 'L0_attn_Wq': _L0_attn_in['Wq'], 'L0_attn_Wk': _L0_attn_in['Wk'], 'L0_attn_Wv': _L0_attn_in['Wv'], 'L0_attn_Wo': _L0_attn_in['Wo'], 'L0_attn_bo': _L0_attn_in['bo'], 'L0_ffn_gamma1': _L0_ffn_in['gamma1'], 'L0_ffn_Wq': _L0_ffn_in['Wq'], 'L0_ffn_bq': _L0_ffn_in['bq'], 'L0_ffn_Wdown': _L0_ffn_in['Wdown'], 'L0_ffn_bdown': _L0_ffn_in['bdown'], 'L0_ffn_Wup': _L0_ffn_in['Wup'], 'L0_ffn_bup': _L0_ffn_in['bup'], 'L0_ffn_Wo': _L0_ffn_in['Wo'], 'L0_ffn_bo': _L0_ffn_in['bo'], 'L0_ffn_gamma2': _L0_ffn_in['gamma2'], 'L0_ffn_Wg': _L0_ffn_in['Wg'], 'L0_ffn_bg': _L0_ffn_in['bg'], 'L0_ffn_We': _L0_ffn_in['We'], 'L0_c': _L0_c, 'L0_wmod': _L0_wmod, 'L1_attn_Wq': _L1_attn_in['Wq'], 'L1_attn_bq': _L1_attn_in['bq'], 'L1_attn_Wk': _L1_attn_in['Wk'], 'L1_attn_bk': _L1_attn_in['bk'], 'L1_attn_Wv': _L1_attn_in['Wv'], 'L1_attn_bv': _L1_attn_in['bv'], 'L1_attn_Wo': _L1_attn_in['Wo'], 'L1_attn_bo': _L1_attn_in['bo'], 'L1_ffn_gate_w': _L1_ffn_in['gate_w'], 'L1_ffn_w_gate': _L1_ffn_in['w_gate'], 'L1_ffn_w_up': _L1_ffn_in['w_up'], 'L1_ffn_w_down': _L1_ffn_in['w_down'], 'L1_ffn_ws_gate': _L1_ffn_in['ws_gate'], 'L1_ffn_ws_up': _L1_ffn_in['ws_up'], 'L1_ffn_ws_down': _L1_ffn_in['ws_down'], 'L1_c': _L1_c, 'L1_wmod': _L1_wmod}
    _x0 = _d['L0_attn_x']
    _d['L0_attn_x'] = jax.random.normal(jax.random.fold_in(jax.random.key(seed), 1), (1, 2048, 128), dtype=_x0.dtype)
    del _x0
    return _d

def reference(L0_attn_x, L0_attn_Wq, L0_attn_Wk, L0_attn_Wv, L0_attn_Wo, L0_attn_bo, L0_ffn_gamma1, L0_ffn_Wq, L0_ffn_bq, L0_ffn_Wdown, L0_ffn_bdown, L0_ffn_Wup, L0_ffn_bup, L0_ffn_Wo, L0_ffn_bo, L0_ffn_gamma2, L0_ffn_Wg, L0_ffn_bg, L0_ffn_We, L0_c, L0_wmod, L1_attn_Wq, L1_attn_bq, L1_attn_Wk, L1_attn_bk, L1_attn_Wv, L1_attn_bv, L1_attn_Wo, L1_attn_bo, L1_ffn_gate_w, L1_ffn_w_gate, L1_ffn_w_up, L1_ffn_w_down, L1_ffn_ws_gate, L1_ffn_ws_up, L1_ffn_ws_down, L1_c, L1_wmod):

    def _L0_attn_ref(x, Wq, Wk, Wv, Wo, bo):
        import jax, jax.numpy as jnp
        import numpy as np
        HID = 128
        HEADS = 16
        HEAD_DIM = HID // HEADS
        N, S, _ = x.shape
        q = (x @ Wq).reshape(N, S, HEADS, HEAD_DIM)
        k = (x @ Wk).reshape(N, S, HEADS, HEAD_DIM)
        v = (x @ Wv).reshape(N, S, HEADS, HEAD_DIM)
        q = jnp.swapaxes(q, 1, 2)
        k = jnp.swapaxes(k, 1, 2)
        v = jnp.swapaxes(v, 1, 2)
        energy = jnp.einsum('nahd,nbhd->nab', q, k)
        attention = jax.nn.softmax(energy / np.sqrt(HEAD_DIM), axis=2)
        out = jnp.einsum('nab,nbsd->nasd', attention, v)
        out = out.reshape(N, S, HID)
        return out @ Wo + bo

    def _L0_ffn_ref(x, gamma1, Wq, bq, Wdown, bdown, Wup, bup, Wo, bo, gamma2, Wg, bg, We):
        import jax, jax.numpy as jnp
        import numpy as np
        D = 128
        H = 16
        HD = D // H
        L = 64
        E = 8
        B, T = (4, 256)
        EPS = 1e-06

        def _glorot(k, shape):
            fan_in, fan_out = (shape[-2], shape[-1])
            lim = np.sqrt(6.0 / (fan_in + fan_out)).astype(np.float32)
            return jax.random.uniform(k, shape, jnp.float32, -lim, lim)

        def _rmsnorm(x, gamma):
            return gamma * x * jax.lax.rsqrt(jnp.mean(x * x, axis=-1, keepdims=True) + EPS)
        b, t = (x.shape[0], x.shape[1])
        h = _rmsnorm(x, gamma1)
        q = (h @ Wq + bq).reshape(b, t, H, HD)
        kv = ((h @ Wdown + bdown) @ Wup + bup).reshape(b, t, H, 2 * HD)
        k, v = jnp.split(kv, 2, axis=-1)
        att = jnp.einsum('bthd,btgd->bthg', q, k) / np.sqrt(HD).astype(np.float32)
        att = jax.nn.softmax(att, axis=-1)
        out = jnp.einsum('bthg,btgd->bthd', att, v).reshape(b, t, D)
        x = x + (out @ Wo + bo)
        h2 = _rmsnorm(x, gamma2)
        gate = jax.nn.softmax(h2 @ Wg + bg, axis=-1)
        combined = jnp.einsum('btd,edf,bte->btf', h2, We, gate)
        return x + combined

    def _L1_attn_ref(summaries, Wq, bq, Wk, bk, Wv, bv, Wo, bo):
        import jax, jax.numpy as jnp
        import numpy as np
        import math
        B, N, D, K = (4, 512, 128, 8)
        b_, n_, d_ = summaries.shape
        q = summaries @ Wq + bq
        k = summaries @ Wk + bk
        v = summaries @ Wv + bv
        scores = jnp.einsum('bnd,bmd->bnm', q, k) / math.sqrt(d_)
        causal = jnp.triu(jnp.full((n_, n_), -jnp.inf, dtype=scores.dtype), k=1)
        scores = scores + causal
        topk_vals, topk_idx = jax.lax.top_k(scores, K)
        bi = jnp.arange(b_)[:, None, None]
        ri = jnp.arange(n_)[None, :, None]
        sparse = jnp.full_like(scores, -jnp.inf).at[bi, ri, topk_idx].set(topk_vals)
        attn = jax.nn.softmax(sparse, axis=-1)
        out = jnp.einsum('bnm,bmd->bnd', attn, v)
        return out @ Wo + bo

    def _L1_ffn_ref(hidden_states, gate_w, w_gate, w_up, w_down, ws_gate, ws_up, ws_down):
        import jax, jax.numpy as jnp
        import numpy as np
        B, S, H = (4, 256, 128)
        D = 256
        E = 8
        K = 2
        b, s, h = hidden_states.shape
        x = hidden_states.reshape(-1, h)
        scores = jax.nn.softmax(x @ gate_w, axis=-1)
        topk_w, topk_idx = jax.lax.top_k(scores, K)
        topk_w = topk_w / (jnp.sum(topk_w, axis=-1, keepdims=True) + 1e-20)
        onehot = jax.nn.one_hot(topk_idx, E, dtype=x.dtype)
        w_per_expert = jnp.einsum('nke,nk->ne', onehot, topk_w)
        y = jnp.zeros_like(x)
        for e in range(E):
            hid = jax.nn.silu(x @ w_gate[e]) * (x @ w_up[e])
            y = y + w_per_expert[:, e:e + 1] * (hid @ w_down[e])
        shared = jax.nn.silu(x @ ws_gate) * (x @ ws_up) @ ws_down
        return (y + shared).reshape(b, s, h)
    x = L0_attn_x
    mod = (_silu(L0_c) @ L0_wmod).reshape(L0_c.shape[0], 6, 1, -1)
    sa, ca, ga, sb, cb, gb = (mod[:, 0], mod[:, 1], mod[:, 2], mod[:, 3], mod[:, 4], mod[:, 5])
    ga = (2 * (ga >= 0) - 1) * jnp.maximum(jnp.abs(ga), 0.25)
    gb = (2 * (gb >= 0) - 1) * jnp.maximum(jnp.abs(gb), 0.25)
    h = _layernorm(x, axis=-1) * (1 + ca) + sa
    x = x + ga * _L0_attn_ref(h, L0_attn_Wq, L0_attn_Wk, L0_attn_Wv, L0_attn_Wo, L0_attn_bo)
    h = _layernorm(x, axis=-1) * (1 + cb) + sb
    x = x + gb * _L0_ffn_ref(h, L0_ffn_gamma1, L0_ffn_Wq, L0_ffn_bq, L0_ffn_Wdown, L0_ffn_bdown, L0_ffn_Wup, L0_ffn_bup, L0_ffn_Wo, L0_ffn_bo, L0_ffn_gamma2, L0_ffn_Wg, L0_ffn_bg, L0_ffn_We)
    mod = (_silu(L1_c) @ L1_wmod).reshape(L1_c.shape[0], 6, 1, -1)
    sa, ca, ga, sb, cb, gb = (mod[:, 0], mod[:, 1], mod[:, 2], mod[:, 3], mod[:, 4], mod[:, 5])
    ga = (2 * (ga >= 0) - 1) * jnp.maximum(jnp.abs(ga), 0.25)
    gb = (2 * (gb >= 0) - 1) * jnp.maximum(jnp.abs(gb), 0.25)
    h = _layernorm(x, axis=-1) * (1 + ca) + sa
    x = x + ga * _L1_attn_ref(h, L1_attn_Wq, L1_attn_bq, L1_attn_Wk, L1_attn_bk, L1_attn_Wv, L1_attn_bv, L1_attn_Wo, L1_attn_bo)
    h = _layernorm(x, axis=-1) * (1 + cb) + sb
    x = x + gb * _L1_ffn_ref(h, L1_ffn_gate_w, L1_ffn_w_gate, L1_ffn_w_up, L1_ffn_w_down, L1_ffn_ws_gate, L1_ffn_ws_up, L1_ffn_ws_down)
    return x

_drawn_inputs = setup_inputs


def setup_inputs(seed=0):
    import zlib

    import numpy as np

    out = dict(_drawn_inputs(seed))
    spreads = {'L0_attn_bo': (0.0, 0.345),
     'L0_ffn_gamma1': (1.0, 0.6),
     'L0_ffn_bq': (0.0, 0.8),
     'L0_ffn_bdown': (0.0, 0.8),
     'L0_ffn_bup': (0.0, 0.601),
     'L0_ffn_bo': (0.0, 0.27),
     'L0_ffn_gamma2': (1.0, 0.2),
     'L0_ffn_bg': (0.0, 0.8),
     'L1_attn_bq': (0.0, 0.8),
     'L1_attn_bk': (0.0, 0.8),
     'L1_attn_bv': (0.0, 0.8),
     'L1_attn_bo': (0.0, 0.354)}
    factors = {'L1_attn_Wq': 8.0,
     'L1_attn_Wk': 8.0,
     'L1_attn_Wv': 8.0,
     'L1_attn_Wo': 7.109,
     'L1_ffn_gate_w': 8.0,
     'L1_ffn_w_gate': 8.0,
     'L1_ffn_w_up': 8.0,
     'L1_ffn_w_down': 8.0,
     'L1_ffn_ws_gate': 8.0,
     'L1_ffn_ws_up': 8.0,
     'L1_ffn_ws_down': 8.0}
    for name, (base, spread) in spreads.items():
        noise = np.random.default_rng([zlib.crc32(name.encode()), seed]).standard_normal(out[name].shape)
        drawn = base * np.exp(spread * noise) if base else spread * noise
        out[name] = jnp.asarray(drawn.astype(out[name].dtype))
    for name, factor in factors.items():
        out[name] = (out[name] * factor).astype(out[name].dtype)
    return out
```

```python
from contextlib import ExitStack

import concourse.bass as bass
from concourse import mybir

ALU = mybir.AluOpType
ACT = mybir.ActivationFunctionType
F32 = mybir.dt.float32
U32 = mybir.dt.uint32
AX = mybir.AxisListType

P = 128
NB = 16
H = 16
HD = P // H
E = 8
HID = 256
TOPK = 8
LN_EPS = 1e-5
RMS_EPS = 1e-6
MASKED = -1e30
PICKED = -3e38
CH = 512


def build(nc, d, out):
    with ExitStack() as ctx:
        def sb(name, shape, dt=F32):
            return ctx.enter_context(nc.sbuf_tensor(name, shape, dt))

        def sem(name):
            return ctx.enter_context(nc.semaphore(name))

        bank = [ctx.enter_context(nc.psum_tensor(f"bank{i}", [P, CH], F32)) for i in range(8)]
        gu_bank = bank[0:2]
        y_bank = bank[2]
        att_bank = bank[3:5]
        a_bank = bank[5]
        f_bank = bank[6]
        fe_bank = bank[7]

        ident = sb("ident", [P, P])
        ones = sb("ones", [P, P])
        neg_half = sb("neg_half", [P, NB])
        iota8 = sb("iota8", [P, E])
        head_rows = sb("head_rows", [H, P])
        head_cols = sb("head_cols", [P, H])
        lane_rows = sb("lane_rows", [HD, H, HD])
        same_lane = sb("same_lane", [P, P])

        S = sb("S", [P, NB * P])
        R = sb("R", [P, NB * P])
        X = sb("X", [P, NB * P])
        PT = sb("PT", [P, NB * P])

        x_blk = sb("x_blk", [P, NB, P])
        c_col = sb("c_col", [P, 2])
        wmod = sb("wmod", [P, 2, 6 * P])
        w0q = sb("w0q", [P, P])
        w0k = sb("w0k", [P, P])
        w0v = sb("w0v", [P, P])
        w0o = sb("w0o", [P, P])
        rows = sb("rows", [P, 6, P])
        bup_row = sb("bup_row", [P, 2 * P])
        bg_row = sb("bg_row", [P, E])
        cols = sb("cols", [P, 8])
        wfq = sb("wfq", [P, P])
        wdown = sb("wdown", [P, 64])
        wup = sb("wup", [64, 2 * P])
        wfo = sb("wfo", [P, P])
        wfg = sb("wfg", [P, E])
        wfe = sb("wfe", [P, E, P])
        w1q = sb("w1q", [P, P])
        w1k = sb("w1k", [P, P])
        w1v = sb("w1v", [P, P])
        w1o = sb("w1o", [P, P])
        w1r = sb("w1r", [P, E])
        wgate = sb("wgate", [P, E + 1, HID])
        wups = sb("wups", [P, E + 1, HID])
        wdn = sb("wdn", [P, E + 1, 2, P])

        silu_t = sb("silu_t", [P, 2])
        silu_c = sb("silu_c", [P, 2])
        silu_b = sb("silu_b", [P, 2, P])
        mod0 = sb("mod0", [P, 6, P])
        mod1 = sb("mod1", [P, 2, P])
        mcol = sb("mcol", [P, 4])
        gsign = sb("gsign", [P, 4, P])
        gmag = sb("gmag", [P, 4, P])
        w0oG = sb("w0oG", [P, P])
        bo0G = sb("bo0G", [P, P])
        w0vT = sb("w0vT", [P, P])
        wdownT = sb("wdownT", [64, P])
        wqkv = sb("wqkv", [P, 3 * P])
        bqkv = sb("bqkv", [P, 3 * P])
        bkv = sb("bkv", [P, 2 * P])
        bcols = sb("bcols", [P, 2, P])
        wfeG = wfe
        wfgG = sb("wfgG", [P, E])
        w1vT = sb("w1vT", [P, P])
        w1vo = sb("w1vo", [P, P])
        bvo = sb("bvo", [P, P])
        bo1G = sb("bo1G", [P, P])
        wdnG = wdn

        st0 = sb("st0", [P, NB, 6])
        mv0 = sb("mv0", [P, NB, 2])
        rs0 = sb("rs0", [P, NB])
        x_str, h_tmp, h_str, hT_str = (
            t[:].rearrange("p (j f) -> p j f", j=NB) for t in (S, R, X, PT))
        gram = sb("gram", [P, P])
        gramk = sb("gramk", [P, P])
        qk_m = sb("qk_m", [P, P])
        qk_r = sb("qk_r", [P, H])
        hsc = sb("hsc", [H, H])
        hmx = sb("hmx", [H, 4])
        hatt = sb("hatt", [H, H])
        hspread = sb("hspread", [H, P])
        hmix = sb("hmix", [P, P])
        w0vA = sb("w0vA", [P, P])
        mixed = sb("mixed", [P, NB, P])

        xT = sb("xT", [P, P])
        x1 = sb("x1", [P, NB, P])
        stF = sb("stF", [P, NB, 6])
        mvF = sb("mvF", [P, NB, 2])
        rsF = sb("rsF", [P, NB])
        nF = sb("nF", [P, P])
        hF1 = sb("hF1", [P, P])
        hF = sb("hF", [P, P])
        hFb = sb("hFb", [P, P])
        hFT = sb("hFT", [P, P])
        sq_junk = sb("sq_junk", [P, P])
        ssqF = sb("ssqF", [P, NB, 2])
        rmsF = sb("rmsF", [P, NB, 2])
        qkvF = sb("qkvF", [P, 3 * P])
        prod = sb("prod", [P, H * P])
        scF = sb("scF", [P, H, H])
        mxF = sb("mxF", [P, H])
        peF = sb("peF", [P, H, H])
        sumF = sb("sumF", [P, H])
        rinF = sb("rinF", [P, H])
        oF = sb("oF", [P, H, HD])
        onF = sb("onF", [P, H, HD])
        oFT = sb("oFT", [P, P])
        zF = sb("zF", [P, P])
        zg = sb("zg", [P, P])
        zFT = sb("zFT", [P, P])
        lgF = sb("lgF", [P, E])
        nmF = sb("nmF", [P, 1])
        geF = sb("geF", [P, E])
        gsF = sb("gsF", [P, 2])
        wtF = sb("wtF", [P, E])
        accF = sb("accF", [P, 2, P])
        x2 = sb("x2", [P, NB, P])

        stA = sb("stA", [P, NB, 2, 6])
        mvA = sb("mvA", [P, NB, 2, 2])
        rsA = sb("rsA", [P, NB, 2])
        nA = sb("nA", [P, 2, P])
        hAT = sb("hAT", [P, P])
        qT = sb("qT", [P, P])
        kT = sb("kT", [P, NB * P])
        vA = sb("vA", [P, NB, P])
        top = sb("top", [P, TOPK])
        nmA = sb("nmA", [P, 1])
        sumA = sb("sumA", [P, 2])
        x2b = sb("x2b", [P, P])
        x3 = sb("x3", [P, NB, P])
        h2T = sb("h2T", [P, 2, P])
        lgR = sb("lgR", [P, E])
        nmR = sb("nmR", [P, 1])
        peR = sb("peR", [P, E])
        suR = sb("suR", [P, 4])
        prR = sb("prR", [P, E])
        tpR = sb("tpR", [P, E])
        ixR = sb("ixR", [P, E], U32)
        ifR = sb("ifR", [P, E])
        mkR = sb("mkR", [P, 2, E])
        wtR = sb("wtR", [P, NB, E])

        th = sb("th", [P, 2, HID])
        gg = sb("gg", [P, 2, HID])
        hid = sb("hid", [P, 2, HID])
        acc = sb("acc", [P, 2, P])
        x4 = sb("x4", [P, NB, P])

        in_xa, in_xb, in_c, in_mod, in_w0, in_f, in_fe, in_1, in_moe, in_rows = (
            sem(n) for n in ("in_xa", "in_xb", "in_c", "in_mod", "in_w0", "in_f", "in_fe", "in_1", "in_moe", "in_rows"))
        stored = sem("stored")
        consts = sem("consts")
        pool_chain, dve_chain, act_chain = sem("pool_chain"), sem("dve_chain"), sem("act_chain")
        (silu_tanh, silu_rows, mod0_mm, mod0_sb, mod1_mm, mod1_sb, col_mm, col_sb, lane_mm, lane_sb, tr_mm, tr_sb,
         fold_mm, gates_ready, prep_dve, bcol_ready, mods_first) = (
            sem(n) for n in ("silu_tanh", "silu_rows", "mod0_mm", "mod0_sb", "mod1_mm", "mod1_sb", "col_mm", "col_sb",
                             "lane_mm", "lane_sb", "tr_mm", "tr_sb", "fold_mm", "gates_ready", "prep_dve",
                             "bcol_ready", "mods_first"))
        (var0, rstd0, scaled0, h0_ready, gram_mm, gram_sb, gramk_mm, gramk_sb, qk_mm, qkr_ready, hsc_mm, hneg,
         hexp, hatt_ready, hspr_mm, hspr_sb, hmix_mm, hmix_sb, wva_mm, wva_sb, hT0_mm, hT0_sb, z0_mm, z0_sb,
         xb_ready) = (
            sem(n) for n in ("var0", "rstd0", "scaled0", "h0_ready", "gram_mm", "gram_sb", "gramk_mm", "gramk_sb",
                             "qk_mm", "qkr_ready", "hsc_mm", "hneg", "hexp", "hatt_ready", "hspr_mm", "hspr_sb",
                             "hmix_mm", "hmix_sb", "wva_mm", "wva_sb", "hT0_mm", "hT0_sb", "z0_mm", "z0_sb",
                             "xb_ready"))
        (f_xt_mm, f_xt_sb, f_wo_mm, f_var, f_rstd, f_n_done, f_h_ready, f_hb_ready, f_ht_mm, f_ht_sb, f_ssq, f_rms,
         f_qkv_mm, f_qkv_sb, f_sc_ready, f_exp_done, f_o_ready, f_ot_mm, f_ot_sb, f_y_mm, f_z_ready, f_zt_mm,
         f_zt_sb, f_ssq2, f_rms2, f_lg_mm, f_lg_ready, f_ge_done, f_e1_mm, f_e2_mm, f_e1_read, f_base, f_x2) = (
            sem(n) for n in ("f_xt_mm", "f_xt_sb", "f_wo_mm", "f_var", "f_rstd", "f_n_done", "f_h_ready",
                             "f_hb_ready", "f_ht_mm", "f_ht_sb", "f_ssq", "f_rms", "f_qkv_mm", "f_qkv_sb",
                             "f_sc_ready", "f_exp_done", "f_o_ready", "f_ot_mm", "f_ot_sb", "f_y_mm", "f_z_ready",
                             "f_zt_mm", "f_zt_sb", "f_ssq2", "f_rms2", "f_lg_mm", "f_lg_ready", "f_ge_done",
                             "f_e1_mm", "f_e2_mm", "f_e1_read", "f_base", "f_x2"))
        (a_var, a_rstd, a_n_done, a_ht_mm, a_ht_sb, a_qkv_mm, a_qk_sb, a_v_sb, a_sc_mm, a_sc_sb, a_masked, a_top,
         a_exp_done, a_picked, a_p_ready, a_pt_mm, a_pt_sb, a_o_mm, a_base, a_x3, a_var2, a_rstd2, a_n2_done,
         a_h2_mm, a_h2_sb, a_lg_mm, a_lg_ready, a_ge_done, a_w_ready) = (
            sem(n) for n in ("a_var", "a_rstd", "a_n_done", "a_ht_mm", "a_ht_sb", "a_qkv_mm", "a_qk_sb", "a_v_sb",
                             "a_sc_mm", "a_sc_sb", "a_masked", "a_top", "a_exp_done", "a_picked", "a_p_ready",
                             "a_pt_mm", "a_pt_sb", "a_o_mm", "a_base", "a_x3", "a_var2", "a_rstd2", "a_n2_done",
                             "a_h2_mm", "a_h2_sb", "a_lg_mm", "a_lg_ready", "a_ge_done", "a_w_ready"))
        m_gu_mm, m_tanh, m_hid, m_y_mm, m_y_read, m_out = (
            sem(n) for n in ("m_gu_mm", "m_tanh", "m_hid", "m_y_mm", "m_y_read", "m_out"))

        NE = E + 1

        def chunks(a):
            return [(c * CH, min(CH, (a + 1) * P - c * CH)) for c in range(((a + 1) * P + CH - 1) // CH)]

        chunks_before = [sum(len(chunks(b)) for b in range(a)) for a in range(NB + 1)]

        def att_use(a, k, c):
            return 2 * chunks_before[a] + k * len(chunks(a)) + c

        def row(ap, n):
            return ap.rearrange("(o n) -> o n", o=1).broadcast_to([P, n])

        def over_blocks(ap, n):
            return ap.rearrange("p (o f) -> p o f", o=1).broadcast_to([P, n, P])

        def f_blocks(s):
            return s if s < NB else None

        STEPS = NB + 2
        block = ctx.enter_context(nc.Block())

        @block.sync
        def _(sp):
            x = d["L0_attn_x"].rearrange("o t f -> (o t) f")
            sp.dma_start(x_str[:, 0:8, :], x.rearrange("(r j) f -> r j f", j=NB)[:, 0:8, :]).then_inc(in_xa, 16)
            sp.dma_start(x_str[:, 8:16, :], x.rearrange("(r j) f -> r j f", j=NB)[:, 8:16, :]).then_inc(in_xb, 16)
            sp.dma_start(w0q[:], d["L0_attn_Wq"]).then_inc(in_w0, 16)
            sp.dma_start(w0k[:], d["L0_attn_Wk"]).then_inc(in_w0, 16)
            sp.dma_start(w0v[:], d["L0_attn_Wv"]).then_inc(in_w0, 16)
            sp.dma_start(w0o[:], d["L0_attn_Wo"]).then_inc(in_w0, 16)
            sp.dma_start(x_blk[:], x.rearrange("(j r) f -> r j f", r=P)).then_inc(in_w0, 16)
            sp.dma_start(wdown[:], d["L0_ffn_Wdown"]).then_inc(in_f, 16)
            sp.dma_start(wup[:], d["L0_ffn_Wup"]).then_inc(in_f, 16)
            sp.dma_start(wfq[:], d["L0_ffn_Wq"]).then_inc(in_f, 16)
            sp.dma_start(wfo[:], d["L0_ffn_Wo"]).then_inc(in_f, 16)
            sp.dma_start(wfg[:], d["L0_ffn_Wg"]).then_inc(in_f, 16)
            sp.dma_start(wfe[:], d["L0_ffn_We"].rearrange("e i f -> i e f")).then_inc(in_f, 16)
            for t, n in ((w1q, "L1_attn_Wq"), (w1k, "L1_attn_Wk"), (w1v, "L1_attn_Wv"), (w1o, "L1_attn_Wo"),
                         (w1r, "L1_ffn_gate_w")):
                sp.dma_start(t[:], d[n]).then_inc(in_1, 16)
            sp.dma_start(wgate[:, 0:E, :], d["L1_ffn_w_gate"].rearrange("e i f -> i e f")).then_inc(in_moe, 16)
            sp.dma_start(wups[:, 0:E, :], d["L1_ffn_w_up"].rearrange("e i f -> i e f")).then_inc(in_moe, 16)
            sp.dma_start(wdn[:, 0:E, :, :],
                         d["L1_ffn_w_down"].rearrange("e (c r) f -> r e c f", r=P)).then_inc(in_moe, 16)
            sp.dma_start(wgate[:, E, :], d["L1_ffn_ws_gate"]).then_inc(in_moe, 16)
            sp.dma_start(wups[:, E, :], d["L1_ffn_ws_up"]).then_inc(in_moe, 16)
            sp.dma_start(wdn[:, E, :, :], d["L1_ffn_ws_down"].rearrange("(c r) f -> r c f", r=P)).then_inc(in_moe, 16)
            o = out.rearrange("o (b r) f -> (o b) r f", r=P)
            for m in range(NB):
                sp.wait_ge(m_out, m + 1)
                sp.dma_start(o[m], x4[:, m, :]).then_inc(stored, 16)
            sp.wait_ge(stored, 16 * NB)

        @block.gpsimd
        def _(pool):
            n = [0]

            def link(ins):
                n[0] += 1
                ins.then_inc(pool_chain, 1)
                pool.wait_ge(pool_chain, n[0])

            g = nc.gpsimd
            g.memset(ones[:], 1.0)
            g.memset(neg_half[:], -0.5)
            g.memset(head_rows[:], 1.0)
            g.memset(head_cols[:], 1.0)
            g.memset(lane_rows[:], 0.0)
            link(g.memset(ident[:], 0.0))
            g.affine_select(out=ident[:], in_=ident[:], compare_op=ALU.not_equal, fill=1.0, base=0,
                            pattern=[[-1, P]], channel_multiplier=1)
            g.affine_select(out=head_rows[:], in_=head_rows[:], compare_op=ALU.is_ge, fill=0.0, base=0,
                            pattern=[[1, P]], channel_multiplier=-HD)
            g.affine_select(out=head_cols[:], in_=head_cols[:], compare_op=ALU.is_ge, fill=0.0, base=0,
                            pattern=[[-HD, H]], channel_multiplier=1)
            link(g.affine_select(out=lane_rows[:], in_=lane_rows[:], compare_op=ALU.not_equal, fill=1.0, base=0,
                                 pattern=[[0, H], [1, HD]], channel_multiplier=-1))
            g.affine_select(out=head_rows[:], in_=head_rows[:], compare_op=ALU.is_ge, fill=0.0, base=HD - 1,
                            pattern=[[-1, P]], channel_multiplier=HD)
            g.affine_select(out=head_cols[:], in_=head_cols[:], compare_op=ALU.is_ge, fill=0.0, base=HD - 1,
                            pattern=[[HD, H]], channel_multiplier=-1)
            g.iota(iota8[:], pattern=[[1, E]], base=0, channel_multiplier=0,
                   allow_small_or_imprecise_dtypes=True).then_inc(consts, 1)

            def rsqrt(out, var, scale, eps, done):
                link(g.tensor_scalar(out, var, scale, eps, ALU.mult, ALU.add))
                g.tensor_tensor(out, out, neg_half[:, 0:out.shape[1]], ALU.pow).then_inc(done, 1)

            pool.wait_ge(var0, 1)
            rsqrt(rs0[:], mv0[:, :, 1], 1.0, LN_EPS, rstd0)
            for q in range(4):
                pool.wait_ge(scaled0, q + 1)
                j = slice(4 * q, 4 * q + 4)
                g.tensor_tensor(h_str[:, j, :], h_tmp[:, j, :], over_blocks(mod0[:, 0, :], 4),
                                ALU.add).then_inc(h0_ready, 1)
            pool.wait_ge(in_w0, 80)
            pool.wait_ge(gates_ready, 1)
            for q in range(4):
                j = slice(4 * q, 4 * q + 4)
                g.tensor_tensor(x_blk[:, j, :], x_blk[:, j, :], over_blocks(bo0G[:], 4), ALU.add).then_inc(xb_ready, 1)

            def f_norm(f):
                pool.wait_ge(f_var, f + 1)
                rsqrt(rsF[:, f:f + 1], mvF[:, f, 1:2], 1.0, LN_EPS, f_rstd)

            def f_modulate(f):
                pool.wait_ge(f_n_done, f + 1)
                if f >= 1:
                    pool.wait_ge(f_ssq, f)
                    pool.wait_ge(f_z_ready, f)
                link(g.tensor_tensor(hF1[:], nF[:], mod0[:, 4, :], ALU.mult))
                g.tensor_tensor(hF[:], hF1[:], mod0[:, 3, :], ALU.add).then_inc(f_h_ready, 1)
                pool.wait_ge(f_h_ready, f + 1)
                g.tensor_tensor(hFb[:], hF[:], rows[:, 2, :], ALU.add).then_inc(f_hb_ready, 1)

            def f_rms1(f):
                pool.wait_ge(f_ssq, f + 1)
                rsqrt(rmsF[:, f, 0:1], ssqF[:, f, 0:1], 1.0 / P, RMS_EPS, f_rms)

            def f_rms2_(f):
                pool.wait_ge(f_ssq2, f + 1)
                rsqrt(rmsF[:, f, 1:2], ssqF[:, f, 1:2], 1.0 / P, RMS_EPS, f_rms2)

            def f_base_(f):
                pool.wait_ge(f_z_ready, f + 1)
                link(g.tensor_tensor(zg[:], zF[:], mod0[:, 5, :], ALU.mult))
                if f >= 1:
                    pool.wait_ge(f_x2, f)
                g.tensor_tensor(accF[:, 0, :], zg[:], x1[:, f, :], ALU.add).then_inc(f_base, 1)

            def a_norm(a, k):
                pool.wait_ge((a_var, a_var2)[k], a + 1)
                rsqrt(rsA[:, a, k:k + 1], mvA[:, a, k, 1:2], 1.0, LN_EPS, (a_rstd, a_rstd2)[k])

            def a_base_(a):
                pool.wait_ge(f_x2, a + 1)
                if a == 0:
                    pool.wait_ge(prep_dve, 1)
                if a >= 1:
                    pool.wait_ge(a_x3, a)
                g.tensor_tensor(x2b[:], x2[:, a, :], bo1G[:], ALU.add).then_inc(a_base, 1)

            def a_mask(a):
                pool.wait_ge(a_sc_sb, chunks_before[a + 1])
                diag = S[:, a * P:(a + 1) * P]
                g.affine_select(out=diag, in_=diag, compare_op=ALU.is_ge, fill=MASKED, base=0,
                                pattern=[[-1, P]], channel_multiplier=1).then_inc(a_masked, 1)

            for s in range(STEPS):
                f, a = s, s - 1
                if 0 <= a < NB:
                    a_norm(a, 0)
                    a_base_(a)
                if f < NB:
                    f_norm(f)
                    f_modulate(f)
                    f_rms1(f)
                if 0 <= a < NB:
                    a_mask(a)
                    a_norm(a, 1)
                if f < NB:
                    f_rms2_(f)
                    f_base_(f)

        @block.scalar
        def _(act):
            n = [0]

            def link(ins):
                n[0] += 1
                ins.then_inc(act_chain, 1)
                act.wait_ge(act_chain, n[0])

            sc = nc.scalar
            act.dma_start(c_col[:, 0:1], d["L0_c"].rearrange("o f -> f o")).then_inc(in_c, 16)
            act.dma_start(c_col[:, 1:2], d["L1_c"].rearrange("o f -> f o")).then_inc(in_c, 16)
            act.dma_start(wmod[:, 0, :], d["L0_wmod"]).then_inc(in_mod, 16)
            act.dma_start(wmod[:, 1, :], d["L1_wmod"]).then_inc(in_mod, 16)
            for k, name in enumerate(("L0_attn_bo", "L0_ffn_bq", "L0_ffn_bo", "L1_attn_bo")):
                act.dma_start(rows[:, k, :], row(d[name], P)).then_inc(in_rows, 16)
            act.dma_start(bup_row[:], row(d["L0_ffn_bup"], 2 * P)).then_inc(in_rows, 16)
            act.dma_start(bg_row[:], row(d["L0_ffn_bg"], E)).then_inc(in_rows, 16)
            for k, name in enumerate(("L0_ffn_gamma1", "L0_ffn_gamma2", "L0_ffn_bdown", "L1_attn_bq", "L1_attn_bk",
                                      "L1_attn_bv")):
                m = d[name].shape[0]
                act.dma_start(cols[0:m, k:k + 1], d[name].rearrange("(f o) -> f o", o=1)).then_inc(in_rows, 16)

            act.wait_ge(in_c, 32)
            sc.activation(silu_t[:], c_col[:], ACT.Tanh, scale=0.5).then_inc(silu_tanh, 1)
            act.wait_ge(mod0_mm, 1)
            sc.copy(mod0[:, 0:3, :], bank[0][:, 0:3 * P].rearrange("p (c f) -> p c f", c=3))
            sc.copy(mod0[:, 3:6, :], bank[1][:, 0:3 * P].rearrange("p (c f) -> p c f", c=3)).then_inc(mod0_sb, 1)
            act.wait_ge(mod1_mm, 1)
            sc.copy(mod1[:], bank[2][:, 0:2 * P].rearrange("p (c f) -> p c f", c=2)).then_inc(mod1_sb, 1)
            act.wait_ge(col_mm, 1)
            sc.copy(mcol[:], bank[3][:, 0:4]).then_inc(col_sb, 1)
            act.wait_ge(lane_mm, 1)
            sc.copy(same_lane[:], bank[4][:, 0:P]).then_inc(lane_sb, 1)
            act.wait_ge(tr_mm, 1)
            sc.copy(w0vT[:], bank[5][:, 0:P])
            sc.copy(w1vT[:], bank[5][:, P:2 * P])
            sc.copy(wdownT[:], bank[5][0:64, 2 * P:3 * P]).then_inc(tr_sb, 1)
            for q in range(4):
                act.wait_ge(hT0_mm, q + 1)
                sc.copy(hT_str[:, 4 * q:4 * q + 4, :],
                        bank[q % 2][:].rearrange("p (j t) -> p j t", j=4)).then_inc(hT0_sb, 1)
            act.wait_ge(hneg, 1)
            sc.activation(hatt[:], hsc[:], ACT.Exp, bias=hmx[:, 1:2], scale=HD ** -0.5,
                          accum_out=hmx[:, 2:3]).then_inc(hexp, 1)
            for q in range(1, 4, 2):
                act.wait_ge(z0_mm, q + 1)
                sc.copy(mixed[:].rearrange("r a (j d) -> r j a d", j=NB)[:, 4 * q:4 * q + 4, :, :],
                        bank[4 + q][:].rearrange("r (j a d) -> r j a d", j=4, a=H)).then_inc(z0_sb, 1)

            def f_xt(f):
                act.wait_ge(f_xt_mm, f + 1)
                sc.copy(xT[:], f_bank[:, 0:P]).then_inc(f_xt_sb, 1)

            def f_ht(f):
                act.wait_ge(f_ht_mm, f + 1)
                sc.copy(hFT[:], f_bank[:, 0:P]).then_inc(f_ht_sb, 1)
                sc.activation(sq_junk[:], hF[:], ACT.Square, accum_out=ssqF[:, f, 0:1]).then_inc(f_ssq, 1)

            def f_exp(f):
                act.wait_ge(f_sc_ready, f + 1)
                sc.activation(peF[:], scF[:], ACT.Exp, scale=HD ** -0.5).then_inc(f_exp_done, 1)

            def f_ot(f):
                act.wait_ge(f_ot_mm, f + 1)
                sc.copy(oFT[:], f_bank[:, 0:P]).then_inc(f_ot_sb, 1)

            def f_zt(f):
                act.wait_ge(f_zt_mm, f + 1)
                sc.copy(zFT[:], f_bank[:, 0:P]).then_inc(f_zt_sb, 1)
                sc.activation(sq_junk[:], zF[:], ACT.Square, accum_out=ssqF[:, f, 1:2]).then_inc(f_ssq2, 1)

            def f_ge(f):
                act.wait_ge(f_lg_ready, f + 1)
                sc.activation(geF[:], lgF[:], ACT.Exp, bias=nmF[:], accum_out=gsF[:, 0:1]).then_inc(f_ge_done, 1)

            def a_ht(a, k):
                act.wait_ge((a_ht_mm, a_h2_mm)[k], a + 1)
                if a == 0 and k == 0:
                    act.wait_ge(prep_dve, 1)
                dst = hAT[:] if k == 0 else h2T[:, a % 2, :]
                sc.activation(dst, a_bank[:, 0:P], ACT.Identity, scale=mcol[:, 2 * k + 1:2 * k + 2],
                              bias=mcol[:, 2 * k:2 * k + 1]).then_inc((a_ht_sb, a_h2_sb)[k], 1)

            def a_qk(a):
                act.wait_ge(a_qkv_mm, a + 1)
                sc.activation(qT[:], a_bank[:, 0:P], ACT.Identity, bias=cols[:, 3:4])
                sc.activation(kT[:, a * P:(a + 1) * P], a_bank[:, P:2 * P], ACT.Identity,
                              bias=cols[:, 4:5]).then_inc(a_qk_sb, 1)

            def a_scores(a):
                for c, (lo, w) in enumerate(chunks(a)):
                    u = att_use(a, 0, c)
                    act.wait_ge(a_sc_mm, chunks_before[a] + c + 1)
                    if c == 0 and a >= 1:
                        act.wait_ge(a_pt_mm, chunks_before[a])
                    sc.mul(S[:, lo:lo + w], att_bank[u % 2][:, 0:w], P ** -0.5).then_inc(a_sc_sb, 1)

            def a_exp(a):
                act.wait_ge(a_top, a + 1)
                sc.activation(X[:, 0:(a + 1) * P], S[:, 0:(a + 1) * P], ACT.Exp,
                              bias=nmA[:]).then_inc(a_exp_done, 1)

            def a_pt(a):
                for c, (lo, w) in enumerate(chunks(a)):
                    u = att_use(a, 1, c)
                    act.wait_ge(a_pt_mm, chunks_before[a] + c + 1)
                    if c == 0 and a >= 1:
                        act.wait_ge(a_o_mm, a)
                    sc.copy(PT[:, lo:lo + w], att_bank[u % 2][:, 0:w]).then_inc(a_pt_sb, 1)

            def a_ge(a):
                act.wait_ge(a_lg_ready, a + 1)
                sc.activation(peR[:], lgR[:], ACT.Exp, bias=nmR[:], accum_out=suR[:, 0:1]).then_inc(a_ge_done, 1)

            def m_th(m, e):
                u = m * NE + e
                act.wait_ge(m_gu_mm, u + 1)
                if u >= 2:
                    act.wait_ge(m_hid, u - 1)
                sc.activation(th[:, u % 2, :], gu_bank[u % 2][:, 0:HID], ACT.Tanh, scale=0.5).then_inc(m_tanh, 1)

            for s in range(STEPS):
                f, a, m = s, s - 1, s - 2
                hf, ha, hm = f < NB, 0 <= a < NB, m >= 0
                if hf:
                    f_xt(f)
                if hm:
                    m_th(m, 0)
                if ha:
                    a_ht(a, 0)
                if hm:
                    m_th(m, 1)
                if hf:
                    f_ht(f)
                if ha:
                    a_qk(a)
                if hm:
                    m_th(m, 2)
                if ha:
                    a_scores(a)
                if hm:
                    m_th(m, 3)
                    m_th(m, 4)
                if ha:
                    a_exp(a)
                if hf:
                    f_exp(f)
                if hm:
                    m_th(m, 5)
                if ha:
                    a_pt(a)
                if hm:
                    m_th(m, 6)
                if hf:
                    f_ot(f)
                if ha:
                    a_ht(a, 1)
                if hm:
                    m_th(m, 7)
                if hf:
                    f_zt(f)
                if ha:
                    a_ge(a)
                if hf:
                    f_ge(f)
                if hm:
                    m_th(m, 8)

        @block.vector
        def _(dve):
            n = [0]

            def link(ins):
                n[0] += 1
                ins.then_inc(dve_chain, 1)
                dve.wait_ge(dve_chain, n[0])

            v = nc.vector

            def stats(x, st, mv, done):
                link(v.bn_stats(st, x))
                v.bn_aggr(mv, st).then_inc(done, 1)

            for j in range(NB):
                if j % 8 == 0:
                    dve.wait_ge((in_xa, in_xb)[j // 8], 16)
                last = v.bn_stats(st0[:, j, :], x_str[:, j, :])
            link(last)
            for j in range(NB):
                last = v.bn_aggr(mv0[:, j, :], st0[:, j, :])
            last.then_inc(var0, 1)
            dve.wait_ge(var0, 1)
            dve.wait_ge(silu_tanh, 1)
            dve.wait_ge(consts, 1)
            link(v.scalar_tensor_tensor(silu_c[:], silu_t[:], 1.0, c_col[:], ALU.add, ALU.mult))
            v.tensor_scalar(silu_b[:, 0, :], ones[:], silu_c[:, 0:1], 0.5, ALU.mult, ALU.mult)
            v.tensor_scalar(silu_b[:, 1, :], ones[:], silu_c[:, 1:2], 0.5, ALU.mult, ALU.mult).then_inc(silu_rows, 1)
            dve.wait_ge(rstd0, 1)
            for j in range(NB):
                last = v.tensor_scalar(h_tmp[:, j, :], x_str[:, j, :], mv0[:, j, 0:1], rs0[:, j:j + 1],
                                       ALU.subtract, ALU.mult)
            link(last)
            dve.wait_ge(mod0_sb, 1)
            v.tensor_scalar(mod0[:, 4, :], mod0[:, 4, :], 1.0, None, ALU.add)
            link(v.tensor_scalar(mod0[:, 1, :], mod0[:, 1, :], 1.0, None, ALU.add))
            for q in range(4):
                j = slice(4 * q, 4 * q + 4)
                v.tensor_tensor(h_tmp[:, j, :], h_tmp[:, j, :], over_blocks(mod0[:, 1, :], 4),
                                ALU.mult).then_inc(scaled0, 1)

            def gates(src, k):
                v.tensor_scalar(gsign[:, k, :], src, 0.0, 2.0, ALU.is_ge, ALU.mult)
                link(v.scalar_tensor_tensor(gmag[:, k, :], src, -1.0, src, ALU.mult, ALU.max))
                link(v.tensor_scalar(gmag[:, k, :], gmag[:, k, :], 0.25, None, ALU.max))
                link(v.scalar_tensor_tensor(src, gsign[:, k, :], 1.0, gmag[:, k, :], ALU.subtract, ALU.mult))

            gates(mod0[:, 2, :], 0)
            gates(mod0[:, 5, :], 1)
            dve.wait_ge(in_rows, 16 * 12)
            dve.wait_ge(in_w0, 80)
            v.tensor_tensor(bo0G[:], rows[:, 0, :], mod0[:, 2, :], ALU.mult)
            v.tensor_tensor(w0oG[:], w0o[:], mod0[:, 2, :], ALU.mult).then_inc(gates_ready, 1)

            dve.wait_ge(gram_mm, 1)
            v.tensor_copy(gram[:], bank[2][:, 0:P]).then_inc(gram_sb, 1)
            dve.wait_ge(gramk_mm, 1)
            v.tensor_copy(gramk[:], bank[3][:, 0:P]).then_inc(gramk_sb, 1)
            dve.wait_ge(qk_mm, 1)
            dve.wait_ge(lane_sb, 1)
            link(v.tensor_tensor(qk_m[:], bank[2][:, 0:P], same_lane[:], ALU.mult))
            v.tensor_reduce(qk_r[:], qk_m[:].rearrange("p (b d) -> p b d", d=HD), AX.X, ALU.add).then_inc(qkr_ready, 1)
            dve.wait_ge(hsc_mm, 1)
            link(v.tensor_copy(hsc[:], bank[3][0:H, 0:H]))
            link(v.tensor_reduce(hmx[:, 0:1], hsc[:], AX.X, ALU.max))
            v.tensor_scalar(hmx[:, 1:2], hmx[:, 0:1], -HD ** -0.5, None, ALU.mult).then_inc(hneg, 1)
            dve.wait_ge(hexp, 1)
            link(v.reciprocal(hmx[:, 3:4], hmx[:, 2:3]))
            link(v.tensor_scalar(hatt[:], hatt[:], hmx[:, 3:4], None, ALU.mult))
            v.tensor_copy(hspread[:], ones[0:H, :]).then_inc(hatt_ready, 1)
            dve.wait_ge(hspr_mm, 1)
            v.tensor_copy(hspread[:], bank[2][0:H, 0:P]).then_inc(hspr_sb, 1)
            dve.wait_ge(hmix_mm, 1)
            v.tensor_tensor(hmix[:], bank[3][:, 0:P], same_lane[:], ALU.mult).then_inc(hmix_sb, 1)
            dve.wait_ge(wva_mm, 1)
            v.tensor_copy(w0vA[:], bank[2][:, 0:P]).then_inc(wva_sb, 1)
            for q in range(0, 4, 2):
                dve.wait_ge(z0_mm, q + 1)
                v.tensor_copy(mixed[:].rearrange("r a (j d) -> r j a d", j=NB)[:, 4 * q:4 * q + 4, :, :],
                              bank[4 + q][:].rearrange("r (j a d) -> r j a d", j=4, a=H)).then_inc(z0_sb, 1)

            dve.wait_ge(in_f, 96)
            v.tensor_scalar(bcols[:, 1, :], ones[:], cols[:, 5:6], None, ALU.mult)
            v.tensor_scalar(bcols[0:64, 0, :], ones[0:64, :], cols[0:64, 2:3], None, ALU.mult).then_inc(bcol_ready, 1)
            v.tensor_scalar(wqkv[:, 0:P], wfq[:], cols[:, 0:1], None, ALU.mult)
            v.tensor_copy(bqkv[:, 0:P], rows[:, 1, :])
            v.tensor_scalar(wfgG[:], wfg[:], cols[:, 1:2], None, ALU.mult)
            v.scalar_tensor_tensor(wfeG[:], wfe[:], cols[:, 1:2], over_blocks(mod0[:, 5, :], E), ALU.mult, ALU.mult)
            dve.wait_ge(fold_mm, 1)
            wkv = bank[0][:, 0:2 * P].rearrange("p (g k d) -> p k g d", g=H, k=2)
            v.tensor_scalar(wqkv[:, P:2 * P].rearrange("p (g d) -> p g d", g=H), wkv[:, 0], cols[:, 0:1], None,
                            ALU.mult)
            v.tensor_scalar(wqkv[:, 2 * P:].rearrange("p (d g) -> p g d", g=H), wkv[:, 1], cols[:, 0:1], None,
                            ALU.mult)
            link(v.tensor_tensor(bkv[:], bank[1][:, 0:2 * P], bup_row[:], ALU.add))
            bk = bkv[:].rearrange("p (g k d) -> p k g d", g=H, k=2)
            v.tensor_copy(bqkv[:, P:2 * P].rearrange("p (g d) -> p g d", g=H), bk[:, 0])
            link(v.tensor_copy(bqkv[:, 2 * P:].rearrange("p (d g) -> p g d", g=H), bk[:, 1]))
            v.memset(hmx[:, 0:1], 0.0).then_inc(mods_first, 1)
            dve.wait_ge(mod1_sb, 1)
            dve.wait_ge(col_sb, 1)
            gates(mod1[:, 0, :], 2)
            gates(mod1[:, 1, :], 3)
            v.tensor_scalar(mcol[:, 1:2], mcol[:, 1:2], 1.0, None, ALU.add)
            v.tensor_scalar(mcol[:, 3:4], mcol[:, 3:4], 1.0, None, ALU.add)
            v.tensor_tensor(bo1G[:], rows[:, 3, :], mod1[:, 0, :], ALU.mult)
            dve.wait_ge(fold_mm, 2)
            v.tensor_tensor(w1vo[:], bank[2][:, 0:P], mod1[:, 0, :], ALU.mult)
            v.tensor_tensor(bvo[:], bank[2][:, P:2 * P], mod1[:, 0, :], ALU.mult).then_inc(prep_dve, 1)
            dve.wait_ge(in_moe, 96)
            v.scalar_tensor_tensor(wdnG[:].rearrange("p e c f -> p (e c) f"), wdn[:].rearrange("p e c f -> p (e c) f"),
                                   0.5, over_blocks(mod1[:, 1, :], 2 * NE), ALU.mult, ALU.mult).then_inc(prep_dve, 1)

            def f_x1(f):
                dve.wait_ge(f_wo_mm, f + 1)
                dve.wait_ge(xb_ready, f // 4 + 1)
                link(v.tensor_tensor(x1[:, f, :], f_bank[:, 0:P], x_blk[:, f, :], ALU.add))
                stats(x1[:, f, :], stF[:, f, :], mvF[:, f, :], f_var)

            def f_n(f):
                dve.wait_ge(f_rstd, f + 1)
                if f >= 1:
                    dve.wait_ge(f_h_ready, f)
                v.tensor_scalar(nF[:], x1[:, f, :], mvF[:, f, 0:1], rsF[:, f:f + 1], ALU.subtract,
                                ALU.mult).then_inc(f_n_done, 1)

            def f_qkv(f):
                dve.wait_ge(f_qkv_mm, f + 1)
                dve.wait_ge(f_rms, f + 1)
                v.scalar_tensor_tensor(qkvF[:], f_bank[:, 0:3 * P], rmsF[:, f, 0:1], bqkv[:], ALU.mult,
                                       ALU.add).then_inc(f_qkv_sb, 1)
                dve.wait_ge(f_qkv_sb, f + 1)

            def f_qk(f, q):
                hs = slice(4 * q, 4 * q + 4)
                k = prod[:, q * CH:(q + 1) * CH].rearrange("p (h g d) -> p h g d", h=4, g=H)
                qq = qkvF[:, 0:P].rearrange("p (h o d) -> p h o d", h=H, o=1)[:, hs].broadcast_to([P, 4, H, HD])
                kk = qkvF[:, P:2 * P].rearrange("p (o g d) -> p o g d", o=1, g=H).broadcast_to([P, 4, H, HD])
                link(v.tensor_tensor(k, qq, kk, ALU.mult))
                last = v.tensor_reduce(scF[:, hs, :], k, AX.X, ALU.add)
                if q == 3:
                    link(last)

            def f_max(f):
                link(v.tensor_reduce(mxF[:], scF[:], AX.X, ALU.max))
                v.tensor_tensor(scF[:], scF[:], mxF[:].rearrange("p (h o) -> p h o", o=1).broadcast_to([P, H, H]),
                                ALU.subtract).then_inc(f_sc_ready, 1)

            def f_av(f, q):
                if q == 0:
                    dve.wait_ge(f_exp_done, f + 1)
                    v.tensor_reduce(sumF[:], peF[:], AX.X, ALU.add)
                hs = slice(4 * q, 4 * q + 4)
                k = prod[:, q * CH:(q + 1) * CH].rearrange("p (h d g) -> p h d g", h=4, d=HD)
                pp = peF[:].rearrange("p h (o g) -> p h o g", o=1)[:, hs].broadcast_to([P, 4, HD, H])
                vv = qkvF[:, 2 * P:].rearrange("p (o d g) -> p o d g", o=1, g=H).broadcast_to([P, 4, HD, H])
                link(v.tensor_tensor(k, pp, vv, ALU.mult))
                last = v.tensor_reduce(oF[:, hs, :], k, AX.X, ALU.add)
                if q == 3:
                    link(last)
                    link(v.reciprocal(rinF[:], sumF[:]))
                    v.tensor_tensor(onF[:], oF[:], rinF[:].rearrange("p (h o) -> p h o", o=1).broadcast_to([P, H, HD]),
                                    ALU.mult).then_inc(f_o_ready, 1)

            def f_z(f):
                dve.wait_ge(f_y_mm, f + 1)
                dve.wait_ge(f_hb_ready, f + 1)
                if f >= 1:
                    dve.wait_ge(f_base, f)
                    dve.wait_ge(f_ssq2, f)
                v.tensor_tensor(zF[:], f_bank[:, 0:P], hFb[:], ALU.add).then_inc(f_z_ready, 1)

            def f_lg(f):
                dve.wait_ge(f_lg_mm, f + 1)
                dve.wait_ge(f_rms2, f + 1)
                link(v.scalar_tensor_tensor(lgF[:], f_bank[:, 0:E], rmsF[:, f, 1:2], bg_row[:], ALU.mult, ALU.add))
                v.tensor_reduce(nmF[:], lgF[:], AX.X, ALU.max, negate=True).then_inc(f_lg_ready, 1)

            def f_wt(f):
                dve.wait_ge(f_ge_done, f + 1)
                link(v.reciprocal(gsF[:, 1:2], gsF[:, 0:1]))
                link(v.tensor_scalar(wtF[:], geF[:], gsF[:, 1:2], rmsF[:, f, 1:2], ALU.mult, ALU.mult))

            def f_experts(f, half):
                dve.wait_ge((f_e1_mm, f_e2_mm)[half], f + 1)
                if half == 0:
                    dve.wait_ge(f_base, f + 1)
                src = (fe_bank, f_bank)[half]
                for i in range(4):
                    e = 4 * half + i
                    dst = x2[:, f, :] if e == E - 1 else accF[:, (e + 1) % 2, :]
                    ins = v.scalar_tensor_tensor(dst, src[:, i * P:(i + 1) * P], wtF[:, e:e + 1], accF[:, e % 2, :],
                                                 ALU.mult, ALU.add)
                    if e == E - 1:
                        ins.then_inc(f_x2, 1)
                    elif e == 3:
                        ins.then_inc(f_e1_read, 1)
                        dve.wait_ge(f_e1_read, f + 1)
                    else:
                        link(ins)

            def a_stats(a, k):
                src = (x2, x3)[k][:, a, :]
                if k == 0:
                    dve.wait_ge(f_x2, a + 1)
                else:
                    dve.wait_ge(a_x3, a + 1)
                stats(src, stA[:, a, k, :], mvA[:, a, k, :], (a_var, a_var2)[k])

            def a_n(a, k):
                dve.wait_ge((a_rstd, a_rstd2)[k], a + 1)
                v.tensor_scalar(nA[:, k, :], (x2, x3)[k][:, a, :], mvA[:, a, k, 0:1], rsA[:, a, k:k + 1],
                                ALU.subtract, ALU.mult).then_inc((a_n_done, a_n2_done)[k], 1)

            def a_v(a):
                dve.wait_ge(a_qk_sb, a + 1)
                v.tensor_tensor(vA[:, a, :], a_bank[:, 2 * P:3 * P], bvo[:], ALU.add).then_inc(a_v_sb, 1)

            def a_max(a):
                dve.wait_ge(a_masked, a + 1)
                link(v.max(top[:], S[:, 0:(a + 1) * P]))
                v.tensor_scalar(nmA[:], top[:, 0:1], -1.0, None, ALU.mult).then_inc(a_top, 1)

            def a_pick(a):
                link(v.match_replace(R[:, 0:(a + 1) * P], top[:], S[:, 0:(a + 1) * P], PICKED))

            def a_probs(a):
                dve.wait_ge(a_exp_done, a + 1)
                w = (a + 1) * P
                v.scalar_tensor_tensor(S[:, 0:w], R[:, 0:w], PICKED, X[:, 0:w], ALU.is_equal, ALU.mult,
                                       accum_out=sumA[:, 0:1]).then_inc(a_p_ready, 1)
                dve.wait_ge(a_p_ready, a + 1)
                link(v.reciprocal(sumA[:, 1:2], sumA[:, 0:1]))

            def a_x3_(a):
                dve.wait_ge(a_o_mm, a + 1)
                dve.wait_ge(a_base, a + 1)
                v.scalar_tensor_tensor(x3[:, a, :], a_bank[:, 0:P], sumA[:, 1:2], x2b[:], ALU.mult,
                                       ALU.add).then_inc(a_x3, 1)

            def a_lg(a):
                dve.wait_ge(a_lg_mm, a + 1)
                link(v.tensor_copy(lgR[:], a_bank[:, 0:E]))
                v.tensor_reduce(nmR[:], lgR[:], AX.X, ALU.max, negate=True).then_inc(a_lg_ready, 1)

            def a_route(a):
                dve.wait_ge(a_ge_done, a + 1)
                link(v.reciprocal(suR[:, 1:2], suR[:, 0:1]))
                link(v.tensor_scalar(prR[:], peR[:], suR[:, 1:2], None, ALU.mult))
                link(v.max(tpR[:], prR[:]))
                v.tensor_scalar(suR[:, 2:3], tpR[:, 0:1], tpR[:, 1:2], 1e-20, ALU.add, ALU.add)
                link(v.max_index(ixR[:], tpR[:], prR[:]))
                link(v.tensor_copy(ifR[:], ixR[:]))
                link(v.tensor_scalar(mkR[:, 0, :], iota8[:], ifR[:, 0:1], None, ALU.is_equal))
                link(v.scalar_tensor_tensor(mkR[:, 1, :], iota8[:], ifR[:, 1:2], mkR[:, 0, :], ALU.is_equal, ALU.add))
                link(v.reciprocal(suR[:, 3:4], suR[:, 2:3]))
                v.scalar_tensor_tensor(wtR[:, a, :], prR[:], suR[:, 3:4], mkR[:, 1, :], ALU.mult,
                                       ALU.mult).then_inc(a_w_ready, 1)

            def m_hidden(m, e):
                u = m * NE + e
                dve.wait_ge(m_tanh, u + 1)
                if u >= 2:
                    dve.wait_ge(m_y_mm, u - 1)
                b = gu_bank[u % 2]
                link(v.scalar_tensor_tensor(gg[:, u % 2, :], th[:, u % 2, :], 1.0, b[:, 0:HID], ALU.add, ALU.mult))
                v.tensor_tensor(hid[:, u % 2, :], gg[:, u % 2, :], b[:, HID:2 * HID], ALU.mult).then_inc(m_hid, 1)

            def m_acc(m, grp):
                es = (range(0, 4), range(4, 8), range(8, 9))[grp]
                dve.wait_ge(m_y_mm, m * NE + es[-1] + 1)
                if grp == 0:
                    dve.wait_ge(a_w_ready, m + 1)
                for i, e in enumerate(es):
                    src = y_bank[:, i * P:(i + 1) * P]
                    old = x3[:, m, :] if e == 0 else acc[:, e % 2, :]
                    if e == E:
                        v.tensor_tensor(x4[:, m, :], src, old, ALU.add).then_inc(m_out, 1)
                        continue
                    ins = v.scalar_tensor_tensor(acc[:, (e + 1) % 2, :], src, wtR[:, m, e:e + 1], old,
                                                 ALU.mult, ALU.add)
                    if i == 3:
                        ins.then_inc(m_y_read, 1)
                        dve.wait_ge(m_y_read, 2 * m + grp + 1)
                    else:
                        link(ins)

            for s in range(STEPS):
                f, a, m = s, s - 1, s - 2
                hf, ha, hm = f < NB, 0 <= a < NB, m >= 0
                if ha:
                    a_stats(a, 0)
                if hf:
                    f_x1(f)
                if hm:
                    m_hidden(m, 0)
                if ha:
                    a_n(a, 0)
                if hf:
                    f_n(f)
                if hm:
                    m_hidden(m, 1)
                if ha:
                    a_v(a)
                if hm:
                    m_hidden(m, 2)
                if hf:
                    f_qkv(f)
                    f_qk(f, 0)
                if hm:
                    m_hidden(m, 3)
                if hf:
                    f_qk(f, 1)
                if ha:
                    a_max(a)
                if hm:
                    m_hidden(m, 4)
                if hf:
                    f_qk(f, 2)
                if ha:
                    a_pick(a)
                if hm:
                    m_acc(m, 0)
                if hf:
                    f_qk(f, 3)
                    f_max(f)
                if ha:
                    a_probs(a)
                if hm:
                    m_hidden(m, 5)
                if hf:
                    f_av(f, 0)
                    f_av(f, 1)
                if hm:
                    m_hidden(m, 6)
                if hf:
                    f_av(f, 2)
                if ha:
                    a_x3_(a)
                    a_stats(a, 1)
                if hf:
                    f_av(f, 3)
                if ha:
                    a_n(a, 1)
                if hm:
                    m_hidden(m, 7)
                if hf:
                    f_z(f)
                if ha:
                    a_lg(a)
                if hf:
                    f_lg(f)
                if hm:
                    m_hidden(m, 8)
                    m_acc(m, 1)
                if ha:
                    a_route(a)
                if hf:
                    f_wt(f)
                    f_experts(f, 0)
                    f_experts(f, 1)
                if hm:
                    m_acc(m, 2)

        @block.tensor
        def _(pe):
            t = nc.tensor

            def mm(out, lhsT, rhs, start=True, stop=True):
                return t.matmul(out, lhsT, rhs, start=start, stop=stop)

            def tr(out, src, k=P):
                return t.transpose(out, src, ident[0:k, 0:k])

            pe.wait_ge(in_mod, 32)
            pe.wait_ge(silu_rows, 1)
            mm(bank[0][:, 0:3 * P], silu_b[:, 0, :], wmod[:, 0, 0:3 * P])
            mm(bank[1][:, 0:3 * P], silu_b[:, 0, :], wmod[:, 0, 3 * P:]).then_inc(mod0_mm, 1)
            mm(bank[2][:, 0:P], silu_b[:, 1, :], wmod[:, 1, 2 * P:3 * P])
            mm(bank[2][:, P:2 * P], silu_b[:, 1, :], wmod[:, 1, 5 * P:6 * P]).then_inc(mod1_mm, 1)
            for k, c in enumerate((0, 1, 3, 4)):
                last = mm(bank[3][:, k:k + 1], wmod[:, 1, c * P:(c + 1) * P], silu_b[:, 1, 0:1])
            last.then_inc(col_mm, 1)
            pe.wait_ge(consts, 1)
            lanes = lane_rows[:].rearrange("d h e -> d (h e)")
            mm(bank[4][:, 0:P], lanes, lanes).then_inc(lane_mm, 1)
            pe.wait_ge(in_w0, 80)
            pe.wait_ge(in_1, 80)
            pe.wait_ge(in_f, 96)
            tr(bank[5][:, 0:P], w0v[:])
            tr(bank[5][:, P:2 * P], w1v[:])
            tr(bank[5][0:64, 2 * P:3 * P], wdown[:]).then_inc(tr_mm, 1)

            pe.wait_ge(mod1_sb, 1)
            for q in range(4):
                pe.wait_ge(h0_ready, q + 1)
                if q == 0:
                    pe.wait_ge(mod0_sb, 1)
                else:
                    pe.wait_ge(hT0_sb, max(q - 1, 1))
                for j in range(4 * q, 4 * q + 4):
                    last = mm(bank[2][:, 0:P], h_str[:, j, :], h_str[:, j, :], start=(j == 0), stop=(j == NB - 1))
                if q == 3:
                    last.then_inc(gram_mm, 1)
                for j in range(4):
                    last = tr(bank[q % 2][:, j * P:(j + 1) * P], h_str[:, 4 * q + j, :])
                last.then_inc(hT0_mm, 1)
            pe.wait_ge(gram_sb, 1)
            pe.wait_ge(col_sb, 1)
            mm(bank[3][:, 0:P], gram[:], w0k[:]).then_inc(gramk_mm, 1)
            pe.wait_ge(gramk_sb, 1)
            mm(bank[2][:, 0:P], w0q[:], gramk[:]).then_inc(qk_mm, 1)
            pe.wait_ge(qkr_ready, 1)
            mm(bank[3][0:H, 0:H], head_cols[:], qk_r[:]).then_inc(hsc_mm, 1)
            pe.wait_ge(hT0_sb, 4)
            pe.wait_ge(tr_sb, 1)
            pe.wait_ge(hatt_ready, 1)
            mm(bank[2][0:H, 0:P], hatt[:], head_rows[:]).then_inc(hspr_mm, 1)
            pe.wait_ge(hspr_sb, 1)
            mm(bank[3][:, 0:P], head_rows[:], hspread[:]).then_inc(hmix_mm, 1)
            pe.wait_ge(hmix_sb, 1)
            mm(bank[2][:, 0:P], w0vT[:], hmix[:]).then_inc(wva_mm, 1)
            pe.wait_ge(wva_sb, 1)
            pe.wait_ge(lane_sb, 1)
            for q in range(4):
                for j in range(4):
                    last = mm(bank[4 + q][:, j * P:(j + 1) * P], hT_str[:, 4 * q + j, :], w0vA[:])
                last.then_inc(z0_mm, 1)
            pe.wait_ge(bcol_ready, 1)
            mm(bank[0][:, 0:2 * P], wdownT[:], wup[:])
            mm(bank[1][:, 0:2 * P], bcols[0:64, 0, :], wup[:]).then_inc(fold_mm, 1)
            mm(bank[2][:, 0:P], w1vT[:], w1o[:])
            mm(bank[2][:, P:2 * P], bcols[:, 1, :], w1o[:]).then_inc(fold_mm, 1)
            pe.wait_ge(z0_sb, 4)
            pe.wait_ge(gates_ready, 1)

            def f_xt(f):
                if f >= 1:
                    pe.wait_ge(f_x2, f)
                tr(f_bank[:, 0:P], mixed[:, f, :]).then_inc(f_xt_mm, 1)

            def f_wo(f):
                pe.wait_ge(f_xt_sb, f + 1)
                mm(f_bank[:, 0:P], xT[:], w0oG[:]).then_inc(f_wo_mm, 1)

            def f_ht(f):
                pe.wait_ge(f_h_ready, f + 1)
                tr(f_bank[:, 0:P], hF[:]).then_inc(f_ht_mm, 1)

            def f_qkv(f):
                pe.wait_ge(f_ht_sb, f + 1)
                if f == 0:
                    pe.wait_ge(mods_first, 1)
                mm(f_bank[:, 0:3 * P], hFT[:], wqkv[:]).then_inc(f_qkv_mm, 1)

            def f_ot(f):
                pe.wait_ge(f_o_ready, f + 1)
                tr(f_bank[:, 0:P], onF[:].rearrange("p h d -> p (h d)")).then_inc(f_ot_mm, 1)

            def f_y(f):
                pe.wait_ge(f_ot_sb, f + 1)
                mm(f_bank[:, 0:P], oFT[:], wfo[:]).then_inc(f_y_mm, 1)

            def f_zt(f):
                pe.wait_ge(f_z_ready, f + 1)
                tr(f_bank[:, 0:P], zF[:]).then_inc(f_zt_mm, 1)

            def f_experts(f):
                pe.wait_ge(f_zt_sb, f + 1)
                mm(f_bank[:, 0:E], zFT[:], wfgG[:]).then_inc(f_lg_mm, 1)
                if f >= 1:
                    pe.wait_ge(f_e1_read, f)
                mm(fe_bank[:], zFT[:], wfeG[:, 0:4, :].rearrange("p e f -> p (e f)")).then_inc(f_e1_mm, 1)
                pe.wait_ge(f_lg_ready, f + 1)
                mm(f_bank[:], zFT[:], wfeG[:, 4:8, :].rearrange("p e f -> p (e f)")).then_inc(f_e2_mm, 1)

            def a_ht(a, k):
                pe.wait_ge((a_n_done, a_n2_done)[k], a + 1)
                if k == 0 and a >= 1:
                    pe.wait_ge(a_lg_ready, a)
                tr(a_bank[:, 0:P], nA[:, k, :]).then_inc((a_ht_mm, a_h2_mm)[k], 1)

            def a_qkv(a):
                pe.wait_ge(a_ht_sb, a + 1)
                mm(a_bank[:, 0:P], w1q[:], hAT[:])
                mm(a_bank[:, P:2 * P], w1k[:], hAT[:])
                mm(a_bank[:, 2 * P:3 * P], hAT[:], w1vo[:]).then_inc(a_qkv_mm, 1)

            def bank_free(a, k, c):
                u = att_use(a, k, c) - 2
                if u < 0:
                    return
                for b, kk, cc in ((b, kk, cc) for b in range(max(0, a - 1), a + 1) for kk in range(2)
                                  for cc in range(len(chunks(b)))):
                    if att_use(b, kk, cc) == u:
                        pe.wait_ge((a_sc_sb, a_pt_sb)[kk], chunks_before[b] + cc + 1)
                        return

            def a_scores(a):
                pe.wait_ge(a_qk_sb, a + 1)
                for c, (lo, w) in enumerate(chunks(a)):
                    bank_free(a, 0, c)
                    mm(att_bank[att_use(a, 0, c) % 2][:, 0:w], qT[:], kT[:, lo:lo + w]).then_inc(a_sc_mm, 1)

            def a_av(a):
                pe.wait_ge(a_p_ready, a + 1)

                def weights_t(c):
                    lo, w = chunks(a)[c]
                    bank_free(a, 1, c)
                    for j in range(w // P):
                        last = tr(att_bank[att_use(a, 1, c) % 2][:, j * P:(j + 1) * P],
                                  S[:, lo + j * P:lo + (j + 1) * P])
                    last.then_inc(a_pt_mm, 1)

                weights_t(0)
                for c, (lo, w) in enumerate(chunks(a)):
                    if c + 1 < len(chunks(a)):
                        weights_t(c + 1)
                    pe.wait_ge(a_pt_sb, chunks_before[a] + c + 1)
                    if c == 0:
                        pe.wait_ge(a_v_sb, a + 1)
                    for j in range(w // P):
                        b = lo // P + j
                        last = mm(a_bank[:, 0:P], PT[:, b * P:(b + 1) * P], vA[:, b, :], start=(b == 0), stop=(b == a))
                last.then_inc(a_o_mm, 1)

            def a_lg(a):
                pe.wait_ge(a_h2_sb, a + 1)
                mm(a_bank[:, 0:E], h2T[:, a % 2, :], w1r[:]).then_inc(a_lg_mm, 1)

            def m_gu(m, e):
                u = m * NE + e
                if u == 0:
                    pe.wait_ge(prep_dve, 2)
                if u >= 2:
                    pe.wait_ge(m_hid, u - 1)
                b, x = gu_bank[u % 2], h2T[:, m % 2, :]
                for c in range(2):
                    mm(b[:, c * P:(c + 1) * P], wgate[:, e, c * P:(c + 1) * P], x)
                for c in range(2):
                    last = mm(b[:, HID + c * P:HID + (c + 1) * P], wups[:, e, c * P:(c + 1) * P], x)
                last.then_inc(m_gu_mm, 1)

            def m_down(m, e):
                u = m * NE + e
                pe.wait_ge(m_hid, u + 1)
                if e == 4:
                    pe.wait_ge(m_y_read, 2 * m + 1)
                if e == 8:
                    pe.wait_ge(m_y_read, 2 * m + 2)
                if e == 0 and m >= 1:
                    pe.wait_ge(m_out, m)
                y = y_bank[:, (e % 4) * P:(e % 4 + 1) * P]
                mm(y, hid[:, u % 2, 0:P], wdnG[:, e, 0, :], start=True, stop=False)
                mm(y, hid[:, u % 2, P:HID], wdnG[:, e, 1, :], start=False, stop=True).then_inc(m_y_mm, 1)

            for s in range(STEPS):
                f, a, m = s, s - 1, s - 2
                hf, ha, hm = f < NB, 0 <= a < NB, m >= 0
                if hf:
                    f_xt(f)
                if hm:
                    m_gu(m, 0)
                if hf:
                    f_wo(f)
                if ha:
                    a_ht(a, 0)
                if hm:
                    m_gu(m, 1)
                if ha:
                    a_qkv(a)
                if hf:
                    f_ht(f)
                if hm:
                    m_down(m, 0)
                    m_gu(m, 2)
                if hf:
                    f_qkv(f)
                if ha:
                    a_scores(a)
                if hm:
                    m_down(m, 1)
                    m_gu(m, 3)
                    m_down(m, 2)
                    m_gu(m, 4)
                    m_down(m, 3)
                    m_gu(m, 5)
                if ha:
                    a_av(a)
                if hm:
                    m_down(m, 4)
                    m_gu(m, 6)
                    m_down(m, 5)
                if hf:
                    f_ot(f)
                if ha:
                    a_ht(a, 1)
                if hm:
                    m_gu(m, 7)
                if hf:
                    f_y(f)
                if ha:
                    a_lg(a)
                if hm:
                    m_down(m, 6)
                if hf:
                    f_zt(f)
                if hm:
                    m_gu(m, 8)
                    m_down(m, 7)
                if hf:
                    f_experts(f)
                if hm:
                    m_down(m, 8)


def kernel(**inputs):
    import numpy as np
    import concourse.bacc as bacc
    from concourse.bass_utils import run_bass_kernel_spmd

    nc = bacc.Bacc("TRN2", target_bir_lowering=False, num_devices=1)
    arrays, aps = {}, {}
    for name, a in inputs.items():
        a = np.ascontiguousarray(a)
        arrays[f"in_{name}"] = a
        aps[name] = nc.dram_tensor(f"in_{name}", a.shape, mybir.dt.from_np(a.dtype), kind="ExternalInput").ap()
    shape = inputs["L0_attn_x"].shape
    out = nc.dram_tensor("out_x", shape, F32, kind="ExternalOutput").ap()
    build(nc, aps, out)
    r = run_bass_kernel_spmd(nc, [arrays], core_ids=[0])
    return r.results[0]["out_x"]
```

```python
from contextlib import ExitStack

import concourse.bass as bass
from concourse import mybir

ALU = mybir.AluOpType
ACT = mybir.ActivationFunctionType
F32 = mybir.dt.float32
U32 = mybir.dt.uint32
AX = mybir.AxisListType

P = 128
NB = 16
H = 16
HD = P // H
E = 8
HID = 256
TOPK = 8
LN_EPS = 1e-5
RMS_EPS = 1e-6
MASKED = -1e30
PICKED = -3e38
CH = 512
NA0 = 4
PH = 8
VH = H - PH
VG = 2


def build(nc, d, out):
    with ExitStack() as ctx:
        def sb(name, shape, dt=F32):
            return ctx.enter_context(nc.sbuf_tensor(name, shape, dt))

        def sem(name):
            return ctx.enter_context(nc.semaphore(name))

        bank = [ctx.enter_context(nc.psum_tensor(f"bank{i}", [P, CH], F32)) for i in range(8)]
        gu_bank = bank[0:2]
        y_bank = bank[2]
        att_bank = bank[3:5]
        a_bank = bank[5]
        f1_bank = bank[6]
        f2_bank = bank[7]

        ident = sb("ident", [P, P])
        ones = sb("ones", [P, P])
        neg_half = sb("neg_half", [P, NB])
        iota8 = sb("iota8", [P, E])
        head_rows = sb("head_rows", [H, P])
        head_cols = sb("head_cols", [P, H])
        lane_rows = sb("lane_rows", [HD, H, HD])
        same_lane = sb("same_lane", [P, P])

        S = sb("S", [P, NB * P])
        R = sb("R", [P, NB * P])
        X = sb("X", [P, NB * P])
        PT = sb("PT", [P, NB * P])
        W = sb("W", [P, 2, NB * P])

        x_blk = sb("x_blk", [P, NB, P])
        c_col = sb("c_col", [P, 2])
        wmod = W[:, 0, 0:12 * P].rearrange("p (l c) -> p l c", l=2)
        w0q = sb("w0q", [P, P])
        w0k = sb("w0k", [P, P])
        w0v = sb("w0v", [P, P])
        w0o = sb("w0o", [P, P])
        rows = sb("rows", [P, 6, P])
        bup_row = sb("bup_row", [P, 2 * P])
        bg_row = sb("bg_row", [P, E])
        cols = sb("cols", [P, 8])
        wfq = sb("wfq", [P, P])
        wdown = sb("wdown", [P, 64])
        wup = sb("wup", [64, 2 * P])
        wfo = sb("wfo", [P, P])
        wfg = sb("wfg", [P, E])
        wfe = sb("wfe", [P, E, P])
        w1q = sb("w1q", [P, P])
        w1k = sb("w1k", [P, P])
        w1v = sb("w1v", [P, P])
        w1o = sb("w1o", [P, P])
        w1r = sb("w1r", [P, E])
        wgate = sb("wgate", [P, E + 1, HID])
        wups = sb("wups", [P, E + 1, HID])
        wdn = sb("wdn", [P, E + 1, 2, P])

        silu_t = sb("silu_t", [P, 2])
        silu_c = sb("silu_c", [P, 2])
        silu_b = sb("silu_b", [P, 2, P])
        mod0 = sb("mod0", [P, 6, P])
        mod1 = sb("mod1", [P, 2, P])
        mcol = sb("mcol", [P, 4])
        gsign = W[:, 1, 0:4 * P].rearrange("p (k f) -> p k f", k=4)
        gmag = W[:, 1, 4 * P:8 * P].rearrange("p (k f) -> p k f", k=4)
        w0oG = sb("w0oG", [P, P])
        bo0G = sb("bo0G", [P, P])
        w0vT = sb("w0vT", [P, P])
        wdownT = sb("wdownT", [64, P])
        wqkv = sb("wqkv", [P, 3 * P])
        bqkv = sb("bqkv", [P, 3 * P])
        bkv = sb("bkv", [P, 2 * P])
        bcols = sb("bcols", [P, 2, P])
        wfeG = wfe
        wfgG = sb("wfgG", [P, E])
        w1vT = sb("w1vT", [P, P])
        w1vo = sb("w1vo", [P, P])
        bvo = sb("bvo", [P, P])
        bo1G = sb("bo1G", [P, P])
        wdnG = wdn

        st0 = sb("st0", [P, NB, 6])
        mv0 = sb("mv0", [P, NB, 2])
        rs0 = sb("rs0", [P, NB])
        sh0 = sb("sh0", [P, NB])
        x_str, h_tmp, h_str, hT_str = (
            t[:].rearrange("p (j f) -> p j f", j=NB) for t in (S, R, X, PT))
        gram = sb("gram", [P, P])
        gramk = sb("gramk", [P, P])
        qk_m = sb("qk_m", [P, P])
        qk_r = sb("qk_r", [P, H])
        hsc = sb("hsc", [H, H])
        hmx = sb("hmx", [H, 4])
        hatt = sb("hatt", [H, H])
        hspread = sb("hspread", [H, P])
        hmix = sb("hmix", [P, P])
        w0vA = sb("w0vA", [P, P])
        mixed = sb("mixed", [P, NB, P])

        xT = sb("xT", [P, P])
        x1 = x_blk
        stF = sb("stF", [P, NB, 6])
        mvF = sb("mvF", [P, NB, 2])
        rsF = sb("rsF", [P, NB])
        shF = sb("shF", [P, NB])
        nF = sb("nF", [P, P])
        hF1 = sb("hF1", [P, P])
        hF = sb("hF", [P, P])
        hFb = sb("hFb", [P, 2, P])
        hFT = sb("hFT", [P, P])
        sq_junk = sb("sq_junk", [P, 2, P])
        ssqF = sb("ssqF", [P, NB, 2])
        rmsF = sb("rmsF", [P, NB, 2])
        qkvF = sb("qkvF", [P, 2, 3 * P])
        prod = sb("prod", [P, 2, VH * P])
        prodP = sb("prodP", [P, 2, PH * P])
        scF = sb("scF", [P, H, H])
        mxF = sb("mxF", [P, H])
        peF = sb("peF", [P, 2, H, H])
        sumF = sb("sumF", [P, H])
        rinF = sb("rinF", [P, H])
        oF = sb("oF", [P, H, HD])
        onF = sb("onF", [P, H, HD])
        oFT = sb("oFT", [P, P])
        zF = sb("zF", [P, P])
        zg = sb("zg", [P, P])
        zFT = sb("zFT", [P, P])
        lgF = sb("lgF", [P, E])
        nmF = sb("nmF", [P, 1])
        geF = sb("geF", [P, E])
        gsF = sb("gsF", [P, 2])
        wtF = sb("wtF", [P, E])
        exF = sb("exF", [P, P, E + 1])
        x2 = x_blk

        stA = sb("stA", [P, NB, 2, 6])
        mvA = sb("mvA", [P, NB, 2, 2])
        rsA = sb("rsA", [P, NB, 2])
        shA = sb("shA", [P, NB, 2])
        nA = sb("nA", [P, 2, P])
        hAT = sb("hAT", [P, P])
        qT = sb("qT", [P, P])
        kT = sb("kT", [P, NB * P])
        vA = sb("vA", [P, NB, P])
        top = sb("top", [P, TOPK])
        nmA = sb("nmA", [P, 1])
        x2b = sb("x2b", [P, 2, P])
        x3 = sb("x3", [P, 4, P])
        sumA = sb("sumA", [P, 2, 2])
        top_e = sb("top_e", [P, TOPK])
        h2T = sb("h2T", [P, 2, P])
        lgR = sb("lgR", [P, E])
        nmR = sb("nmR", [P, 1])
        peR = sb("peR", [P, E])
        suR = sb("suR", [P, 4])
        prR = sb("prR", [P, E])
        tpR = sb("tpR", [P, E])
        ixR = sb("ixR", [P, E], U32)
        ifR = sb("ifR", [P, E])
        mkR = sb("mkR", [P, 2, E])
        wtR = sb("wtR", [P, NB, E])

        th = sb("th", [P, 2, HID])
        gg = sb("gg", [P, 2, HID])
        hid = sb("hid", [P, 2, HID])
        exM = sb("exM", [P, 2, P, E + 1])
        ysum = sb("ysum", [P, 2, P])
        x4 = sb("x4", [P, 4, P])

        in_xa, in_xb, in_x, in_c, in_mod0, in_mod1, in_tr, in_w0, in_f, in_1, in_moe, in_cols, in_rows = (
            sem(n) for n in ("in_xa", "in_xb", "in_x", "in_c", "in_mod0", "in_mod1", "in_tr", "in_w0", "in_f", "in_1",
                             "in_moe", "in_cols", "in_rows"))
        consts = sem("consts")
        pool_chain, dve_chain, act_chain = sem("pool_chain"), sem("dve_chain"), sem("act_chain")
        (silu_tanh, silu_rows, mod0_mm, mod0_sb, mod1_mm, mod1_sb, col_mm, col_sb, lane_mm, lane_sb, tr_mm, tr_sb,
         fold_mm, gates_ready, gates1_ready, prep_dve, prep_pool, bcol_ready, mods_first, wfe_ready) = (
            sem(n) for n in ("silu_tanh", "silu_rows", "mod0_mm", "mod0_sb", "mod1_mm", "mod1_sb", "col_mm", "col_sb",
                             "lane_mm", "lane_sb", "tr_mm", "tr_sb", "fold_mm", "gates_ready",
                             "gates1_ready", "prep_dve", "prep_pool", "bcol_ready", "mods_first", "wfe_ready"))
        (var0, rstd0, shift0, n0_act, scaled0, h0_ready, h0_dve, gram_mm, gram_sb, gramk_mm, gramk_sb, qk_mm, qkr_ready, hsc_mm, hneg,
         hexp, hatt_ready, hspr_mm, hspr_sb, hmix_mm, hmix_sb, wva_mm, wva_sb, hT0_mm, hT0_sb, z0_mm, z0_sb,
         xb_ready) = (
            sem(n) for n in ("var0", "rstd0", "shift0", "n0_act", "scaled0", "h0_ready", "h0_dve", "gram_mm", "gram_sb", "gramk_mm", "gramk_sb",
                             "qk_mm", "qkr_ready", "hsc_mm", "hneg", "hexp", "hatt_ready", "hspr_mm", "hspr_sb",
                             "hmix_mm", "hmix_sb", "wva_mm", "wva_sb", "hT0_mm", "hT0_sb", "z0_mm", "z0_sb",
                             "xb_ready"))
        (f_xt_mm, f_xt_sb, f_wo_mm, f_var, f_rstd, f_n_done, f_h_ready, f_hb_ready, f_ht_mm, f_ht_sb, f_ssq, f_rms,
         f_qkv_mm, f_qkv_sb, f_sc_ready, f_exp_done, f_o_ready, f_ot_mm, f_ot_sb, f_y_mm, f_z_ready, f_zt_mm,
         f_zt_sb, f_ssq2, f_rms2, f_lg_mm, f_lg_ready, f_ge_done, f_e_mm, f_e_sb, f_wt_ready, f_base, f_x2, f_qkp_ready,
         f_avp_ready) = (
            sem(n) for n in ("f_xt_mm", "f_xt_sb", "f_wo_mm", "f_var", "f_rstd", "f_n_done", "f_h_ready",
                             "f_hb_ready", "f_ht_mm", "f_ht_sb", "f_ssq", "f_rms", "f_qkv_mm", "f_qkv_sb",
                             "f_sc_ready", "f_exp_done", "f_o_ready", "f_ot_mm", "f_ot_sb", "f_y_mm", "f_z_ready",
                             "f_zt_mm", "f_zt_sb", "f_ssq2", "f_rms2", "f_lg_mm", "f_lg_ready", "f_ge_done",
                             "f_e_mm", "f_e_sb", "f_wt_ready", "f_base", "f_x2", "f_qkp_ready", "f_avp_ready"))
        (a_var, a_rstd, a_n_done, a_ht_mm, a_ht_sb, a_qkv_mm, a_qk_sb, a_v_sb, a_sc_mm, a_sc_sb, a_masked, a_top,
         a_exp_done, a_picked, a_p_ready, a_pt_mm, a_pt_sb, a_o_mm, a_base, a_x3, a_var2, a_rstd2, a_n2_done,
         a_h2_mm, a_h2_sb, a_lg_mm, a_lg_ready, a_ge_done, a_w_ready, a_rexp_done, a_pv_free) = (
            sem(n) for n in ("a_var", "a_rstd", "a_n_done", "a_ht_mm", "a_ht_sb", "a_qkv_mm", "a_qk_sb", "a_v_sb",
                             "a_sc_mm", "a_sc_sb", "a_masked", "a_top", "a_exp_done", "a_picked", "a_p_ready",
                             "a_pt_mm", "a_pt_sb", "a_o_mm", "a_base", "a_x3", "a_var2", "a_rstd2", "a_n2_done",
                             "a_h2_mm", "a_h2_sb", "a_lg_mm", "a_lg_ready", "a_ge_done", "a_w_ready", "a_rexp_done", "a_pv_free"))
        m_gu_mm, m_tanh, m_hid, m_y_mm, m_y_sb, m_sum, m_out = (
            sem(n) for n in ("m_gu_mm", "m_tanh", "m_hid", "m_y_mm", "m_y_sb", "m_sum", "m_out"))
        slot_free = [sem(f"slot_free{i}") for i in range(4)]

        NE = E + 1

        def chunks(a):
            return [(c * CH, min(CH, (a + 1) * P - c * CH)) for c in range(((a + 1) * P + CH - 1) // CH)]

        chunks_before = [sum(len(chunks(b)) for b in range(a)) for a in range(NB + 1)]

        def att_uses():
            n = 0
            for s in range(NB + 1):
                for a, k in ((s - 1, 1), (s, 0)):
                    if 0 <= a < NB:
                        for c in range(len(chunks(a))):
                            yield (a, k, c), n
                            n += 1

        att_use = dict(att_uses())
        att_user = {n: key for key, n in att_use.items()}

        def row(ap, n):
            return ap.rearrange("(o n) -> o n", o=1).broadcast_to([P, n])

        def over_blocks(ap, n):
            return ap.rearrange("p (o f) -> p o f", o=1).broadcast_to([P, n, P])

        STEPS = NB + 7

        def on(b):
            return 0 <= b < NB

        block = ctx.enter_context(nc.Block())

        @block.sync
        def _(sp):
            x = d["L0_attn_x"].rearrange("o t f -> (o t) f")
            sp.dma_start(x_str[:, 0:8, :], x.rearrange("(r j) f -> r j f", j=NB)[:, 0:8, :]).then_inc(in_xa, 16)
            sp.dma_start(x_str[:, 8:16, :], x.rearrange("(r j) f -> r j f", j=NB)[:, 8:16, :]).then_inc(in_xb, 16)
            for t, n in ((w0v, "L0_attn_Wv"), (wdown, "L0_ffn_Wdown"), (wup, "L0_ffn_Wup"), (w1v, "L1_attn_Wv"),
                         (w1o, "L1_attn_Wo")):
                sp.dma_start(t[:], d[n]).then_inc(in_tr, 16)
            for t, n in ((w0q, "L0_attn_Wq"), (w0k, "L0_attn_Wk"), (w0o, "L0_attn_Wo")):
                sp.dma_start(t[:], d[n]).then_inc(in_w0, 16)
            sp.dma_start(bup_row[:], row(d["L0_ffn_bup"], 2 * P)).then_inc(in_rows, 16)
            for k, name in enumerate(("L0_attn_bo", "L0_ffn_bq", "L0_ffn_bo", "L1_attn_bo")):
                sp.dma_start(rows[:, k, :], row(d[name], P)).then_inc(in_rows, 16)
            for t, n in ((wfq, "L0_ffn_Wq"), (wfo, "L0_ffn_Wo"), (wfg, "L0_ffn_Wg")):
                sp.dma_start(t[:], d[n]).then_inc(in_f, 16)
            sp.dma_start(x_blk[:], x.rearrange("(j r) f -> r j f", r=P)).then_inc(in_x, 16)
            sp.dma_start(wfe[:], d["L0_ffn_We"].rearrange("e i f -> i e f")).then_inc(in_f, 16)
            for k, name in ((3, "L1_attn_bq"), (4, "L1_attn_bk")):
                sp.dma_start(cols[:, k:k + 1], d[name].rearrange("(f o) -> f o", o=1)).then_inc(in_1, 16)
            for t, n in ((w1q, "L1_attn_Wq"), (w1k, "L1_attn_Wk"), (w1r, "L1_ffn_gate_w")):
                sp.dma_start(t[:], d[n]).then_inc(in_1, 16)
            sp.dma_start(bg_row[:], row(d["L0_ffn_bg"], E)).then_inc(in_1, 16)
            sp.dma_start(wgate[:, 0:E, :], d["L1_ffn_w_gate"].rearrange("e i f -> i e f")).then_inc(in_moe, 16)
            sp.dma_start(wups[:, 0:E, :], d["L1_ffn_w_up"].rearrange("e i f -> i e f")).then_inc(in_moe, 16)
            sp.dma_start(wdn[:, 0:E, :, :],
                         d["L1_ffn_w_down"].rearrange("e (c r) f -> r e c f", r=P)).then_inc(in_moe, 16)
            sp.dma_start(wgate[:, E, :], d["L1_ffn_ws_gate"]).then_inc(in_moe, 16)
            sp.dma_start(wups[:, E, :], d["L1_ffn_ws_up"]).then_inc(in_moe, 16)
            sp.dma_start(wdn[:, E, :, :], d["L1_ffn_ws_down"].rearrange("(c r) f -> r c f", r=P)).then_inc(in_moe, 16)
            o = out.rearrange("o (b r) f -> (o b) r f", r=P)
            for m in range(NB):
                sp.wait_ge(m_out, m + 1)
                sp.dma_start(o[m], x4[:, m % 4, :]).then_inc(slot_free[m % 4], 16)
            for k in range(4):
                sp.wait_ge(slot_free[k], 16 * NB // 4)

        @block.gpsimd
        def _(pool):
            n = [0]

            def link(ins):
                n[0] += 1
                ins.then_inc(pool_chain, 1)
                pool.wait_ge(pool_chain, n[0])

            g = nc.gpsimd
            g.memset(ones[:], 1.0)
            g.memset(neg_half[:], -0.5)
            g.memset(head_rows[:], 1.0)
            g.memset(head_cols[:], 1.0)
            g.memset(lane_rows[:], 0.0)
            link(g.memset(ident[:], 0.0))
            g.affine_select(out=ident[:], in_=ident[:], compare_op=ALU.not_equal, fill=1.0, base=0,
                            pattern=[[-1, P]], channel_multiplier=1)
            g.affine_select(out=head_rows[:], in_=head_rows[:], compare_op=ALU.is_ge, fill=0.0, base=0,
                            pattern=[[1, P]], channel_multiplier=-HD)
            g.affine_select(out=head_cols[:], in_=head_cols[:], compare_op=ALU.is_ge, fill=0.0, base=0,
                            pattern=[[-HD, H]], channel_multiplier=1)
            link(g.affine_select(out=lane_rows[:], in_=lane_rows[:], compare_op=ALU.not_equal, fill=1.0, base=0,
                                 pattern=[[0, H], [1, HD]], channel_multiplier=-1))
            g.affine_select(out=head_rows[:], in_=head_rows[:], compare_op=ALU.is_ge, fill=0.0, base=HD - 1,
                            pattern=[[-1, P]], channel_multiplier=HD)
            g.affine_select(out=head_cols[:], in_=head_cols[:], compare_op=ALU.is_ge, fill=0.0, base=HD - 1,
                            pattern=[[HD, H]], channel_multiplier=-1)
            g.iota(iota8[:], pattern=[[1, E]], base=0, channel_multiplier=0,
                   allow_small_or_imprecise_dtypes=True).then_inc(consts, 1)

            def rsqrt(out, var, scale, eps, done):
                link(g.tensor_scalar(out, var, scale, eps, ALU.mult, ALU.add))
                ins = g.tensor_tensor(out, out, neg_half[:, 0:out.shape[1]], ALU.pow)
                if done is None:
                    link(ins)
                else:
                    ins.then_inc(done, 1)

            def norm(rs, shift, mv, done):
                rsqrt(rs, mv[:, 1:2], 1.0, LN_EPS, None)
                g.tensor_scalar(shift, mv[:, 0:1], rs, -1.0, ALU.mult, ALU.mult).then_inc(done, 1)

            for k in range(2):
                j = slice(8 * k, 8 * k + 8)
                pool.wait_ge(var0, k + 1)
                rsqrt(rs0[:, j], mv0[:, j, 1], 1.0, LN_EPS, rstd0)
            pool.wait_ge(in_cols, 64)
            g.tensor_scalar(bcols[:, 1, :], ones[:], cols[:, 5:6], None, ALU.mult)
            g.tensor_scalar(bcols[0:64, 0, :], ones[0:64, :], cols[0:64, 2:3], None, ALU.mult).then_inc(bcol_ready, 1)
            for q in (0, 1, 3):
                pool.wait_ge(scaled0, q + 1)
                j = slice(4 * q, 4 * q + 4)
                g.tensor_tensor(h_str[:, j, :], h_tmp[:, j, :], over_blocks(mod0[:, 0, :], 4),
                                ALU.add).then_inc(h0_ready, 1)
            pool.wait_ge(in_x, 16)
            pool.wait_ge(gates_ready, 1)
            for q in range(4):
                j = slice(4 * q, 4 * q + 4)
                g.tensor_tensor(x_blk[:, j, :], x_blk[:, j, :], over_blocks(bo0G[:], 4), ALU.add).then_inc(xb_ready, 1)
            pool.wait_ge(in_moe, 96)
            pool.wait_ge(gates1_ready, 1)
            w = wdnG[:].rearrange("p e c f -> p (e c) f")
            g.tensor_tensor(w, w, over_blocks(mod1[:, 1, :], 2 * NE), ALU.mult).then_inc(prep_pool, 1)

            def f_norm(f):
                pool.wait_ge(f_var, f + 1)
                norm(rsF[:, f:f + 1], shF[:, f:f + 1], mvF[:, f, :], f_rstd)

            def f_modulate(f):
                pool.wait_ge(f_n_done, f + 1)
                if f >= 1:
                    pool.wait_ge(f_ssq, f)
                link(g.tensor_tensor(hF1[:], nF[:], mod0[:, 4, :], ALU.mult))
                g.tensor_tensor(hF[:], hF1[:], mod0[:, 3, :], ALU.add).then_inc(f_h_ready, 1)

            def f_residual(f):
                pool.wait_ge(f_h_ready, f + 1)
                if f >= 2:
                    pool.wait_ge(f_z_ready, f - 1)
                g.tensor_tensor(hFb[:, f % 2, :], hF[:], rows[:, 2, :], ALU.add).then_inc(f_hb_ready, 1)

            def f_rms1(f):
                pool.wait_ge(f_ssq, f + 1)
                rsqrt(rmsF[:, f, 0:1], ssqF[:, f, 0:1], 1.0 / P, RMS_EPS, f_rms)

            def halve(src, dst, n, done=None):
                ins = g.tensor_tensor(dst, src[:, :, :, 0:n // 2], src[:, :, :, n // 2:n], ALU.add)
                if done is None:
                    link(ins)
                else:
                    ins.then_inc(done, 1)

            def f_qk_pool(f):
                pool.wait_ge(f_qkv_sb, f + 1)
                qkv = qkvF[:, f % 2, :]
                a = prodP[:, 0, :].rearrange("p (h g d) -> p h g d", h=PH, g=H)
                b = prodP[:, 1, :].rearrange("p (h g d) -> p h g d", h=PH, g=H)
                qq = qkv[:, 0:P].rearrange("p (h o d) -> p h o d", h=H, o=1)[:, 0:PH].broadcast_to([P, PH, H, HD])
                kk = qkv[:, P:2 * P].rearrange("p (o g d) -> p o g d", o=1, g=H).broadcast_to([P, PH, H, HD])
                link(g.tensor_tensor(a, qq, kk, ALU.mult))
                halve(a, b[:, :, :, 0:4], 8)
                halve(b, a[:, :, :, 0:2], 4)
                if f >= 1:
                    pool.wait_ge(f_exp_done, f)
                halve(a, scF[:, 0:PH, :].rearrange("p h (g o) -> p h g o", o=1), 2, f_qkp_ready)

            def f_av_pool(f, part):
                qkv = qkvF[:, f % 2, :]
                a = prodP[:, 0, :].rearrange("p (h d g) -> p h d g", h=PH, d=HD)
                b = prodP[:, 1, :].rearrange("p (h d g) -> p h d g", h=PH, d=HD)
                if part == 0:
                    pool.wait_ge(f_exp_done, f + 1)
                    pp = peF[:, f % 2].rearrange("p h (o g) -> p h o g", o=1)[:, 0:PH].broadcast_to([P, PH, HD, H])
                    vv = qkv[:, 2 * P:].rearrange("p (o d g) -> p o d g", o=1, g=H).broadcast_to([P, PH, HD, H])
                    link(g.tensor_tensor(a, pp, vv, ALU.mult))
                else:
                    if f >= 1:
                        pool.wait_ge(f_o_ready, f)
                    halve(a, b[:, :, :, 0:8], 16)
                    halve(b, a[:, :, :, 0:4], 8)
                    halve(a, b[:, :, :, 0:2], 4)
                    halve(b, oF[:, 0:PH, :].rearrange("p h (d o) -> p h d o", o=1), 2, f_avp_ready)

            def f_rms2_(f):
                pool.wait_ge(f_ssq2, f + 1)
                rsqrt(rmsF[:, f, 1:2], ssqF[:, f, 1:2], 1.0 / P, RMS_EPS, f_rms2)

            def f_base_(f):
                pool.wait_ge(f_z_ready, f + 1)
                link(g.tensor_tensor(zg[:], zF[:], mod0[:, 5, :], ALU.mult))
                if f >= 1:
                    pool.wait_ge(f_x2, f)
                g.tensor_tensor(exF[:, :, E], zg[:], x1[:, f, :], ALU.add).then_inc(f_base, 1)

            def a_norm(a, k):
                pool.wait_ge((a_var, a_var2)[k], a + 1)
                norm(rsA[:, a, k:k + 1], shA[:, a, k:k + 1], mvA[:, a, k, :], (a_rstd, a_rstd2)[k])

            def a_base_(a):
                pool.wait_ge(f_x2, a + 1)
                if a == 0:
                    pool.wait_ge(prep_dve, 1)
                if a >= 2:
                    pool.wait_ge(a_x3, a - 1)
                g.tensor_tensor(x2b[:, a % 2, :], x2[:, a, :], bo1G[:], ALU.add).then_inc(a_base, 1)

            def a_mask(a):
                pool.wait_ge(a_sc_sb, chunks_before[a + 1])
                diag = S[:, a * P:(a + 1) * P]
                g.affine_select(out=diag, in_=diag, compare_op=ALU.is_ge, fill=MASKED, base=0,
                                pattern=[[-1, P]], channel_multiplier=1).then_inc(a_masked, 1)

            def a_weights(a):
                pool.wait_ge(a_rexp_done, a + 1)
                if a >= 2:
                    pool.wait_ge(a_pt_mm, chunks_before[a - 1])
                w = (a + 1) * P
                g.tensor_tensor(W[:, a % 2, 0:w], X[:, 0:w], R[:, 0:w], ALU.subtract).then_inc(a_p_ready, 1)

            def m_out_(m):
                pool.wait_ge(m_sum, m + 1)
                if m >= 4:
                    pool.wait_ge(slot_free[m % 4], 16 * (m // 4))
                g.tensor_tensor(x4[:, m % 4, :], ysum[:, m % 2, :], x3[:, m % 4, :], ALU.add).then_inc(m_out, 1)

            for s in range(STEPS):
                if on(s):
                    f_norm(s)
                if on(s - 7):
                    m_out_(s - 7)
                if on(s):
                    f_modulate(s)
                if on(s - 2):
                    a_norm(s - 2, 0)
                if on(s):
                    f_rms1(s)
                if on(s - 1):
                    f_av_pool(s - 1, 1)
                if on(s - 3):
                    a_norm(s - 3, 1)
                if on(s):
                    f_residual(s)
                if on(s - 2):
                    a_base_(s - 2)
                    a_mask(s - 2)
                if on(s):
                    f_qk_pool(s)
                if on(s - 1):
                    f_rms2_(s - 1)
                    f_base_(s - 1)
                if on(s - 2):
                    a_weights(s - 2)
                if on(s):
                    f_av_pool(s, 0)

        @block.scalar
        def _(act):
            n = [0]

            def link(ins):
                n[0] += 1
                ins.then_inc(act_chain, 1)
                act.wait_ge(act_chain, n[0])

            sc = nc.scalar
            act.dma_start(c_col[:, 0:1], d["L0_c"].rearrange("o f -> f o")).then_inc(in_c, 16)
            act.dma_start(c_col[:, 1:2], d["L1_c"].rearrange("o f -> f o")).then_inc(in_c, 16)
            act.dma_start(wmod[:, 0, :], d["L0_wmod"]).then_inc(in_mod0, 16)
            act.dma_start(wmod[:, 1, :], d["L1_wmod"]).then_inc(in_mod1, 16)
            act.wait_ge(in_c, 32)
            sc.activation(silu_t[:], c_col[:], ACT.Tanh, scale=0.5).then_inc(silu_tanh, 1)
            for k, name in ((2, "L0_ffn_bdown"), (5, "L1_attn_bv"), (0, "L0_ffn_gamma1"), (1, "L0_ffn_gamma2")):
                m = d[name].shape[0]
                act.dma_start(cols[0:m, k:k + 1], d[name].rearrange("(f o) -> f o", o=1)).then_inc(in_cols, 16)

            act.wait_ge(mod0_mm, 1)
            sc.copy(mod0[:, 0:3, :], bank[0][:, 0:3 * P].rearrange("p (c f) -> p c f", c=3))
            sc.copy(mod0[:, 3:6, :], bank[1][:, 0:3 * P].rearrange("p (c f) -> p c f", c=3)).then_inc(mod0_sb, 1)
            act.wait_ge(rstd0, 2)
            act.wait_ge(shift0, 1)
            for j in range(NB - NA0, NB):
                last = sc.activation(h_tmp[:, j, :], x_str[:, j, :], ACT.Identity, scale=rs0[:, j:j + 1],
                                     bias=sh0[:, j:j + 1])
            last.then_inc(n0_act, 1)
            act.wait_ge(mod1_mm, 1)
            sc.copy(mod1[:], bank[2][:, 0:2 * P].rearrange("p (c f) -> p c f", c=2)).then_inc(mod1_sb, 1)
            act.wait_ge(col_mm, 1)
            sc.copy(mcol[:], bank[3][:, 0:4]).then_inc(col_sb, 1)
            act.wait_ge(lane_mm, 1)
            sc.copy(same_lane[:], bank[4][:, 0:P]).then_inc(lane_sb, 1)
            act.wait_ge(tr_mm, 1)
            sc.copy(wdownT[:], bank[5][0:64, 2 * P:3 * P])
            sc.copy(w1vT[:], bank[5][:, P:2 * P])
            sc.copy(w0vT[:], bank[5][:, 0:P]).then_inc(tr_sb, 1)
            for q in range(4):
                act.wait_ge(hT0_mm, q + 1)
                sc.copy(hT_str[:, 4 * q:4 * q + 4, :],
                        bank[q % 2][:].rearrange("p (j t) -> p j t", j=4)).then_inc(hT0_sb, 1)
            act.wait_ge(hneg, 1)
            sc.activation(hatt[:], hsc[:], ACT.Exp, bias=hmx[:, 1:2], scale=HD ** -0.5,
                          accum_out=hmx[:, 2:3]).then_inc(hexp, 1)
            for q in range(1, 4, 2):
                act.wait_ge(z0_mm, q + 1)
                sc.copy(mixed[:].rearrange("r a (j d) -> r j a d", j=NB)[:, 4 * q:4 * q + 4, :, :],
                        bank[4 + q][:].rearrange("r (j a d) -> r j a d", j=4, a=H)).then_inc(z0_sb, 1)

            def f_xt(f):
                act.wait_ge(f_xt_mm, f + 1)
                sc.copy(xT[:], f1_bank[:, 0:P]).then_inc(f_xt_sb, 1)

            def f_n(f):
                act.wait_ge(f_rstd, f + 1)
                if f >= 1:
                    act.wait_ge(f_h_ready, f)
                sc.activation(nF[:], x1[:, f, :], ACT.Identity, scale=rsF[:, f:f + 1],
                              bias=shF[:, f:f + 1]).then_inc(f_n_done, 1)

            def a_n(a, k):
                act.wait_ge((a_rstd, a_rstd2)[k], a + 1)
                sc.activation(nA[:, k, :], (x2[:, a, :], x3[:, a % 4, :])[k], ACT.Identity, scale=rsA[:, a, k:k + 1],
                              bias=shA[:, a, k:k + 1]).then_inc((a_n_done, a_n2_done)[k], 1)

            def f_ht(f):
                act.wait_ge(f_ht_mm, f + 1)
                sc.copy(hFT[:], f1_bank[:, 0:P]).then_inc(f_ht_sb, 1)
                sc.activation(sq_junk[:, 0, :], hF[:], ACT.Square, accum_out=ssqF[:, f, 0:1]).then_inc(f_ssq, 1)

            def f_exp(f):
                act.wait_ge(f_sc_ready, f + 1)
                if f >= 2:
                    act.wait_ge(f_o_ready, f - 1)
                sc.activation(peF[:, f % 2], scF[:], ACT.Exp, scale=HD ** -0.5).then_inc(f_exp_done, 1)

            def f_ot(f):
                act.wait_ge(f_ot_mm, f + 1)
                sc.copy(oFT[:], f2_bank[:, 0:P]).then_inc(f_ot_sb, 1)

            def f_zt(f):
                act.wait_ge(f_zt_mm, f + 1)
                sc.copy(zFT[:], f2_bank[:, 0:P]).then_inc(f_zt_sb, 1)
                sc.activation(sq_junk[:, 1, :], zF[:], ACT.Square, accum_out=ssqF[:, f, 1:2]).then_inc(f_ssq2, 1)

            def f_ge(f):
                act.wait_ge(f_lg_ready, f + 1)
                sc.activation(geF[:], lgF[:], ACT.Exp, bias=nmF[:], accum_out=gsF[:, 0:1]).then_inc(f_ge_done, 1)

            def f_shares(f, half):
                act.wait_ge(f_e_mm, 2 * f + half + 1)
                act.wait_ge(f_wt_ready, f + 1)
                if half == 0 and f >= 1:
                    act.wait_ge(f_x2, f)
                for i in range(4):
                    e = 4 * half + i
                    last = sc.activation(exF[:, :, e], f2_bank[:, i * P:(i + 1) * P], ACT.Identity,
                                         scale=wtF[:, e:e + 1])
                last.then_inc(f_e_sb, 1)

            def a_ht(a, k):
                act.wait_ge((a_ht_mm, a_h2_mm)[k], a + 1)
                if a == 0 and k == 0:
                    act.wait_ge(prep_dve, 1)
                if k == 1 and a >= 2:
                    act.wait_ge(m_gu_mm, (a - 1) * NE)
                dst = hAT[:] if k == 0 else h2T[:, a % 2, :]
                sc.activation(dst, a_bank[:, 0:P], ACT.Identity, scale=mcol[:, 2 * k + 1:2 * k + 2],
                              bias=mcol[:, 2 * k:2 * k + 1]).then_inc((a_ht_sb, a_h2_sb)[k], 1)

            def a_qk(a):
                act.wait_ge(a_qkv_mm, a + 1)
                if a >= 1:
                    act.wait_ge(a_sc_mm, chunks_before[a])
                sc.activation(qT[:], a_bank[:, 0:P], ACT.Identity, bias=cols[:, 3:4])
                sc.activation(kT[:, a * P:(a + 1) * P], a_bank[:, P:2 * P], ACT.Identity,
                              bias=cols[:, 4:5]).then_inc(a_qk_sb, 1)
                sc.copy(vA[:, a, :], a_bank[:, 2 * P:3 * P]).then_inc(a_v_sb, 1)

            def a_scores(a):
                if a >= 1:
                    act.wait_ge(a_picked, a)
                for c, (lo, w) in enumerate(chunks(a)):
                    act.wait_ge(a_sc_mm, chunks_before[a] + c + 1)
                    sc.mul(S[:, lo:lo + w], att_bank[att_use[a, 0, c] % 2][:, 0:w], P ** -0.5).then_inc(a_sc_sb, 1)

            def a_exp(a):
                act.wait_ge(a_top, a + 1)
                if a >= 1:
                    act.wait_ge(a_p_ready, a)
                if a >= 2:
                    act.wait_ge(a_x3, a - 1)
                w = (a + 1) * P
                sc.activation(X[:, 0:w], S[:, 0:w], ACT.Exp, bias=nmA[:])
                sc.activation(top_e[:], top[:], ACT.Exp, bias=nmA[:], accum_out=sumA[:, a % 2, 0:1]).then_inc(
                    a_exp_done, 1)

            def a_rexp(a):
                act.wait_ge(a_picked, a + 1)
                w = (a + 1) * P
                sc.activation(R[:, 0:w], R[:, 0:w], ACT.Exp, bias=nmA[:]).then_inc(a_rexp_done, 1)

            def a_pt(a, c):
                if c < len(chunks(a)):
                    lo, w = chunks(a)[c]
                    act.wait_ge(a_pt_mm, chunks_before[a] + c + 1)
                    if c == 0 and a >= 1:
                        act.wait_ge(a_o_mm, a)
                    sc.copy(PT[:, lo:lo + w], att_bank[att_use[a, 1, c] % 2][:, 0:w]).then_inc(a_pt_sb, 1)

            def a_ge(a):
                act.wait_ge(a_lg_ready, a + 1)
                sc.activation(peR[:], lgR[:], ACT.Exp, bias=nmR[:], accum_out=suR[:, 0:1]).then_inc(a_ge_done, 1)

            def m_th(m, e):
                u = m * NE + e
                act.wait_ge(m_gu_mm, u + 1)
                if u >= 2:
                    act.wait_ge(m_hid, u - 1)
                sc.activation(th[:, u % 2, :], gu_bank[u % 2][:, 0:HID], ACT.Tanh, scale=0.5).then_inc(m_tanh, 1)

            def m_shares(m, grp):
                es = (range(0, 4), range(4, 8), range(8, 9))[grp]
                act.wait_ge(m_y_mm, m * NE + es[-1] + 1)
                if grp == 0:
                    act.wait_ge(a_w_ready, m + 1)
                    if m >= 2:
                        act.wait_ge(m_sum, m - 1)
                for i, e in enumerate(es):
                    scale = wtR[:, m, e:e + 1] if e < E else 1.0
                    last = sc.activation(exM[:, m % 2, :, e], y_bank[:, i * P:(i + 1) * P], ACT.Identity, scale=scale)
                last.then_inc(m_y_sb, 1)

            for s in range(STEPS):
                if on(s - 3):
                    f_shares(s - 3, 0)
                if on(s - 6):
                    m_shares(s - 6, 2)
                if on(s - 5):
                    m_th(s - 5, 0)
                if on(s - 3):
                    f_shares(s - 3, 1)
                if on(s - 5):
                    m_th(s - 5, 1)
                if on(s - 4):
                    a_pt(s - 4, 0)
                    a_pt(s - 4, 1)
                if on(s - 1):
                    f_n(s - 1)
                if on(s - 5):
                    m_th(s - 5, 2)
                if on(s - 4):
                    a_pt(s - 4, 2)
                if on(s - 1):
                    f_ht(s - 1)
                if on(s - 4):
                    a_pt(s - 4, 3)
                if on(s - 3):
                    a_n(s - 3, 0)
                    a_ht(s - 3, 0)
                if on(s - 5):
                    m_th(s - 5, 3)
                if on(s - 3):
                    a_qk(s - 3)
                if on(s - 5):
                    m_th(s - 5, 4)
                if on(s - 3):
                    a_scores(s - 3)
                if on(s - 5):
                    m_shares(s - 5, 0)
                if on(s - 2):
                    f_ot(s - 2)
                if on(s - 5):
                    m_th(s - 5, 5)
                if on(s - 4):
                    a_n(s - 4, 1)
                    a_ht(s - 4, 1)
                if on(s - 5):
                    m_th(s - 5, 6)
                if on(s - 2):
                    f_zt(s - 2)
                if on(s - 3):
                    a_exp(s - 3)
                if on(s - 5):
                    m_th(s - 5, 7)
                if on(s - 3):
                    a_rexp(s - 3)
                if on(s - 5):
                    m_th(s - 5, 8)
                if on(s - 2):
                    f_ge(s - 2)
                if on(s - 5):
                    m_shares(s - 5, 1)
                if on(s - 4):
                    a_ge(s - 4)
                if on(s - 1):
                    f_exp(s - 1)
                if on(s):
                    f_xt(s)

        @block.vector
        def _(dve):
            n = [0]

            def link(ins):
                n[0] += 1
                ins.then_inc(dve_chain, 1)
                dve.wait_ge(dve_chain, n[0])

            v = nc.vector

            at = {}

            def mark(what, ins):
                n[0] += 1
                ins.then_inc(dve_chain, 1)
                at[what] = n[0]

            def after(what):
                dve.wait_ge(dve_chain, at[what])

            def stats0(k):
                dve.wait_ge((in_xa, in_xb)[k], 16)
                for j in range(8 * k, 8 * k + 8):
                    last = v.bn_stats(st0[:, j, :], x_str[:, j, :])
                link(last)
                for j in range(8 * k, 8 * k + 8):
                    last = v.bn_aggr(mv0[:, j, :], st0[:, j, :])
                last.then_inc(var0, 1)

            def normalise0(j0, j1):
                for j in range(j0, j1):
                    last = v.tensor_scalar(h_tmp[:, j, :], x_str[:, j, :], mv0[:, j, 0:1], rs0[:, j:j + 1],
                                           ALU.subtract, ALU.mult)
                mark("n0", last)

            stats0(0)
            dve.wait_ge(silu_tanh, 1)
            dve.wait_ge(consts, 1)
            link(v.scalar_tensor_tensor(silu_c[:], silu_t[:], 1.0, c_col[:], ALU.add, ALU.mult))
            v.tensor_scalar(silu_b[:, 0, :], ones[:], silu_c[:, 0:1], 0.5, ALU.mult, ALU.mult)
            v.tensor_scalar(silu_b[:, 1, :], ones[:], silu_c[:, 1:2], 0.5, ALU.mult, ALU.mult).then_inc(silu_rows, 1)
            stats0(1)
            dve.wait_ge(var0, 2)
            dve.wait_ge(rstd0, 1)
            normalise0(0, 8)
            dve.wait_ge(rstd0, 2)
            v.scalar_tensor_tensor(sh0[:, 8:16], mv0[:, 8:16, 0], -1.0, rs0[:, 8:16], ALU.mult,
                                   ALU.mult).then_inc(shift0, 1)
            normalise0(8, NB - NA0)
            dve.wait_ge(mod0_sb, 1)
            mark("1 + ca", v.tensor_scalar(mod0[:, 1, :], mod0[:, 1, :], 1.0, None, ALU.add))
            v.tensor_scalar(mod0[:, 4, :], mod0[:, 4, :], 1.0, None, ALU.add)
            after("n0")
            after("1 + ca")
            dve.wait_ge(n0_act, 1)
            for q in range(4):
                j = slice(4 * q, 4 * q + 4)
                v.tensor_tensor(h_tmp[:, j, :], h_tmp[:, j, :], over_blocks(mod0[:, 1, :], 4),
                                ALU.mult).then_inc(scaled0, 1)
            dve.wait_ge(scaled0, 3)
            v.tensor_tensor(h_str[:, 8:12, :], h_tmp[:, 8:12, :], over_blocks(mod0[:, 0, :], 4),
                            ALU.add).then_inc(h0_dve, 1)

            def gate(src, k, step):
                if step == 0:
                    v.tensor_scalar(gsign[:, k, :], src, 0.0, 2.0, ALU.is_ge, ALU.mult)
                    mark(("gate", k), v.scalar_tensor_tensor(gmag[:, k, :], src, -1.0, src, ALU.mult, ALU.max))
                elif step == 1:
                    after(("gate", k))
                    mark(("gate", k), v.tensor_scalar(gmag[:, k, :], gmag[:, k, :], 0.25, None, ALU.max))
                else:
                    after(("gate", k))
                    mark(("gate", k), v.scalar_tensor_tensor(src, gsign[:, k, :], 1.0, gmag[:, k, :], ALU.subtract,
                                                             ALU.mult))

            for step in range(3):
                gate(mod0[:, 2, :], 0, step)
                gate(mod0[:, 5, :], 1, step)
            dve.wait_ge(in_rows, 16 * 5)
            dve.wait_ge(in_w0, 48)
            after(("gate", 0))
            v.tensor_tensor(bo0G[:], rows[:, 0, :], mod0[:, 2, :], ALU.mult)
            v.tensor_tensor(w0oG[:], w0o[:], mod0[:, 2, :], ALU.mult).then_inc(gates_ready, 1)

            dve.wait_ge(gram_mm, 1)
            v.tensor_copy(gram[:], bank[2][:, 0:P]).then_inc(gram_sb, 1)
            dve.wait_ge(fold_mm, 1)
            dve.wait_ge(in_cols, 64)
            wkv = bank[6][:, 0:2 * P].rearrange("p (g k d) -> p k g d", g=H, k=2)
            v.tensor_scalar(wqkv[:, P:2 * P].rearrange("p (g d) -> p g d", g=H), wkv[:, 0], cols[:, 0:1], None,
                            ALU.mult)
            v.tensor_scalar(wqkv[:, 2 * P:].rearrange("p (d g) -> p g d", g=H), wkv[:, 1], cols[:, 0:1], None,
                            ALU.mult)
            dve.wait_ge(gramk_mm, 1)
            v.tensor_copy(gramk[:], bank[3][:, 0:P]).then_inc(gramk_sb, 1)
            mark("bkv", v.tensor_tensor(bkv[:], bank[6][:, 2 * P:4 * P], bup_row[:], ALU.add))
            v.tensor_copy(bqkv[:, 0:P], rows[:, 1, :])
            dve.wait_ge(qk_mm, 1)
            dve.wait_ge(lane_sb, 1)
            link(v.tensor_tensor(qk_m[:], bank[2][:, 0:P], same_lane[:], ALU.mult))
            v.tensor_reduce(qk_r[:], qk_m[:].rearrange("p (b d) -> p b d", d=HD), AX.X, ALU.add).then_inc(qkr_ready, 1)
            after("bkv")
            bk = bkv[:].rearrange("p (g k d) -> p k g d", g=H, k=2)
            v.tensor_copy(bqkv[:, P:2 * P].rearrange("p (g d) -> p g d", g=H), bk[:, 0])
            v.tensor_copy(bqkv[:, 2 * P:].rearrange("p (d g) -> p g d", g=H), bk[:, 1])
            dve.wait_ge(hsc_mm, 1)
            link(v.tensor_copy(hsc[:], bank[3][0:H, 0:H]))
            link(v.tensor_reduce(hmx[:, 0:1], hsc[:], AX.X, ALU.max))
            v.tensor_scalar(hmx[:, 1:2], hmx[:, 0:1], -HD ** -0.5, None, ALU.mult).then_inc(hneg, 1)
            dve.wait_ge(mod1_sb, 1)
            dve.wait_ge(col_sb, 1)
            gate(mod1[:, 0, :], 2, 0)
            dve.wait_ge(hexp, 1)
            link(v.reciprocal(hmx[:, 3:4], hmx[:, 2:3]))
            v.tensor_scalar(hatt[:], hatt[:], hmx[:, 3:4], None, ALU.mult).then_inc(hatt_ready, 1)
            gate(mod1[:, 1, :], 3, 0)
            dve.wait_ge(hspr_mm, 1)
            v.tensor_copy(hspread[:], bank[2][0:H, 0:P]).then_inc(hspr_sb, 1)
            gate(mod1[:, 0, :], 2, 1)
            gate(mod1[:, 1, :], 3, 1)
            dve.wait_ge(hmix_mm, 1)
            v.tensor_tensor(hmix[:], bank[3][:, 0:P], same_lane[:], ALU.mult).then_inc(hmix_sb, 1)
            gate(mod1[:, 0, :], 2, 2)
            gate(mod1[:, 1, :], 3, 2)
            dve.wait_ge(wva_mm, 1)
            v.tensor_copy(w0vA[:], bank[2][:, 0:P]).then_inc(wva_sb, 1)
            after(("gate", 2))
            v.tensor_tensor(w1vo[:], bank[7][:, 0:P], mod1[:, 0, :], ALU.mult)
            mark("bvo", v.tensor_tensor(bvo[:], bank[7][:, P:2 * P], rows[:, 3, :], ALU.add))
            after(("gate", 3))
            v.tensor_scalar(mod1[:, 1, :], mod1[:, 1, :], 0.5, None, ALU.mult).then_inc(gates1_ready, 1)
            v.tensor_scalar(mcol[:, 1:2], mcol[:, 1:2], 1.0, None, ALU.add)
            v.tensor_scalar(mcol[:, 3:4], mcol[:, 3:4], 1.0, None, ALU.add)
            after("bvo")
            v.tensor_tensor(bo1G[:], bvo[:], mod1[:, 0, :], ALU.mult).then_inc(prep_dve, 1)
            dve.wait_ge(in_f, 64)
            v.tensor_scalar(wqkv[:, 0:P], wfq[:], cols[:, 0:1], None, ALU.mult).then_inc(mods_first, 1)
            dve.wait_ge(z0_mm, 1)
            v.tensor_copy(mixed[:].rearrange("r a (j d) -> r j a d", j=NB)[:, 0:4, :, :],
                          bank[4][:].rearrange("r (j a d) -> r j a d", j=4, a=H)).then_inc(z0_sb, 1)
            v.tensor_scalar(wfgG[:], wfg[:], cols[:, 1:2], None, ALU.mult)
            after(("gate", 1))
            v.scalar_tensor_tensor(wfeG[:], wfe[:], cols[:, 1:2], over_blocks(mod0[:, 5, :], E), ALU.mult,
                                   ALU.mult).then_inc(wfe_ready, 1)
            dve.wait_ge(z0_mm, 3)
            v.tensor_copy(mixed[:].rearrange("r a (j d) -> r j a d", j=NB)[:, 8:12, :, :],
                          bank[6][:].rearrange("r (j a d) -> r j a d", j=4, a=H)).then_inc(z0_sb, 1)

            def f_x1(f):
                dve.wait_ge(f_wo_mm, f + 1)
                dve.wait_ge(xb_ready, f // 4 + 1)
                mark("x1", v.tensor_tensor(x1[:, f, :], f1_bank[:, 0:P], x_blk[:, f, :], ALU.add))

            def f_bn(f):
                after("x1")
                mark("x1 stats", v.bn_stats(stF[:, f, :], x1[:, f, :]))

            def f_aggr(f):
                after("x1 stats")
                v.bn_aggr(mvF[:, f, :], stF[:, f, :]).then_inc(f_var, 1)

            def f_qkv(f):
                dve.wait_ge(f_qkv_mm, f + 1)
                dve.wait_ge(f_rms, f + 1)
                if f >= 2:
                    dve.wait_ge(f_avp_ready, f - 1)
                v.scalar_tensor_tensor(qkvF[:, f % 2, :], f1_bank[:, 0:3 * P], rmsF[:, f, 0:1], bqkv[:], ALU.mult,
                                       ALU.add).then_inc(f_qkv_sb, 1)

            def heads(q):
                n0, n1 = VH * q // VG, VH * (q + 1) // VG
                return slice(PH + n0, PH + n1), n1 - n0, slice(n0 * P, n1 * P)

            def f_qk_mul(f, q):
                hs, nh, cs = heads(q)
                if q == 0:
                    dve.wait_ge(f_qkv_sb, f + 1)
                qkv = qkvF[:, f % 2, :]
                qq = qkv[:, 0:P].rearrange("p (h o d) -> p h o d", h=H, o=1)[:, hs].broadcast_to([P, nh, H, HD])
                kk = qkv[:, P:2 * P].rearrange("p (o g d) -> p o g d", o=1, g=H).broadcast_to([P, nh, H, HD])
                mark(("qk", q), v.tensor_tensor(prod[:, 0, cs].rearrange("p (h g d) -> p h g d", h=nh, g=H), qq, kk,
                                            ALU.mult))

            def f_qk_sum(f, q):
                hs, nh, cs = heads(q)
                after(("qk", q))
                if q == 0 and f >= 1:
                    dve.wait_ge(f_exp_done, f)
                mark(("scores", q), v.tensor_reduce(scF[:, hs, :], prod[:, 0, cs].rearrange("p (h g d) -> p h g d", h=nh, g=H),
                                            AX.X, ALU.add))

            def f_max(f):
                after(("scores", VG - 1))
                dve.wait_ge(f_qkp_ready, f + 1)
                mark("maxima", v.tensor_reduce(mxF[:], scF[:], AX.X, ALU.max))

            def f_sub(f):
                after("maxima")
                v.tensor_tensor(scF[:], scF[:], mxF[:].rearrange("p (h o) -> p h o", o=1).broadcast_to([P, H, H]),
                                ALU.subtract).then_inc(f_sc_ready, 1)

            def f_sum(f):
                dve.wait_ge(f_exp_done, f + 1)
                mark("sums", v.tensor_reduce(sumF[:], peF[:, f % 2], AX.X, ALU.add))

            def f_recip(f):
                after("sums")
                mark("1 / sums", v.reciprocal(rinF[:], sumF[:]))

            def f_av_mul(f, q):
                hs, nh, cs = heads(q)
                pp = peF[:, f % 2].rearrange("p h (o g) -> p h o g", o=1)[:, hs].broadcast_to([P, nh, HD, H])
                vv = qkvF[:, f % 2, 2 * P:].rearrange("p (o d g) -> p o d g", o=1, g=H).broadcast_to([P, nh, HD, H])
                mark(("av", q), v.tensor_tensor(prod[:, 1, cs].rearrange("p (h d g) -> p h d g", h=nh, d=HD), pp, vv,
                                            ALU.mult))

            def f_av_sum(f, q):
                hs, nh, cs = heads(q)
                after(("av", q))
                mark(("values", q), v.tensor_reduce(oF[:, hs, :], prod[:, 1, cs].rearrange("p (h d g) -> p h d g", h=nh, d=HD),
                                            AX.X, ALU.add))

            def f_o(f):
                after(("values", VG - 1))
                after("1 / sums")
                dve.wait_ge(f_avp_ready, f + 1)
                v.tensor_tensor(onF[:], oF[:], rinF[:].rearrange("p (h o) -> p h o", o=1).broadcast_to([P, H, HD]),
                                ALU.mult).then_inc(f_o_ready, 1)

            def f_z(f):
                dve.wait_ge(f_y_mm, f + 1)
                dve.wait_ge(f_hb_ready, f + 1)
                if f >= 1:
                    dve.wait_ge(f_base, f)
                    dve.wait_ge(f_ssq2, f)
                v.tensor_tensor(zF[:], f2_bank[:, 0:P], hFb[:, f % 2, :], ALU.add).then_inc(f_z_ready, 1)

            def f_lg(f):
                dve.wait_ge(f_lg_mm, f + 1)
                dve.wait_ge(f_rms2, f + 1)
                mark("gate logits", v.scalar_tensor_tensor(lgF[:], f2_bank[:, 0:E], rmsF[:, f, 1:2], bg_row[:], ALU.mult,
                                                   ALU.add))

            def f_lgmax(f):
                after("gate logits")
                v.tensor_reduce(nmF[:], lgF[:], AX.X, ALU.max, negate=True).then_inc(f_lg_ready, 1)

            def f_wt(f):
                dve.wait_ge(f_ge_done, f + 1)
                if f >= 1:
                    dve.wait_ge(f_e_sb, 2 * f)
                link(v.reciprocal(gsF[:, 1:2], gsF[:, 0:1]))
                v.tensor_scalar(wtF[:], geF[:], gsF[:, 1:2], rmsF[:, f, 1:2], ALU.mult, ALU.mult).then_inc(f_wt_ready, 1)

            def f_x2_(f):
                dve.wait_ge(f_e_sb, 2 * f + 2)
                dve.wait_ge(f_base, f + 1)
                v.tensor_reduce(x2[:, f, :], exF[:], AX.X, ALU.add).then_inc(f_x2, 1)

            def a_bn(a, k):
                dve.wait_ge((f_x2, a_x3)[k], a + 1)
                mark(("stats", k), v.bn_stats(stA[:, a, k, :], (x2[:, a, :], x3[:, a % 4, :])[k]))

            def a_aggr(a, k):
                after(("stats", k))
                v.bn_aggr(mvA[:, a, k, :], stA[:, a, k, :]).then_inc((a_var, a_var2)[k], 1)

            def a_max(a):
                dve.wait_ge(a_masked, a + 1)
                if a >= 1:
                    dve.wait_ge(a_rexp_done, a)
                mark("top", v.max(top[:], S[:, 0:(a + 1) * P]))

            def a_negmax(a):
                after("top")
                v.tensor_scalar(nmA[:], top[:, 0:1], -1.0, None, ALU.mult).then_inc(a_top, 1)

            def a_pick(a):
                if a >= 1:
                    dve.wait_ge(a_p_ready, a)
                v.match_replace(R[:, 0:(a + 1) * P], top[:], S[:, 0:(a + 1) * P], PICKED).then_inc(a_picked, 1)

            def a_sum(a):
                dve.wait_ge(a_exp_done, a + 1)
                mark("1 / sum", v.reciprocal(sumA[:, a % 2, 1:2], sumA[:, a % 2, 0:1]))

            def a_x3_(a):
                after("1 / sum")
                dve.wait_ge(a_o_mm, a + 1)
                dve.wait_ge(a_base, a + 1)
                if a >= 4:
                    dve.wait_ge(m_out, a - 3)
                v.scalar_tensor_tensor(x3[:, a % 4, :], a_bank[:, 0:P], sumA[:, a % 2, 1:2], x2b[:, a % 2, :], ALU.mult,
                                       ALU.add).then_inc(a_x3, 1)

            def a_lg(a):
                dve.wait_ge(a_lg_mm, a + 1)
                mark("router logits", v.tensor_copy(lgR[:], a_bank[:, 0:E]))

            def a_lgmax(a):
                after("router logits")
                v.tensor_reduce(nmR[:], lgR[:], AX.X, ALU.max, negate=True).then_inc(a_lg_ready, 1)

            def a_route(a):
                dve.wait_ge(a_ge_done, a + 1)
                link(v.reciprocal(suR[:, 1:2], suR[:, 0:1]))
                link(v.tensor_scalar(prR[:], peR[:], suR[:, 1:2], None, ALU.mult))
                link(v.max(tpR[:], prR[:]))
                v.tensor_scalar(suR[:, 2:3], tpR[:, 0:1], tpR[:, 1:2], 1e-20, ALU.add, ALU.add)
                link(v.max_index(ixR[:], tpR[:], prR[:]))
                link(v.tensor_copy(ifR[:], ixR[:]))
                v.reciprocal(suR[:, 3:4], suR[:, 2:3])
                link(v.tensor_scalar(mkR[:, 0, :], iota8[:], ifR[:, 0:1], None, ALU.is_equal))
                link(v.scalar_tensor_tensor(mkR[:, 1, :], iota8[:], ifR[:, 1:2], mkR[:, 0, :], ALU.is_equal, ALU.add))
                v.scalar_tensor_tensor(wtR[:, a, :], prR[:], suR[:, 3:4], mkR[:, 1, :], ALU.mult,
                                       ALU.mult).then_inc(a_w_ready, 1)

            def m_gated(m, e):
                u = m * NE + e
                dve.wait_ge(m_tanh, u + 1)
                mark("gated", v.scalar_tensor_tensor(gg[:, u % 2, :], th[:, u % 2, :], 1.0, gu_bank[u % 2][:, 0:HID],
                                                   ALU.add, ALU.mult))

            def m_hidden(m, e):
                u = m * NE + e
                after("gated")
                if u >= 2:
                    dve.wait_ge(m_y_mm, u - 1)
                v.tensor_tensor(hid[:, u % 2, :], gg[:, u % 2, :], gu_bank[u % 2][:, HID:2 * HID],
                                ALU.mult).then_inc(m_hid, 1)

            def m_sum_(m):
                dve.wait_ge(m_y_sb, 3 * m + 3)
                if m >= 2:
                    dve.wait_ge(m_out, m - 1)
                v.tensor_reduce(ysum[:, m % 2, :], exM[:, m % 2], AX.X, ALU.add).then_inc(m_sum, 1)

            for s in range(STEPS):
                if on(s - 5):
                    a_lgmax(s - 5)
                if on(s - 3):
                    f_lgmax(s - 3)
                if on(s - 6):
                    m_gated(s - 6, 8)
                if on(s - 2):
                    f_sub(s - 2)
                if on(s - 6):
                    m_hidden(s - 6, 8)
                if on(s - 3):
                    f_wt(s - 3)
                if on(s - 5):
                    a_route(s - 5)
                if on(s - 1):
                    f_x1(s - 1)
                if on(s - 5):
                    m_gated(s - 5, 0)
                if on(s - 1):
                    f_bn(s - 1)
                if on(s - 5):
                    m_hidden(s - 5, 0)
                if on(s - 1):
                    f_aggr(s - 1)
                if on(s - 7):
                    m_sum_(s - 7)
                if on(s - 3):
                    f_x2_(s - 3)
                if on(s - 5):
                    m_gated(s - 5, 1)
                if on(s - 3):
                    a_bn(s - 3, 0)
                if on(s - 5):
                    m_hidden(s - 5, 1)
                if on(s - 3):
                    a_aggr(s - 3, 0)
                if on(s - 5):
                    m_gated(s - 5, 2)
                if on(s - 4):
                    a_sum(s - 4)
                if on(s - 2):
                    f_sum(s - 2)
                if on(s - 5):
                    m_hidden(s - 5, 2)
                if on(s - 4):
                    a_x3_(s - 4)
                if on(s - 2):
                    f_av_mul(s - 2, 0)
                if on(s - 4):
                    a_bn(s - 4, 1)
                if on(s - 2):
                    f_av_sum(s - 2, 0)
                if on(s - 4):
                    a_aggr(s - 4, 1)
                if on(s - 2):
                    f_av_mul(s - 2, 1)
                if on(s - 5):
                    m_gated(s - 5, 3)
                if on(s - 1):
                    f_qkv(s - 1)
                if on(s - 2):
                    f_recip(s - 2)
                if on(s - 1):
                    f_qk_mul(s - 1, 0)
                if on(s - 5):
                    m_hidden(s - 5, 3)
                if on(s - 1):
                    f_qk_sum(s - 1, 0)
                if on(s - 2):
                    f_av_sum(s - 2, 1)
                if on(s - 5):
                    m_gated(s - 5, 4)
                if on(s - 2):
                    f_o(s - 2)
                if on(s - 5):
                    m_hidden(s - 5, 4)
                if on(s - 1):
                    f_qk_mul(s - 1, 1)
                if on(s - 3):
                    a_max(s - 3)
                if on(s - 5):
                    m_gated(s - 5, 5)
                if on(s - 2):
                    f_z(s - 2)
                if on(s - 3):
                    a_negmax(s - 3)
                if on(s - 5):
                    m_hidden(s - 5, 5)
                if on(s - 3):
                    a_pick(s - 3)
                if on(s - 5):
                    m_gated(s - 5, 6)
                    m_hidden(s - 5, 6)
                if on(s - 1):
                    f_qk_sum(s - 1, 1)
                if on(s - 5):
                    m_gated(s - 5, 7)
                if on(s - 4):
                    a_lg(s - 4)
                if on(s - 5):
                    m_hidden(s - 5, 7)
                if on(s - 1):
                    f_max(s - 1)
                if on(s - 2):
                    f_lg(s - 2)

        @block.tensor
        def _(pe):
            t = nc.tensor

            def mm(out, lhsT, rhs, start=True, stop=True):
                return t.matmul(out, lhsT, rhs, start=start, stop=stop)

            def tr(out, src, k=P):
                return t.transpose(out, src, ident[0:k, 0:k])

            pe.wait_ge(in_mod0, 16)
            pe.wait_ge(silu_rows, 1)
            mm(bank[0][:, 0:3 * P], silu_b[:, 0, :], wmod[:, 0, 0:3 * P])
            mm(bank[1][:, 0:3 * P], silu_b[:, 0, :], wmod[:, 0, 3 * P:]).then_inc(mod0_mm, 1)
            pe.wait_ge(in_mod1, 16)
            mm(bank[2][:, 0:P], silu_b[:, 1, :], wmod[:, 1, 2 * P:3 * P])
            mm(bank[2][:, P:2 * P], silu_b[:, 1, :], wmod[:, 1, 5 * P:6 * P]).then_inc(mod1_mm, 1)
            for k, c in enumerate((0, 1, 3, 4)):
                last = mm(bank[3][:, k:k + 1], wmod[:, 1, c * P:(c + 1) * P], silu_b[:, 1, 0:1])
            last.then_inc(col_mm, 1)
            pe.wait_ge(consts, 1)
            lanes = lane_rows[:].rearrange("d h e -> d (h e)")
            mm(bank[4][:, 0:P], lanes, lanes).then_inc(lane_mm, 1)
            pe.wait_ge(in_tr, 80)
            tr(bank[5][:, 0:P], w0v[:])
            tr(bank[5][:, P:2 * P], w1v[:])
            tr(bank[5][0:64, 2 * P:3 * P], wdown[:]).then_inc(tr_mm, 1)
            pe.wait_ge(tr_sb, 1)
            pe.wait_ge(bcol_ready, 1)
            mm(bank[6][:, 0:2 * P], wdownT[:], wup[:])
            mm(bank[6][:, 2 * P:4 * P], bcols[0:64, 0, :], wup[:])
            mm(bank[7][:, 0:P], w1vT[:], w1o[:])
            mm(bank[7][:, P:2 * P], bcols[:, 1, :], w1o[:]).then_inc(fold_mm, 1)

            pe.wait_ge(mod1_sb, 1)
            for q in range(4):
                if q == 2:
                    pe.wait_ge(h0_dve, 1)
                else:
                    pe.wait_ge(h0_ready, min(q + 1, 3))
                if q >= 2:
                    pe.wait_ge(hT0_sb, q - 1)
                for j in range(4 * q, 4 * q + 4):
                    last = mm(bank[2][:, 0:P], h_str[:, j, :], h_str[:, j, :], start=(j == 0), stop=(j == NB - 1))
                if q == 3:
                    last.then_inc(gram_mm, 1)
                for j in range(4):
                    last = tr(bank[q % 2][:, j * P:(j + 1) * P], h_str[:, 4 * q + j, :])
                last.then_inc(hT0_mm, 1)
            pe.wait_ge(gram_sb, 1)
            pe.wait_ge(col_sb, 1)
            pe.wait_ge(in_w0, 48)
            mm(bank[3][:, 0:P], gram[:], w0k[:]).then_inc(gramk_mm, 1)
            pe.wait_ge(gramk_sb, 1)
            mm(bank[2][:, 0:P], w0q[:], gramk[:]).then_inc(qk_mm, 1)
            pe.wait_ge(qkr_ready, 1)
            mm(bank[3][0:H, 0:H], head_cols[:], qk_r[:]).then_inc(hsc_mm, 1)
            pe.wait_ge(hT0_sb, 4)
            pe.wait_ge(hatt_ready, 1)
            mm(bank[2][0:H, 0:P], hatt[:], head_rows[:]).then_inc(hspr_mm, 1)
            pe.wait_ge(hspr_sb, 1)
            mm(bank[3][:, 0:P], head_rows[:], hspread[:]).then_inc(hmix_mm, 1)
            pe.wait_ge(hmix_sb, 1)
            mm(bank[2][:, 0:P], w0vT[:], hmix[:]).then_inc(wva_mm, 1)
            pe.wait_ge(wva_sb, 1)
            pe.wait_ge(lane_sb, 1)
            for q in range(4):
                if q == 3:
                    pe.wait_ge(prep_dve, 1)
                for j in range(4):
                    last = mm(bank[4 + q][:, j * P:(j + 1) * P], hT_str[:, 4 * q + j, :], w0vA[:])
                last.then_inc(z0_mm, 1)
            pe.wait_ge(z0_sb, 4)
            pe.wait_ge(in_1, 96)

            def f_xt(f):
                if f >= 1:
                    pe.wait_ge(f_qkv_sb, f)
                tr(f1_bank[:, 0:P], mixed[:, f, :]).then_inc(f_xt_mm, 1)

            def f_wo(f):
                pe.wait_ge(f_xt_sb, f + 1)
                mm(f1_bank[:, 0:P], xT[:], w0oG[:]).then_inc(f_wo_mm, 1)

            def f_ht(f):
                pe.wait_ge(f_h_ready, f + 1)
                tr(f1_bank[:, 0:P], hF[:]).then_inc(f_ht_mm, 1)

            def f_qkv(f):
                pe.wait_ge(f_ht_sb, f + 1)
                if f == 0:
                    pe.wait_ge(mods_first, 1)
                mm(f1_bank[:, 0:3 * P], hFT[:], wqkv[:]).then_inc(f_qkv_mm, 1)

            def f_ot(f):
                pe.wait_ge(f_o_ready, f + 1)
                if f >= 1:
                    pe.wait_ge(f_e_sb, 2 * f)
                tr(f2_bank[:, 0:P], onF[:].rearrange("p h d -> p (h d)")).then_inc(f_ot_mm, 1)

            def f_y(f):
                pe.wait_ge(f_ot_sb, f + 1)
                mm(f2_bank[:, 0:P], oFT[:], wfo[:]).then_inc(f_y_mm, 1)

            def f_zt(f):
                pe.wait_ge(f_z_ready, f + 1)
                tr(f2_bank[:, 0:P], zF[:]).then_inc(f_zt_mm, 1)

            def f_logits(f):
                pe.wait_ge(f_zt_sb, f + 1)
                mm(f2_bank[:, 0:E], zFT[:], wfgG[:]).then_inc(f_lg_mm, 1)

            def f_experts(f, half):
                if half == 0:
                    pe.wait_ge(f_lg_ready, f + 1)
                    if f == 0:
                        pe.wait_ge(wfe_ready, 1)
                else:
                    pe.wait_ge(f_e_sb, 2 * f + 1)
                mm(f2_bank[:], zFT[:],
                   wfeG[:, 4 * half:4 * half + 4, :].rearrange("p e f -> p (e f)")).then_inc(f_e_mm, 1)

            def a_ht(a, k):
                pe.wait_ge((a_n_done, a_n2_done)[k], a + 1)
                if k == 0 and a >= 1:
                    pe.wait_ge(a_x3, a)
                if k == 1 and a + 1 < NB:
                    pe.wait_ge(a_v_sb, a + 2)
                tr(a_bank[:, 0:P], nA[:, k, :]).then_inc((a_ht_mm, a_h2_mm)[k], 1)

            def a_qkv(a):
                pe.wait_ge(a_ht_sb, a + 1)
                mm(a_bank[:, 0:P], w1q[:], hAT[:])
                mm(a_bank[:, P:2 * P], w1k[:], hAT[:])
                mm(a_bank[:, 2 * P:3 * P], hAT[:], w1vo[:]).then_inc(a_qkv_mm, 1)

            def bank_free(a, k, c):
                u = att_use[a, k, c] - 2
                if u >= 0:
                    b, kk, cc = att_user[u]
                    pe.wait_ge((a_sc_sb, a_pt_sb)[kk], chunks_before[b] + cc + 1)

            def a_scores(a):
                pe.wait_ge(a_qk_sb, a + 1)
                for c, (lo, w) in enumerate(chunks(a)):
                    bank_free(a, 0, c)
                    mm(att_bank[att_use[a, 0, c] % 2][:, 0:w], qT[:], kT[:, lo:lo + w]).then_inc(a_sc_mm, 1)

            def a_wt(a, c):
                if c < len(chunks(a)):
                    lo, w = chunks(a)[c]
                    if c == 0:
                        pe.wait_ge(a_p_ready, a + 1)
                    bank_free(a, 1, c)
                    for j in range(w // P):
                        last = tr(att_bank[att_use[a, 1, c] % 2][:, j * P:(j + 1) * P],
                                  W[:, a % 2, lo + j * P:lo + (j + 1) * P])
                    last.then_inc(a_pt_mm, 1)

            def a_av(a, c):
                if c < len(chunks(a)):
                    lo, w = chunks(a)[c]
                    pe.wait_ge(a_pt_sb, chunks_before[a] + c + 1)
                    if c == 0:
                        pe.wait_ge(a_v_sb, a + 1)
                        if a >= 1:
                            pe.wait_ge(a_lg_ready, a)
                    for b in range(lo // P, (lo + w) // P):
                        last = mm(a_bank[:, 0:P], PT[:, b * P:(b + 1) * P], vA[:, b, :], start=(b == 0), stop=(b == a))
                    if c == len(chunks(a)) - 1:
                        last.then_inc(a_o_mm, 1)

            def a_lg(a):
                pe.wait_ge(a_h2_sb, a + 1)
                mm(a_bank[:, 0:E], h2T[:, a % 2, :], w1r[:]).then_inc(a_lg_mm, 1)

            def m_gu(m, e):
                u = m * NE + e
                if u == 0:
                    pe.wait_ge(prep_pool, 1)
                if u >= 2:
                    pe.wait_ge(m_hid, u - 1)
                b, x = gu_bank[u % 2], h2T[:, m % 2, :]
                for c in range(2):
                    mm(b[:, c * P:(c + 1) * P], wgate[:, e, c * P:(c + 1) * P], x)
                for c in range(2):
                    last = mm(b[:, HID + c * P:HID + (c + 1) * P], wups[:, e, c * P:(c + 1) * P], x)
                last.then_inc(m_gu_mm, 1)

            def m_down(m, e):
                u = m * NE + e
                pe.wait_ge(m_hid, u + 1)
                if e % 4 == 0 and u > 0:
                    pe.wait_ge(m_y_sb, 3 * m + e // 4)
                y = y_bank[:, (e % 4) * P:(e % 4 + 1) * P]
                mm(y, hid[:, u % 2, 0:P], wdnG[:, e, 0, :], start=True, stop=False)
                mm(y, hid[:, u % 2, P:HID], wdnG[:, e, 1, :], start=False, stop=True).then_inc(m_y_mm, 1)

            for s in range(STEPS):
                if on(s - 5):
                    m_gu(s - 5, 0)
                if on(s - 1):
                    f_wo(s - 1)
                if on(s - 3):
                    f_experts(s - 3, 1)
                if on(s - 5):
                    m_gu(s - 5, 1)
                if on(s - 4):
                    a_wt(s - 4, 0)
                if on(s - 5):
                    m_down(s - 5, 0)
                if on(s - 4):
                    a_wt(s - 4, 1)
                if on(s - 5):
                    m_gu(s - 5, 2)
                if on(s - 4):
                    a_av(s - 4, 0)
                    a_wt(s - 4, 2)
                    a_av(s - 4, 1)
                if on(s - 1):
                    f_ht(s - 1)
                if on(s - 4):
                    a_wt(s - 4, 3)
                    a_av(s - 4, 2)
                    a_av(s - 4, 3)
                if on(s - 5):
                    m_down(s - 5, 1)
                    m_gu(s - 5, 3)
                if on(s - 3):
                    a_ht(s - 3, 0)
                if on(s - 5):
                    m_down(s - 5, 2)
                if on(s - 1):
                    f_qkv(s - 1)
                if on(s - 3):
                    a_qkv(s - 3)
                if on(s - 5):
                    m_gu(s - 5, 4)
                if on(s - 3):
                    a_scores(s - 3)
                if on(s - 5):
                    m_down(s - 5, 3)
                    m_gu(s - 5, 5)
                if on(s - 2):
                    f_ot(s - 2)
                    f_y(s - 2)
                if on(s - 5):
                    m_down(s - 5, 4)
                if on(s - 4):
                    a_ht(s - 4, 1)
                if on(s - 5):
                    m_gu(s - 5, 6)
                if on(s):
                    f_xt(s)
                if on(s - 2):
                    f_zt(s - 2)
                if on(s - 5):
                    m_down(s - 5, 5)
                    m_gu(s - 5, 7)
                if on(s - 4):
                    a_lg(s - 4)
                if on(s - 2):
                    f_logits(s - 2)
                if on(s - 5):
                    m_down(s - 5, 6)
                    m_gu(s - 5, 8)
                    m_down(s - 5, 7)
                if on(s - 2):
                    f_experts(s - 2, 0)
                if on(s - 5):
                    m_down(s - 5, 8)


def kernel(**inputs):
    import numpy as np
    import concourse.bacc as bacc
    from concourse.bass_utils import run_bass_kernel_spmd

    nc = bacc.Bacc("TRN2", target_bir_lowering=False, num_devices=1)
    arrays, aps = {}, {}
    for name, a in inputs.items():
        a = np.ascontiguousarray(a)
        arrays[f"in_{name}"] = a
        aps[name] = nc.dram_tensor(f"in_{name}", a.shape, mybir.dt.from_np(a.dtype), kind="ExternalInput").ap()
    shape = inputs["L0_attn_x"].shape
    out = nc.dram_tensor("out_x", shape, F32, kind="ExternalOutput").ap()
    build(nc, aps, out)
    r = run_bass_kernel_spmd(nc, [arrays], core_ids=[0])
    return r.results[0]["out_x"]
```

```python
from contextlib import ExitStack

import concourse.bass as bass
from concourse import mybir

ALU = mybir.AluOpType
ACT = mybir.ActivationFunctionType
F32 = mybir.dt.float32
U32 = mybir.dt.uint32
AX = mybir.AxisListType

P = 128
NB = 16
H = 16
HD = P // H
E = 8
HID = 256
TOPK = 8
LN_EPS = 1e-5
RMS_EPS = 1e-6
MASKED = -1e30
PICKED = -3e38
CH = 512
FILL = 4
PH_FILL = 6
PH_FULL = 9
VG = 2


def build(nc, d, out):
    with ExitStack() as ctx:
        def sb(name, shape, dt=F32):
            return ctx.enter_context(nc.sbuf_tensor(name, shape, dt))

        def sem(name):
            return ctx.enter_context(nc.semaphore(name))

        bank = [ctx.enter_context(nc.psum_tensor(f"bank{i}", [P, CH], F32)) for i in range(8)]
        gate_bank = bank[0]
        up_bank = bank[1]
        y_bank = bank[2]
        att_bank = bank[3:5]
        a_bank = bank[5]
        f1_bank = bank[6]
        f2_bank = bank[7]

        ident = sb("ident", [P, P])
        ones = sb("ones", [P, P])
        neg_half = sb("neg_half", [P, NB])
        iota8 = sb("iota8", [P, E])
        head_rows = sb("head_rows", [H, P])
        head_cols = sb("head_cols", [P, H])
        lane_rows = sb("lane_rows", [HD, H, HD])
        same_lane = sb("same_lane", [P, P])

        S = sb("S", [P, NB * P])
        R = sb("R", [P, NB * P])
        X = sb("X", [P, NB * P])
        PT = sb("PT", [P, NB * P])
        W = sb("W", [P, 2, NB * P])

        x_blk = sb("x_blk", [P, NB, P])
        c_col = sb("c_col", [P, 2])
        wmod = W[:, 0, 0:12 * P].rearrange("p (l c) -> p l c", l=2)
        w0q = sb("w0q", [P, P])
        w0k = sb("w0k", [P, P])
        w0v = sb("w0v", [P, P])
        w0o = sb("w0o", [P, P])
        rows = sb("rows", [P, 6, P])
        bup_row = sb("bup_row", [P, 2 * P])
        bg_row = sb("bg_row", [P, E])
        cols = sb("cols", [P, 8])
        wfq = sb("wfq", [P, P])
        wdown = sb("wdown", [P, 64])
        wup = sb("wup", [64, 2 * P])
        wfo = sb("wfo", [P, P])
        wfg = sb("wfg", [P, E])
        wfe = sb("wfe", [P, E, P])
        w1q = sb("w1q", [P, P])
        w1k = sb("w1k", [P, P])
        w1v = sb("w1v", [P, P])
        w1o = sb("w1o", [P, P])
        w1r = sb("w1r", [P, E])
        wgate = sb("wgate", [P, E + 1, HID])
        wups = sb("wups", [P, E + 1, HID])
        wdn = sb("wdn", [P, E + 1, 2, P])

        silu_t = sb("silu_t", [P, 2])
        silu_c = sb("silu_c", [P, 2])
        silu_b = sb("silu_b", [P, 2, P])
        mod0 = sb("mod0", [P, 6, P])
        mod1 = sb("mod1", [P, 2, P])
        mcol = sb("mcol", [P, 4])
        gsign = W[:, 1, 0:4 * P].rearrange("p (k f) -> p k f", k=4)
        gmag = W[:, 1, 4 * P:8 * P].rearrange("p (k f) -> p k f", k=4)
        w0oG = sb("w0oG", [P, P])
        bo0G = sb("bo0G", [P, P])
        w0vT = sb("w0vT", [P, P])
        wdownT = sb("wdownT", [64, P])
        wqkv = sb("wqkv", [P, 3 * P])
        bqkv = sb("bqkv", [P, 3 * P])
        bkv = sb("bkv", [P, 2 * P])
        bcols = sb("bcols", [P, 2, P])
        wfeG = wfe
        wfgG = sb("wfgG", [P, E])
        w1vT = sb("w1vT", [P, P])
        w1vo = sb("w1vo", [P, P])
        bvo = sb("bvo", [P, P])
        bo1G = sb("bo1G", [P, P])
        wdnG = wdn

        hid = sb("hid", [P, 2, 2 * HID])

        st0 = sb("st0", [P, NB, 6])
        mv0 = sb("mv0", [P, NB, 2])
        rs0 = sb("rs0", [P, NB])
        x_str, h_tmp, h_str, hT_str = (
            t[:].rearrange("p (j f) -> p j f", j=NB) for t in (S, R, X, PT))
        gram, gramk, qk_m, hmix = (hid[:, 0, k * P:(k + 1) * P] for k in range(4))
        qk_r = sb("qk_r", [P, H])
        hsc = sb("hsc", [H, H])
        hmx = sb("hmx", [H, 4])
        hatt = sb("hatt", [H, H])
        hspread = sb("hspread", [H, P])
        w0vA = sb("w0vA", [P, P])
        mixed = sb("mixed", [P, NB, P])

        xT = sb("xT", [P, P])
        x1 = x_blk
        stF = sb("stF", [P, NB, 6])
        mvF = sb("mvF", [P, NB, 2])
        rsF = sb("rsF", [P, NB])
        shF = sb("shF", [P, NB])
        nF = sb("nF", [P, P])
        hF1 = sb("hF1", [P, P])
        hF = sb("hF", [P, P])
        hFb = sb("hFb", [P, 2, P])
        hFT = sb("hFT", [P, P])
        sq_junk = sb("sq_junk", [P, 2, P])
        ssqF = sb("ssqF", [P, NB, 2])
        rmsF = sb("rmsF", [P, NB, 2])
        qkvF = sb("qkvF", [P, 2, 3 * P])
        prod = sb("prod", [P, 2, (H - PH_FILL) * P])
        prodP = sb("prodP", [P, 2, PH_FULL * P])
        scF = sb("scF", [P, H, H])
        mxF = sb("mxF", [P, H])
        peF = sb("peF", [P, 2, H, H])
        sumF = sb("sumF", [P, H])
        rinF = sb("rinF", [P, H])
        oF = sb("oF", [P, H, HD])
        onF = sb("onF", [P, H, HD])
        oFT = sb("oFT", [P, P])
        zF = sb("zF", [P, P])
        zg = sb("zg", [P, P])
        zFT = sb("zFT", [P, P])
        lgF = sb("lgF", [P, E])
        nmF = sb("nmF", [P, 1])
        geF = sb("geF", [P, E])
        gsF = sb("gsF", [P, 2])
        wtF = sb("wtF", [P, E])
        exF = sb("exF", [P, P, E + 1])
        x2 = x_blk

        stA = sb("stA", [P, NB, 2, 6])
        mvA = sb("mvA", [P, NB, 2, 2])
        rsA = sb("rsA", [P, NB, 2])
        shA = sb("shA", [P, NB, 2])
        nA = sb("nA", [P, 2, P])
        hAT = sb("hAT", [P, P])
        qT = sb("qT", [P, P])
        kT = sb("kT", [P, NB * P])
        vA = sb("vA", [P, NB, P])
        top = sb("top", [P, TOPK])
        nmA = sb("nmA", [P, 1])
        x2b = sb("x2b", [P, 2, P])
        x3 = sb("x3", [P, 4, P])
        sumA = sb("sumA", [P, 2, 2])
        top_e = sb("top_e", [P, TOPK])
        h2T = sb("h2T", [P, 2, P])
        lgR = sb("lgR", [P, E])
        nmR = sb("nmR", [P, 1])
        peR = sb("peR", [P, E])
        suR = sb("suR", [P, 4])
        prR = sb("prR", [P, E])
        tpR = sb("tpR", [P, E])
        ixR = sb("ixR", [P, E], U32)
        ifR = sb("ifR", [P, E])
        mkR = sb("mkR", [P, 2, E])
        wtR = sb("wtR", [P, NB, E])

        th = sb("th", [P, 2 * HID])
        gg = sb("gg", [P, 2 * HID])
        exM = sb("exM", [P, 2, P, E + 1])
        ysum = sb("ysum", [P, 2, P])
        x4 = sb("x4", [P, 4, P])

        in_xa, in_xb, in_x, in_c, in_mod0, in_mod1, in_tr, in_w0, in_f, in_1, in_moe, in_cols, in_rows = (
            sem(n) for n in ("in_xa", "in_xb", "in_x", "in_c", "in_mod0", "in_mod1", "in_tr", "in_w0", "in_f", "in_1",
                             "in_moe", "in_cols", "in_rows"))
        consts = sem("consts")
        pool_chain, dve_chain = sem("pool_chain"), sem("dve_chain")
        (silu_tanh, silu_rows, mod0_mm, mod0_sb, mod1_mm, mod1_sb, col_mm, col_sb, lane_mm, lane_sb, tr_mm, tr_sb,
         fold_mm, gates_ready, gates1_ready, prep_dve, prep_pool, bcol_ready, mods_first, wfe_ready) = (
            sem(n) for n in ("silu_tanh", "silu_rows", "mod0_mm", "mod0_sb", "mod1_mm", "mod1_sb", "col_mm", "col_sb",
                             "lane_mm", "lane_sb", "tr_mm", "tr_sb", "fold_mm", "gates_ready",
                             "gates1_ready", "prep_dve", "prep_pool", "bcol_ready", "mods_first", "wfe_ready"))
        (var0, rstd0, scaled0, h0_ready, h0_dve, gram_mm, gram_sb, gramk_mm, gramk_sb, qk_mm, qkr_ready, hsc_mm, hneg,
         hexp, hatt_ready, hspr_mm, hspr_sb, hmix_mm, hmix_sb, wva_mm, wva_sb, hT0_mm, hT0_sb, z0_mm, z0_sb,
         xb_ready) = (
            sem(n) for n in ("var0", "rstd0", "scaled0", "h0_ready", "h0_dve", "gram_mm", "gram_sb", "gramk_mm", "gramk_sb",
                             "qk_mm", "qkr_ready", "hsc_mm", "hneg", "hexp", "hatt_ready", "hspr_mm", "hspr_sb",
                             "hmix_mm", "hmix_sb", "wva_mm", "wva_sb", "hT0_mm", "hT0_sb", "z0_mm", "z0_sb",
                             "xb_ready"))
        (f_xt_mm, f_xt_sb, f_wo_mm, f_var, f_rstd, f_n_done, f_h_ready, f_hb_ready, f_ht_mm, f_ht_sb, f_ssq, f_rms,
         f_qkv_mm, f_qkv_sb, f_sc_ready, f_exp_done, f_o_ready, f_ot_mm, f_ot_sb, f_y_mm, f_z_ready, f_zt_mm,
         f_zt_sb, f_ssq2, f_rms2, f_lg_mm, f_lg_ready, f_ge_done, f_e_mm, f_e_sb, f_wt_ready, f_base, f_x2, f_qkp_ready,
         f_avp_ready) = (
            sem(n) for n in ("f_xt_mm", "f_xt_sb", "f_wo_mm", "f_var", "f_rstd", "f_n_done", "f_h_ready",
                             "f_hb_ready", "f_ht_mm", "f_ht_sb", "f_ssq", "f_rms", "f_qkv_mm", "f_qkv_sb",
                             "f_sc_ready", "f_exp_done", "f_o_ready", "f_ot_mm", "f_ot_sb", "f_y_mm", "f_z_ready",
                             "f_zt_mm", "f_zt_sb", "f_ssq2", "f_rms2", "f_lg_mm", "f_lg_ready", "f_ge_done",
                             "f_e_mm", "f_e_sb", "f_wt_ready", "f_base", "f_x2", "f_qkp_ready", "f_avp_ready"))
        (a_var, a_rstd, a_n_done, a_ht_mm, a_ht_sb, a_qkv_mm, a_qk_sb, a_v_sb, a_sc_mm, a_sc_sb, a_masked, a_top,
         a_exp_done, a_picked, a_p_ready, a_pt_mm, a_pt_sb, a_o_mm, a_base, a_x3, a_var2, a_rstd2, a_n2_done,
         a_h2_mm, a_h2_sb, a_lg_mm, a_lg_ready, a_ge_done, a_w_ready, a_rexp_done, a_pv_free) = (
            sem(n) for n in ("a_var", "a_rstd", "a_n_done", "a_ht_mm", "a_ht_sb", "a_qkv_mm", "a_qk_sb", "a_v_sb",
                             "a_sc_mm", "a_sc_sb", "a_masked", "a_top", "a_exp_done", "a_picked", "a_p_ready",
                             "a_pt_mm", "a_pt_sb", "a_o_mm", "a_base", "a_x3", "a_var2", "a_rstd2", "a_n2_done",
                             "a_h2_mm", "a_h2_sb", "a_lg_mm", "a_lg_ready", "a_ge_done", "a_w_ready", "a_rexp_done", "a_pv_free"))
        m_gate_mm, m_up_mm, m_tanh, m_gg, m_hid, m_y_mm, m_y_sb, m_sum, m_out = (
            sem(n) for n in ("m_gate_mm", "m_up_mm", "m_tanh", "m_gg", "m_hid", "m_y_mm", "m_y_sb", "m_sum", "m_out"))
        slot_free = [sem(f"slot_free{i}") for i in range(4)]

        NE = E + 1
        NP = (NE + 1) // 2

        def pair(p):
            return range(2 * p, min(2 * p + 2, NE)), HID * min(2, NE - 2 * p)

        def chunks(a):
            return [(c * CH, min(CH, (a + 1) * P - c * CH)) for c in range(((a + 1) * P + CH - 1) // CH)]

        chunks_before = [sum(len(chunks(b)) for b in range(a)) for a in range(NB + 1)]

        def att_uses():
            n = 0
            for s in range(NB + 1):
                for a, k in ((s - 1, 1), (s, 0)):
                    if 0 <= a < NB:
                        for c in range(len(chunks(a))):
                            yield (a, k, c), n
                            n += 1

        att_use = dict(att_uses())
        att_user = {n: key for key, n in att_use.items()}

        def row(ap, n):
            return ap.rearrange("(o n) -> o n", o=1).broadcast_to([P, n])

        def over_blocks(ap, n):
            return ap.rearrange("p (o f) -> p o f", o=1).broadcast_to([P, n, P])

        STEPS = NB + 7

        def pool_heads(f):
            return PH_FILL if f < FILL else PH_FULL

        def on(b):
            return 0 <= b < NB

        block = ctx.enter_context(nc.Block())

        @block.sync
        def _(sp):
            x = d["L0_attn_x"].rearrange("o t f -> (o t) f")
            sp.dma_start(x_str[:, 0:8, :], x.rearrange("(r j) f -> r j f", j=NB)[:, 0:8, :]).then_inc(in_xa, 16)
            sp.dma_start(x_str[:, 8:16, :], x.rearrange("(r j) f -> r j f", j=NB)[:, 8:16, :]).then_inc(in_xb, 16)
            for t, n in ((w0v, "L0_attn_Wv"), (wdown, "L0_ffn_Wdown"), (wup, "L0_ffn_Wup"), (w1v, "L1_attn_Wv"),
                         (w1o, "L1_attn_Wo")):
                sp.dma_start(t[:], d[n]).then_inc(in_tr, 16)
            for t, n in ((w0q, "L0_attn_Wq"), (w0k, "L0_attn_Wk"), (w0o, "L0_attn_Wo")):
                sp.dma_start(t[:], d[n]).then_inc(in_w0, 16)
            sp.dma_start(bup_row[:], row(d["L0_ffn_bup"], 2 * P)).then_inc(in_rows, 16)
            for k, name in enumerate(("L0_attn_bo", "L0_ffn_bq", "L0_ffn_bo", "L1_attn_bo")):
                sp.dma_start(rows[:, k, :], row(d[name], P)).then_inc(in_rows, 16)
            for t, n in ((wfq, "L0_ffn_Wq"), (wfo, "L0_ffn_Wo"), (wfg, "L0_ffn_Wg")):
                sp.dma_start(t[:], d[n]).then_inc(in_f, 16)
            sp.dma_start(x_blk[:], x.rearrange("(j r) f -> r j f", r=P)).then_inc(in_x, 16)
            sp.dma_start(wfe[:], d["L0_ffn_We"].rearrange("e i f -> i e f")).then_inc(in_f, 16)
            for k, name in ((3, "L1_attn_bq"), (4, "L1_attn_bk")):
                sp.dma_start(cols[:, k:k + 1], d[name].rearrange("(f o) -> f o", o=1)).then_inc(in_1, 16)
            for t, n in ((w1q, "L1_attn_Wq"), (w1k, "L1_attn_Wk"), (w1r, "L1_ffn_gate_w")):
                sp.dma_start(t[:], d[n]).then_inc(in_1, 16)
            sp.dma_start(bg_row[:], row(d["L0_ffn_bg"], E)).then_inc(in_1, 16)
            sp.dma_start(wgate[:, 0:E, :], d["L1_ffn_w_gate"].rearrange("e i f -> i e f")).then_inc(in_moe, 16)
            sp.dma_start(wups[:, 0:E, :], d["L1_ffn_w_up"].rearrange("e i f -> i e f")).then_inc(in_moe, 16)
            sp.dma_start(wdn[:, 0:E, :, :],
                         d["L1_ffn_w_down"].rearrange("e (c r) f -> r e c f", r=P)).then_inc(in_moe, 16)
            sp.dma_start(wgate[:, E, :], d["L1_ffn_ws_gate"]).then_inc(in_moe, 16)
            sp.dma_start(wups[:, E, :], d["L1_ffn_ws_up"]).then_inc(in_moe, 16)
            sp.dma_start(wdn[:, E, :, :], d["L1_ffn_ws_down"].rearrange("(c r) f -> r c f", r=P)).then_inc(in_moe, 16)
            o = out.rearrange("o (b r) f -> (o b) r f", r=P)
            for m in range(NB):
                sp.wait_ge(m_out, m + 1)
                sp.dma_start(o[m], x4[:, m % 4, :]).then_inc(slot_free[m % 4], 16)
            for k in range(4):
                sp.wait_ge(slot_free[k], 16 * NB // 4)

        @block.gpsimd
        def _(pool):
            n = [0]

            def link(ins):
                n[0] += 1
                ins.then_inc(pool_chain, 1)
                pool.wait_ge(pool_chain, n[0])

            g = nc.gpsimd
            g.memset(ones[:], 1.0)
            g.memset(neg_half[:], -0.5)
            g.memset(head_rows[:], 1.0)
            g.memset(head_cols[:], 1.0)
            g.memset(lane_rows[:], 0.0)
            link(g.memset(ident[:], 0.0))
            g.affine_select(out=ident[:], in_=ident[:], compare_op=ALU.not_equal, fill=1.0, base=0,
                            pattern=[[-1, P]], channel_multiplier=1)
            g.affine_select(out=head_rows[:], in_=head_rows[:], compare_op=ALU.is_ge, fill=0.0, base=0,
                            pattern=[[1, P]], channel_multiplier=-HD)
            g.affine_select(out=head_cols[:], in_=head_cols[:], compare_op=ALU.is_ge, fill=0.0, base=0,
                            pattern=[[-HD, H]], channel_multiplier=1)
            link(g.affine_select(out=lane_rows[:], in_=lane_rows[:], compare_op=ALU.not_equal, fill=1.0, base=0,
                                 pattern=[[0, H], [1, HD]], channel_multiplier=-1))
            g.affine_select(out=head_rows[:], in_=head_rows[:], compare_op=ALU.is_ge, fill=0.0, base=HD - 1,
                            pattern=[[-1, P]], channel_multiplier=HD)
            g.affine_select(out=head_cols[:], in_=head_cols[:], compare_op=ALU.is_ge, fill=0.0, base=HD - 1,
                            pattern=[[HD, H]], channel_multiplier=-1)
            g.iota(iota8[:], pattern=[[1, E]], base=0, channel_multiplier=0,
                   allow_small_or_imprecise_dtypes=True).then_inc(consts, 1)

            def rsqrt(out, var, scale, eps, done):
                link(g.tensor_scalar(out, var, scale, eps, ALU.mult, ALU.add))
                g.tensor_tensor(out, out, neg_half[:, 0:out.shape[1]], ALU.pow).then_inc(done, 1)

            at = {}

            def mark(what, ins):
                n[0] += 1
                ins.then_inc(pool_chain, 1)
                at[what] = n[0]

            def after(what):
                pool.wait_ge(pool_chain, at[what])

            def norm(step, name, rs, shift, mv, done):
                if step == 0:
                    mark(name, g.tensor_scalar(rs, mv[:, 1:2], 1.0, LN_EPS, ALU.mult, ALU.add))
                elif step == 1:
                    after(name)
                    mark(name, g.tensor_tensor(rs, rs, neg_half[:, 0:1], ALU.pow))
                else:
                    after(name)
                    g.tensor_scalar(shift, mv[:, 0:1], rs, -1.0, ALU.mult, ALU.mult).then_inc(done, 1)

            for k in range(2):
                j = slice(8 * k, 8 * k + 8)
                pool.wait_ge(var0, k + 1)
                rsqrt(rs0[:, j], mv0[:, j, 1], 1.0, LN_EPS, rstd0)
            pool.wait_ge(in_cols, 64)
            g.tensor_scalar(bcols[:, 1, :], ones[:], cols[:, 5:6], None, ALU.mult)
            g.tensor_scalar(bcols[0:64, 0, :], ones[0:64, :], cols[0:64, 2:3], None, ALU.mult).then_inc(bcol_ready, 1)
            for q in (0, 1, 3):
                pool.wait_ge(scaled0, q + 1)
                j = slice(4 * q, 4 * q + 4)
                g.tensor_tensor(h_str[:, j, :], h_tmp[:, j, :], over_blocks(mod0[:, 0, :], 4),
                                ALU.add).then_inc(h0_ready, 1)
            pool.wait_ge(in_x, 16)
            pool.wait_ge(gates_ready, 1)
            for q in range(4):
                j = slice(4 * q, 4 * q + 4)
                g.tensor_tensor(x_blk[:, j, :], x_blk[:, j, :], over_blocks(bo0G[:], 4), ALU.add).then_inc(xb_ready, 1)
            pool.wait_ge(in_moe, 96)
            pool.wait_ge(gates1_ready, 1)
            w = wdnG[:].rearrange("p e c f -> p (e c) f")
            g.tensor_tensor(w, w, over_blocks(mod1[:, 1, :], 2 * NE), ALU.mult).then_inc(prep_pool, 1)

            def f_norm(f, step):
                if step == 0:
                    pool.wait_ge(f_var, f + 1)
                norm(step, "norm F", rsF[:, f:f + 1], shF[:, f:f + 1], mvF[:, f, :], f_rstd)

            def f_modulate(f, step):
                if step == 0:
                    pool.wait_ge(f_n_done, f + 1)
                    mark("scaled", g.tensor_tensor(hF1[:], nF[:], mod0[:, 4, :], ALU.mult))
                else:
                    if f >= 1:
                        pool.wait_ge(f_ssq, f)
                        pool.wait_ge(f_ht_mm, f)
                    after("scaled")
                    g.tensor_tensor(hF[:], hF1[:], mod0[:, 3, :], ALU.add).then_inc(f_h_ready, 1)

            def f_residual(f):
                pool.wait_ge(f_h_ready, f + 1)
                if f >= 2:
                    pool.wait_ge(f_z_ready, f - 1)
                g.tensor_tensor(hFb[:, f % 2, :], hF[:], rows[:, 2, :], ALU.add).then_inc(f_hb_ready, 1)

            def f_rms1(f, step):
                if step == 0:
                    pool.wait_ge(f_ssq, f + 1)
                    mark("rms 1", g.tensor_scalar(rmsF[:, f, 0:1], ssqF[:, f, 0:1], 1.0 / P, RMS_EPS, ALU.mult,
                                                  ALU.add))
                else:
                    after("rms 1")
                    g.tensor_tensor(rmsF[:, f, 0:1], rmsF[:, f, 0:1], neg_half[:, 0:1], ALU.pow).then_inc(f_rms, 1)

            def f_rms2_(f, step):
                if step == 0:
                    pool.wait_ge(f_ssq2, f + 1)
                    mark("rms 2", g.tensor_scalar(rmsF[:, f, 1:2], ssqF[:, f, 1:2], 1.0 / P, RMS_EPS, ALU.mult,
                                                  ALU.add))
                else:
                    after("rms 2")
                    g.tensor_tensor(rmsF[:, f, 1:2], rmsF[:, f, 1:2], neg_half[:, 0:1], ALU.pow).then_inc(f_rms2, 1)

            def halve(src, dst, n):
                return g.tensor_tensor(dst, src[:, :, :, 0:n // 2], src[:, :, :, n // 2:n], ALU.add)

            def f_qk_pool(f, step):
                qkv, nh = qkvF[:, f % 2, :], pool_heads(f)
                a = prodP[:, 0, 0:nh * P].rearrange("p (h g d) -> p h g d", h=nh, g=H)
                b = prodP[:, 1, 0:nh * P].rearrange("p (h g d) -> p h g d", h=nh, g=H)
                if step == 0:
                    pool.wait_ge(f_qkv_sb, f + 1)
                    qq = qkv[:, 0:P].rearrange("p (h o d) -> p h o d", h=H, o=1)[:, 0:nh].broadcast_to([P, nh, H, HD])
                    kk = qkv[:, P:2 * P].rearrange("p (o g d) -> p o g d", o=1, g=H).broadcast_to([P, nh, H, HD])
                    mark("pool scores", g.tensor_tensor(a, qq, kk, ALU.mult))
                    return
                after("pool scores")
                if step == 1:
                    mark("pool scores", halve(a, b[:, :, :, 0:4], 8))
                elif step == 2:
                    mark("pool scores", halve(b, a[:, :, :, 0:2], 4))
                else:
                    if f >= 1:
                        pool.wait_ge(f_exp_done, f)
                    halve(a, scF[:, 0:nh, :].rearrange("p h (g o) -> p h g o", o=1), 2).then_inc(f_qkp_ready, 1)

            def f_av_pool(f, step):
                qkv, nh = qkvF[:, f % 2, :], pool_heads(f)
                a = prodP[:, 0, 0:nh * P].rearrange("p (h d g) -> p h d g", h=nh, d=HD)
                b = prodP[:, 1, 0:nh * P].rearrange("p (h d g) -> p h d g", h=nh, d=HD)
                if step == 0:
                    pool.wait_ge(f_exp_done, f + 1)
                    pp = peF[:, f % 2].rearrange("p h (o g) -> p h o g", o=1)[:, 0:nh].broadcast_to([P, nh, HD, H])
                    vv = qkv[:, 2 * P:].rearrange("p (o d g) -> p o d g", o=1, g=H).broadcast_to([P, nh, HD, H])
                    mark("pool values", g.tensor_tensor(a, pp, vv, ALU.mult))
                    return
                after("pool values")
                if step == 1:
                    mark("pool values", halve(a, b[:, :, :, 0:8], 16))
                elif step == 2:
                    mark("pool values", halve(b, a[:, :, :, 0:4], 8))
                elif step == 3:
                    mark("pool values", halve(a, b[:, :, :, 0:2], 4))
                else:
                    if f >= 1:
                        pool.wait_ge(f_o_ready, f)
                    halve(b, oF[:, 0:nh, :].rearrange("p h (d o) -> p h d o", o=1), 2).then_inc(f_avp_ready, 1)

            def f_base_(f, step):
                if step == 0:
                    pool.wait_ge(f_z_ready, f + 1)
                    mark("gated z", g.tensor_tensor(zg[:], zF[:], mod0[:, 5, :], ALU.mult))
                else:
                    if f >= 1:
                        pool.wait_ge(f_x2, f)
                    after("gated z")
                    g.tensor_tensor(exF[:, :, E], zg[:], x1[:, f, :], ALU.add).then_inc(f_base, 1)

            def a_norm(a, k, step):
                if step == 0:
                    pool.wait_ge((a_var, a_var2)[k], a + 1)
                norm(step, ("norm A", k), rsA[:, a, k:k + 1], shA[:, a, k:k + 1], mvA[:, a, k, :],
                     (a_rstd, a_rstd2)[k])

            def a_base_(a):
                pool.wait_ge(f_x2, a + 1)
                if a == 0:
                    pool.wait_ge(prep_dve, 1)
                if a >= 2:
                    pool.wait_ge(a_x3, a - 1)
                g.tensor_tensor(x2b[:, a % 2, :], x2[:, a, :], bo1G[:], ALU.add).then_inc(a_base, 1)

            def a_mask(a):
                pool.wait_ge(a_sc_sb, chunks_before[a + 1])
                diag = S[:, a * P:(a + 1) * P]
                g.affine_select(out=diag, in_=diag, compare_op=ALU.is_ge, fill=MASKED, base=0,
                                pattern=[[-1, P]], channel_multiplier=1).then_inc(a_masked, 1)

            def a_weights(a):
                pool.wait_ge(a_rexp_done, a + 1)
                if a >= 2:
                    pool.wait_ge(a_pt_mm, chunks_before[a - 1])
                w = (a + 1) * P
                g.tensor_tensor(W[:, a % 2, 0:w], X[:, 0:w], R[:, 0:w], ALU.subtract).then_inc(a_p_ready, 1)

            def m_out_(m):
                pool.wait_ge(m_sum, m + 1)
                if m >= 4:
                    pool.wait_ge(slot_free[m % 4], 16 * (m // 4))
                g.tensor_tensor(x4[:, m % 4, :], ysum[:, m % 2, :], x3[:, m % 4, :], ALU.add).then_inc(m_out, 1)

            for s in range(STEPS):
                if on(s - 3):
                    a_norm(s - 3, 0,2)
                if on(s - 2):
                    f_av_pool(s - 2, 3)
                if on(s - 1):
                    f_rms1(s - 1, 0)
                if on(s - 2):
                    f_av_pool(s - 2, 4)
                if on(s - 1):
                    f_rms1(s - 1, 1)
                if on(s - 3):
                    a_base_(s - 3)
                if on(s - 4):
                    a_norm(s - 4, 1,0)
                if on(s - 1):
                    f_residual(s - 1)
                if on(s - 4):
                    a_norm(s - 4, 1,1)
                    a_norm(s - 4, 1,2)
                if on(s - 1):
                    f_qk_pool(s - 1, 0)
                if on(s - 3):
                    a_mask(s - 3)
                if on(s - 2):
                    f_rms2_(s - 2, 0)
                    f_rms2_(s - 2, 1)
                if on(s - 1):
                    f_qk_pool(s - 1, 1)
                if on(s - 7):
                    m_out_(s - 7)
                if on(s - 1):
                    f_qk_pool(s - 1, 2)
                if on(s - 2):
                    f_base_(s - 2, 0)
                if on(s - 1):
                    f_qk_pool(s - 1, 3)
                if on(s - 2):
                    f_base_(s - 2, 1)
                if on(s - 3):
                    a_weights(s - 3)
                if on(s - 1):
                    f_av_pool(s - 1, 0)
                if on(s):
                    f_norm(s, 0)
                    f_norm(s, 1)
                    f_norm(s, 2)
                if on(s - 1):
                    f_av_pool(s - 1, 1)
                if on(s):
                    f_modulate(s, 0)
                if on(s - 2):
                    a_norm(s - 2, 0,0)
                if on(s):
                    f_modulate(s, 1)
                if on(s - 2):
                    a_norm(s - 2, 0,1)
                if on(s - 1):
                    f_av_pool(s - 1, 2)

        @block.scalar
        def _(act):
            sc = nc.scalar
            act.dma_start(c_col[:, 0:1], d["L0_c"].rearrange("o f -> f o")).then_inc(in_c, 16)
            act.dma_start(c_col[:, 1:2], d["L1_c"].rearrange("o f -> f o")).then_inc(in_c, 16)
            act.dma_start(wmod[:, 0, :], d["L0_wmod"]).then_inc(in_mod0, 16)
            act.dma_start(wmod[:, 1, :], d["L1_wmod"]).then_inc(in_mod1, 16)
            act.wait_ge(in_c, 32)
            sc.activation(silu_t[:], c_col[:], ACT.Tanh, scale=0.5).then_inc(silu_tanh, 1)
            for k, name in ((2, "L0_ffn_bdown"), (5, "L1_attn_bv"), (0, "L0_ffn_gamma1"), (1, "L0_ffn_gamma2")):
                m = d[name].shape[0]
                act.dma_start(cols[0:m, k:k + 1], d[name].rearrange("(f o) -> f o", o=1)).then_inc(in_cols, 16)

            act.wait_ge(mod0_mm, 1)
            sc.copy(mod0[:, 0:3, :], bank[0][:, 0:3 * P].rearrange("p (c f) -> p c f", c=3))
            sc.copy(mod0[:, 3:6, :], bank[1][:, 0:3 * P].rearrange("p (c f) -> p c f", c=3)).then_inc(mod0_sb, 1)
            act.wait_ge(mod1_mm, 1)
            sc.copy(mod1[:], bank[2][:, 0:2 * P].rearrange("p (c f) -> p c f", c=2)).then_inc(mod1_sb, 1)
            act.wait_ge(col_mm, 1)
            sc.copy(mcol[:], bank[3][:, 0:4]).then_inc(col_sb, 1)
            act.wait_ge(lane_mm, 1)
            sc.copy(same_lane[:], bank[4][:, 0:P]).then_inc(lane_sb, 1)
            act.wait_ge(tr_mm, 1)
            sc.copy(wdownT[:], bank[5][0:64, 2 * P:3 * P])
            sc.copy(w1vT[:], bank[5][:, P:2 * P])
            sc.copy(w0vT[:], bank[5][:, 0:P]).then_inc(tr_sb, 1)
            for q in range(4):
                act.wait_ge(hT0_mm, q + 1)
                sc.copy(hT_str[:, 4 * q:4 * q + 4, :],
                        bank[q % 2][:].rearrange("p (j t) -> p j t", j=4)).then_inc(hT0_sb, 1)
            act.wait_ge(hneg, 1)
            sc.activation(hatt[:], hsc[:], ACT.Exp, bias=hmx[:, 1:2], scale=HD ** -0.5,
                          accum_out=hmx[:, 2:3]).then_inc(hexp, 1)
            for q in range(1, 4, 2):
                act.wait_ge(z0_mm, q + 1)
                sc.copy(mixed[:].rearrange("r a (j d) -> r j a d", j=NB)[:, 4 * q:4 * q + 4, :, :],
                        bank[4 + q][:].rearrange("r (j a d) -> r j a d", j=4, a=H)).then_inc(z0_sb, 1)

            def f_xt(f):
                act.wait_ge(f_xt_mm, f + 1)
                sc.copy(xT[:], f1_bank[:, 0:P]).then_inc(f_xt_sb, 1)

            def f_n(f):
                act.wait_ge(f_rstd, f + 1)
                if f >= 1:
                    act.wait_ge(f_h_ready, f)
                sc.activation(nF[:], x1[:, f, :], ACT.Identity, scale=rsF[:, f:f + 1],
                              bias=shF[:, f:f + 1]).then_inc(f_n_done, 1)

            def a_n(a, k):
                act.wait_ge((a_rstd, a_rstd2)[k], a + 1)
                sc.activation(nA[:, k, :], (x2[:, a, :], x3[:, a % 4, :])[k], ACT.Identity, scale=rsA[:, a, k:k + 1],
                              bias=shA[:, a, k:k + 1]).then_inc((a_n_done, a_n2_done)[k], 1)

            def f_ht(f):
                act.wait_ge(f_ht_mm, f + 1)
                sc.copy(hFT[:], f1_bank[:, 0:P]).then_inc(f_ht_sb, 1)

            def f_squares1(f):
                act.wait_ge(f_h_ready, f + 1)
                sc.activation(sq_junk[:, 0, :], hF[:], ACT.Square, accum_out=ssqF[:, f, 0:1]).then_inc(f_ssq, 1)

            def f_exp(f):
                act.wait_ge(f_sc_ready, f + 1)
                if f >= 2:
                    act.wait_ge(f_o_ready, f - 1)
                sc.activation(peF[:, f % 2], scF[:], ACT.Exp, scale=HD ** -0.5).then_inc(f_exp_done, 1)

            def f_ot(f):
                act.wait_ge(f_ot_mm, f + 1)
                sc.copy(oFT[:], f2_bank[:, 0:P]).then_inc(f_ot_sb, 1)

            def f_zt(f):
                act.wait_ge(f_zt_mm, f + 1)
                sc.copy(zFT[:], f2_bank[:, 0:P]).then_inc(f_zt_sb, 1)

            def f_squares2(f):
                act.wait_ge(f_z_ready, f + 1)
                sc.activation(sq_junk[:, 1, :], zF[:], ACT.Square, accum_out=ssqF[:, f, 1:2]).then_inc(f_ssq2, 1)

            def f_ge(f):
                act.wait_ge(f_lg_ready, f + 1)
                sc.activation(geF[:], lgF[:], ACT.Exp, bias=nmF[:], accum_out=gsF[:, 0:1]).then_inc(f_ge_done, 1)

            def f_shares(f, half):
                act.wait_ge(f_e_mm, 2 * f + half + 1)
                act.wait_ge(f_wt_ready, f + 1)
                if half == 0 and f >= 1:
                    act.wait_ge(f_x2, f)
                for i in range(4):
                    e = 4 * half + i
                    last = sc.activation(exF[:, :, e], f2_bank[:, i * P:(i + 1) * P], ACT.Identity,
                                         scale=wtF[:, e:e + 1])
                last.then_inc(f_e_sb, 1)

            def a_ht(a, k):
                act.wait_ge((a_ht_mm, a_h2_mm)[k], a + 1)
                if a == 0 and k == 0:
                    act.wait_ge(prep_dve, 1)
                if k == 1 and a >= 2:
                    act.wait_ge(m_up_mm, (a - 1) * NP)
                dst = hAT[:] if k == 0 else h2T[:, a % 2, :]
                sc.activation(dst, a_bank[:, 0:P], ACT.Identity, scale=mcol[:, 2 * k + 1:2 * k + 2],
                              bias=mcol[:, 2 * k:2 * k + 1]).then_inc((a_ht_sb, a_h2_sb)[k], 1)

            def a_qk(a):
                act.wait_ge(a_qkv_mm, a + 1)
                if a >= 1:
                    act.wait_ge(a_sc_mm, chunks_before[a])
                sc.activation(qT[:], a_bank[:, 0:P], ACT.Identity, bias=cols[:, 3:4])
                sc.activation(kT[:, a * P:(a + 1) * P], a_bank[:, P:2 * P], ACT.Identity,
                              bias=cols[:, 4:5]).then_inc(a_qk_sb, 1)

            def a_v(a):
                act.wait_ge(a_qkv_mm, a + 1)
                sc.copy(vA[:, a, :], a_bank[:, 2 * P:3 * P]).then_inc(a_v_sb, 1)

            def a_scores(a):
                if a >= 1:
                    act.wait_ge(a_picked, a)
                for c, (lo, w) in enumerate(chunks(a)):
                    act.wait_ge(a_sc_mm, chunks_before[a] + c + 1)
                    sc.mul(S[:, lo:lo + w], att_bank[att_use[a, 0, c] % 2][:, 0:w], P ** -0.5).then_inc(a_sc_sb, 1)

            def a_exp(a):
                act.wait_ge(a_top, a + 1)
                if a >= 1:
                    act.wait_ge(a_p_ready, a)
                w = (a + 1) * P
                sc.activation(X[:, 0:w], S[:, 0:w], ACT.Exp, bias=nmA[:])

            def a_top_exp(a):
                act.wait_ge(a_top, a + 1)
                if a >= 2:
                    act.wait_ge(a_x3, a - 1)
                sc.activation(top_e[:], top[:], ACT.Exp, bias=nmA[:], accum_out=sumA[:, a % 2, 0:1]).then_inc(
                    a_exp_done, 1)

            def a_rexp(a):
                act.wait_ge(a_picked, a + 1)
                w = (a + 1) * P
                sc.activation(R[:, 0:w], R[:, 0:w], ACT.Exp, bias=nmA[:]).then_inc(a_rexp_done, 1)

            def a_pt(a, c):
                if c < len(chunks(a)):
                    lo, w = chunks(a)[c]
                    act.wait_ge(a_pt_mm, chunks_before[a] + c + 1)
                    if c == 0 and a >= 1:
                        act.wait_ge(a_o_mm, a)
                    sc.copy(PT[:, lo:lo + w], att_bank[att_use[a, 1, c] % 2][:, 0:w]).then_inc(a_pt_sb, 1)

            def a_ge(a):
                act.wait_ge(a_lg_ready, a + 1)
                sc.activation(peR[:], lgR[:], ACT.Exp, bias=nmR[:], accum_out=suR[:, 0:1]).then_inc(a_ge_done, 1)

            def m_th(m, p):
                u, n_cols = m * NP + p, pair(p)[1]
                act.wait_ge(m_gate_mm, u + 1)
                if u >= 1:
                    act.wait_ge(m_gg, u)
                sc.activation(th[:, 0:n_cols], gate_bank[:, 0:n_cols], ACT.Tanh, scale=0.5).then_inc(m_tanh, 1)

            def m_shares(m, grp):
                es = (range(0, 4), range(4, 8), range(8, 9))[grp]
                act.wait_ge(m_y_mm, m * NE + es[-1] + 1)
                if grp == 0:
                    act.wait_ge(a_w_ready, m + 1)
                    if m >= 2:
                        act.wait_ge(m_sum, m - 1)
                for i, e in enumerate(es):
                    scale = wtR[:, m, e:e + 1] if e < E else 1.0
                    last = sc.activation(exM[:, m % 2, :, e], y_bank[:, i * P:(i + 1) * P], ACT.Identity, scale=scale)
                last.then_inc(m_y_sb, 1)

            for s in range(STEPS):
                if on(s - 1):
                    f_ht(s - 1)
                    f_squares1(s - 1)
                if on(s - 3):
                    a_n(s - 3, 0)
                    a_ht(s - 3, 0)
                if on(s - 2):
                    f_ot(s - 2)
                if on(s - 5):
                    m_th(s - 5, 1)
                if on(s - 3):
                    a_qk(s - 3)
                    a_v(s - 3)
                if on(s - 4):
                    a_n(s - 4, 1)
                if on(s - 3):
                    a_scores(s - 3)
                if on(s - 2):
                    f_zt(s - 2)
                    f_squares2(s - 2)
                if on(s - 6):
                    m_shares(s - 6, 2)
                if on(s - 4):
                    a_ht(s - 4, 1)
                if on(s - 5):
                    m_th(s - 5, 2)
                if on(s - 2):
                    f_ge(s - 2)
                if on(s - 3):
                    a_exp(s - 3)
                    a_top_exp(s - 3)
                    a_rexp(s - 3)
                if on(s - 2):
                    f_shares(s - 2, 0)
                if on(s - 5):
                    m_th(s - 5, 3)
                if on(s - 4):
                    a_ge(s - 4)
                if on(s - 1):
                    f_exp(s - 1)
                if on(s):
                    f_xt(s)
                if on(s - 5):
                    m_shares(s - 5, 0)
                if on(s - 2):
                    f_shares(s - 2, 1)
                if on(s - 5):
                    m_th(s - 5, 4)
                if on(s - 3):
                    a_pt(s - 3, 0)
                if on(s):
                    f_n(s)
                if on(s - 3):
                    a_pt(s - 3, 1)
                if on(s - 4):
                    m_th(s - 4, 0)
                if on(s - 3):
                    a_pt(s - 3, 2)
                    a_pt(s - 3, 3)
                if on(s - 5):
                    m_shares(s - 5, 1)

        @block.vector
        def _(dve):
            n = [0]

            def link(ins):
                n[0] += 1
                ins.then_inc(dve_chain, 1)
                dve.wait_ge(dve_chain, n[0])

            v = nc.vector

            at = {}

            def mark(what, ins):
                n[0] += 1
                ins.then_inc(dve_chain, 1)
                at[what] = n[0]

            def after(what):
                dve.wait_ge(dve_chain, at[what])

            def stats0(k):
                dve.wait_ge((in_xa, in_xb)[k], 16)
                for j in range(8 * k, 8 * k + 8):
                    last = v.bn_stats(st0[:, j, :], x_str[:, j, :])
                link(last)
                for j in range(8 * k, 8 * k + 8):
                    last = v.bn_aggr(mv0[:, j, :], st0[:, j, :])
                last.then_inc(var0, 1)

            def normalise0(j0, j1):
                for j in range(j0, j1):
                    last = v.tensor_scalar(h_tmp[:, j, :], x_str[:, j, :], mv0[:, j, 0:1], rs0[:, j:j + 1],
                                           ALU.subtract, ALU.mult)
                mark("n0", last)

            stats0(0)
            dve.wait_ge(silu_tanh, 1)
            dve.wait_ge(consts, 1)
            link(v.scalar_tensor_tensor(silu_c[:], silu_t[:], 1.0, c_col[:], ALU.add, ALU.mult))
            v.tensor_scalar(silu_b[:, 0, :], ones[:], silu_c[:, 0:1], 0.5, ALU.mult, ALU.mult)
            v.tensor_scalar(silu_b[:, 1, :], ones[:], silu_c[:, 1:2], 0.5, ALU.mult, ALU.mult).then_inc(silu_rows, 1)
            stats0(1)
            dve.wait_ge(var0, 2)
            dve.wait_ge(rstd0, 1)
            normalise0(0, 8)
            dve.wait_ge(rstd0, 2)
            normalise0(8, NB)
            dve.wait_ge(mod0_sb, 1)
            mark("1 + ca", v.tensor_scalar(mod0[:, 1, :], mod0[:, 1, :], 1.0, None, ALU.add))
            v.tensor_scalar(mod0[:, 4, :], mod0[:, 4, :], 1.0, None, ALU.add)
            after("n0")
            after("1 + ca")
            for q in range(4):
                j = slice(4 * q, 4 * q + 4)
                v.tensor_tensor(h_tmp[:, j, :], h_tmp[:, j, :], over_blocks(mod0[:, 1, :], 4),
                                ALU.mult).then_inc(scaled0, 1)
            dve.wait_ge(scaled0, 3)
            v.tensor_tensor(h_str[:, 8:12, :], h_tmp[:, 8:12, :], over_blocks(mod0[:, 0, :], 4),
                            ALU.add).then_inc(h0_dve, 1)

            def gate(src, k, step):
                if step == 0:
                    v.tensor_scalar(gsign[:, k, :], src, 0.0, 2.0, ALU.is_ge, ALU.mult)
                    mark(("gate", k), v.scalar_tensor_tensor(gmag[:, k, :], src, -1.0, src, ALU.mult, ALU.max))
                elif step == 1:
                    after(("gate", k))
                    mark(("gate", k), v.tensor_scalar(gmag[:, k, :], gmag[:, k, :], 0.25, None, ALU.max))
                else:
                    after(("gate", k))
                    mark(("gate", k), v.scalar_tensor_tensor(src, gsign[:, k, :], 1.0, gmag[:, k, :], ALU.subtract,
                                                             ALU.mult))

            for step in range(3):
                gate(mod0[:, 2, :], 0, step)
                gate(mod0[:, 5, :], 1, step)
            dve.wait_ge(in_rows, 16 * 5)
            dve.wait_ge(in_w0, 48)
            after(("gate", 0))
            v.tensor_tensor(bo0G[:], rows[:, 0, :], mod0[:, 2, :], ALU.mult)
            v.tensor_tensor(w0oG[:], w0o[:], mod0[:, 2, :], ALU.mult).then_inc(gates_ready, 1)

            dve.wait_ge(gram_mm, 1)
            v.tensor_copy(gram, bank[2][:, 0:P]).then_inc(gram_sb, 1)
            dve.wait_ge(fold_mm, 1)
            dve.wait_ge(in_cols, 64)
            wkv = bank[6][:, 0:2 * P].rearrange("p (g k d) -> p k g d", g=H, k=2)
            v.tensor_scalar(wqkv[:, P:2 * P].rearrange("p (g d) -> p g d", g=H), wkv[:, 0], cols[:, 0:1], None,
                            ALU.mult)
            v.tensor_scalar(wqkv[:, 2 * P:].rearrange("p (d g) -> p g d", g=H), wkv[:, 1], cols[:, 0:1], None,
                            ALU.mult)
            dve.wait_ge(gramk_mm, 1)
            v.tensor_copy(gramk, bank[3][:, 0:P]).then_inc(gramk_sb, 1)
            mark("bkv", v.tensor_tensor(bkv[:], bank[6][:, 2 * P:4 * P], bup_row[:], ALU.add))
            v.tensor_copy(bqkv[:, 0:P], rows[:, 1, :])
            dve.wait_ge(qk_mm, 1)
            dve.wait_ge(lane_sb, 1)
            link(v.tensor_tensor(qk_m, bank[2][:, 0:P], same_lane[:], ALU.mult))
            v.tensor_reduce(qk_r[:], qk_m.rearrange("p (b d) -> p b d", d=HD), AX.X, ALU.add).then_inc(qkr_ready, 1)
            after("bkv")
            bk = bkv[:].rearrange("p (g k d) -> p k g d", g=H, k=2)
            v.tensor_copy(bqkv[:, P:2 * P].rearrange("p (g d) -> p g d", g=H), bk[:, 0])
            v.tensor_copy(bqkv[:, 2 * P:].rearrange("p (d g) -> p g d", g=H), bk[:, 1])
            dve.wait_ge(hsc_mm, 1)
            link(v.tensor_copy(hsc[:], bank[3][0:H, 0:H]))
            link(v.tensor_reduce(hmx[:, 0:1], hsc[:], AX.X, ALU.max))
            v.tensor_scalar(hmx[:, 1:2], hmx[:, 0:1], -HD ** -0.5, None, ALU.mult).then_inc(hneg, 1)
            dve.wait_ge(mod1_sb, 1)
            dve.wait_ge(col_sb, 1)
            gate(mod1[:, 0, :], 2, 0)
            dve.wait_ge(hexp, 1)
            link(v.reciprocal(hmx[:, 3:4], hmx[:, 2:3]))
            v.tensor_scalar(hatt[:], hatt[:], hmx[:, 3:4], None, ALU.mult).then_inc(hatt_ready, 1)
            gate(mod1[:, 1, :], 3, 0)
            dve.wait_ge(hspr_mm, 1)
            v.tensor_copy(hspread[:], bank[2][0:H, 0:P]).then_inc(hspr_sb, 1)
            gate(mod1[:, 0, :], 2, 1)
            gate(mod1[:, 1, :], 3, 1)
            dve.wait_ge(hmix_mm, 1)
            v.tensor_tensor(hmix, bank[3][:, 0:P], same_lane[:], ALU.mult).then_inc(hmix_sb, 1)
            gate(mod1[:, 0, :], 2, 2)
            gate(mod1[:, 1, :], 3, 2)
            dve.wait_ge(wva_mm, 1)
            v.tensor_copy(w0vA[:], bank[2][:, 0:P]).then_inc(wva_sb, 1)
            after(("gate", 2))
            v.tensor_tensor(w1vo[:], bank[7][:, 0:P], mod1[:, 0, :], ALU.mult)
            mark("bvo", v.tensor_tensor(bvo[:], bank[7][:, P:2 * P], rows[:, 3, :], ALU.add))
            after(("gate", 3))
            v.tensor_scalar(mod1[:, 1, :], mod1[:, 1, :], 0.5, None, ALU.mult).then_inc(gates1_ready, 1)
            v.tensor_scalar(mcol[:, 1:2], mcol[:, 1:2], 1.0, None, ALU.add)
            v.tensor_scalar(mcol[:, 3:4], mcol[:, 3:4], 1.0, None, ALU.add)
            after("bvo")
            v.tensor_tensor(bo1G[:], bvo[:], mod1[:, 0, :], ALU.mult).then_inc(prep_dve, 1)
            dve.wait_ge(in_f, 64)
            v.tensor_scalar(wqkv[:, 0:P], wfq[:], cols[:, 0:1], None, ALU.mult).then_inc(mods_first, 1)
            dve.wait_ge(z0_mm, 1)
            v.tensor_copy(mixed[:].rearrange("r a (j d) -> r j a d", j=NB)[:, 0:4, :, :],
                          bank[4][:].rearrange("r (j a d) -> r j a d", j=4, a=H)).then_inc(z0_sb, 1)
            v.tensor_scalar(wfgG[:], wfg[:], cols[:, 1:2], None, ALU.mult)
            after(("gate", 1))
            v.scalar_tensor_tensor(wfeG[:], wfe[:], cols[:, 1:2], over_blocks(mod0[:, 5, :], E), ALU.mult,
                                   ALU.mult).then_inc(wfe_ready, 1)
            dve.wait_ge(z0_mm, 3)
            v.tensor_copy(mixed[:].rearrange("r a (j d) -> r j a d", j=NB)[:, 8:12, :, :],
                          bank[6][:].rearrange("r (j a d) -> r j a d", j=4, a=H)).then_inc(z0_sb, 1)

            def f_x1(f):
                dve.wait_ge(f_wo_mm, f + 1)
                dve.wait_ge(xb_ready, f // 4 + 1)
                mark("x1", v.tensor_tensor(x1[:, f, :], f1_bank[:, 0:P], x_blk[:, f, :], ALU.add))

            def f_bn(f):
                after("x1")
                mark("x1 stats", v.bn_stats(stF[:, f, :], x1[:, f, :]))

            def f_aggr(f):
                after("x1 stats")
                v.bn_aggr(mvF[:, f, :], stF[:, f, :]).then_inc(f_var, 1)

            def f_qkv(f):
                dve.wait_ge(f_qkv_mm, f + 1)
                dve.wait_ge(f_rms, f + 1)
                if f >= 2:
                    dve.wait_ge(f_avp_ready, f - 1)
                v.scalar_tensor_tensor(qkvF[:, f % 2, :], f1_bank[:, 0:3 * P], rmsF[:, f, 0:1], bqkv[:], ALU.mult,
                                       ALU.add).then_inc(f_qkv_sb, 1)

            def heads(f, q):
                ph = pool_heads(f)
                n0, n1 = (H - ph) * q // VG, (H - ph) * (q + 1) // VG
                return slice(ph + n0, ph + n1), n1 - n0, slice(n0 * P, n1 * P)

            def f_qk_mul(f, q):
                hs, nh, cs = heads(f, q)
                if q == 0:
                    dve.wait_ge(f_qkv_sb, f + 1)
                qkv = qkvF[:, f % 2, :]
                qq = qkv[:, 0:P].rearrange("p (h o d) -> p h o d", h=H, o=1)[:, hs].broadcast_to([P, nh, H, HD])
                kk = qkv[:, P:2 * P].rearrange("p (o g d) -> p o g d", o=1, g=H).broadcast_to([P, nh, H, HD])
                mark(("qk", q), v.tensor_tensor(prod[:, 0, cs].rearrange("p (h g d) -> p h g d", h=nh, g=H), qq, kk,
                                            ALU.mult))

            def f_qk_sum(f, q):
                hs, nh, cs = heads(f, q)
                after(("qk", q))
                if q == 0 and f >= 1:
                    dve.wait_ge(f_exp_done, f)
                mark(("scores", q), v.tensor_reduce(scF[:, hs, :], prod[:, 0, cs].rearrange("p (h g d) -> p h g d", h=nh, g=H),
                                            AX.X, ALU.add))

            def f_max(f):
                after(("scores", VG - 1))
                dve.wait_ge(f_qkp_ready, f + 1)
                mark("maxima", v.tensor_reduce(mxF[:], scF[:], AX.X, ALU.max))

            def f_sub(f):
                after("maxima")
                v.tensor_tensor(scF[:], scF[:], mxF[:].rearrange("p (h o) -> p h o", o=1).broadcast_to([P, H, H]),
                                ALU.subtract).then_inc(f_sc_ready, 1)

            def f_sum(f):
                dve.wait_ge(f_exp_done, f + 1)
                mark("sums", v.tensor_reduce(sumF[:], peF[:, f % 2], AX.X, ALU.add))

            def f_recip(f):
                after("sums")
                mark("1 / sums", v.reciprocal(rinF[:], sumF[:]))

            def f_av_mul(f, q):
                hs, nh, cs = heads(f, q)
                pp = peF[:, f % 2].rearrange("p h (o g) -> p h o g", o=1)[:, hs].broadcast_to([P, nh, HD, H])
                vv = qkvF[:, f % 2, 2 * P:].rearrange("p (o d g) -> p o d g", o=1, g=H).broadcast_to([P, nh, HD, H])
                mark(("av", q), v.tensor_tensor(prod[:, 1, cs].rearrange("p (h d g) -> p h d g", h=nh, d=HD), pp, vv,
                                            ALU.mult))

            def f_av_sum(f, q):
                hs, nh, cs = heads(f, q)
                after(("av", q))
                mark(("values", q), v.tensor_reduce(oF[:, hs, :], prod[:, 1, cs].rearrange("p (h d g) -> p h d g", h=nh, d=HD),
                                            AX.X, ALU.add))

            def f_o(f):
                after(("values", VG - 1))
                after("1 / sums")
                dve.wait_ge(f_avp_ready, f + 1)
                v.tensor_tensor(onF[:], oF[:], rinF[:].rearrange("p (h o) -> p h o", o=1).broadcast_to([P, H, HD]),
                                ALU.mult).then_inc(f_o_ready, 1)

            def f_z(f):
                dve.wait_ge(f_y_mm, f + 1)
                dve.wait_ge(f_hb_ready, f + 1)
                if f >= 1:
                    dve.wait_ge(f_base, f)
                    dve.wait_ge(f_ssq2, f)
                    dve.wait_ge(f_zt_mm, f)
                v.tensor_tensor(zF[:], f2_bank[:, 0:P], hFb[:, f % 2, :], ALU.add).then_inc(f_z_ready, 1)

            def f_lg(f):
                dve.wait_ge(f_lg_mm, f + 1)
                dve.wait_ge(f_rms2, f + 1)
                mark("gate logits", v.scalar_tensor_tensor(lgF[:], f2_bank[:, 0:E], rmsF[:, f, 1:2], bg_row[:], ALU.mult,
                                                   ALU.add))

            def f_lgmax(f):
                after("gate logits")
                v.tensor_reduce(nmF[:], lgF[:], AX.X, ALU.max, negate=True).then_inc(f_lg_ready, 1)

            def f_gsum(f):
                dve.wait_ge(f_ge_done, f + 1)
                mark("1 / gates' sum", v.reciprocal(gsF[:, 1:2], gsF[:, 0:1]))

            def f_wt(f):
                if f >= 1:
                    dve.wait_ge(f_e_sb, 2 * f)
                after("1 / gates' sum")
                v.tensor_scalar(wtF[:], geF[:], gsF[:, 1:2], rmsF[:, f, 1:2], ALU.mult, ALU.mult).then_inc(f_wt_ready, 1)

            def f_x2_(f):
                dve.wait_ge(f_e_sb, 2 * f + 2)
                dve.wait_ge(f_base, f + 1)
                v.tensor_reduce(x2[:, f, :], exF[:], AX.X, ALU.add).then_inc(f_x2, 1)

            def a_bn(a, k):
                dve.wait_ge((f_x2, a_x3)[k], a + 1)
                mark(("stats", k), v.bn_stats(stA[:, a, k, :], (x2[:, a, :], x3[:, a % 4, :])[k]))

            def a_aggr(a, k):
                after(("stats", k))
                v.bn_aggr(mvA[:, a, k, :], stA[:, a, k, :]).then_inc((a_var, a_var2)[k], 1)

            def a_max(a):
                dve.wait_ge(a_masked, a + 1)
                if a >= 1:
                    dve.wait_ge(a_rexp_done, a)
                mark("top", v.max(top[:], S[:, 0:(a + 1) * P]))

            def a_negmax(a):
                after("top")
                v.tensor_scalar(nmA[:], top[:, 0:1], -1.0, None, ALU.mult).then_inc(a_top, 1)

            def a_pick(a):
                if a >= 1:
                    dve.wait_ge(a_p_ready, a)
                v.match_replace(R[:, 0:(a + 1) * P], top[:], S[:, 0:(a + 1) * P], PICKED).then_inc(a_picked, 1)

            def a_sum(a):
                dve.wait_ge(a_exp_done, a + 1)
                mark("1 / sum", v.reciprocal(sumA[:, a % 2, 1:2], sumA[:, a % 2, 0:1]))

            def a_x3_(a):
                after("1 / sum")
                dve.wait_ge(a_o_mm, a + 1)
                dve.wait_ge(a_base, a + 1)
                if a >= 4:
                    dve.wait_ge(m_out, a - 3)
                v.scalar_tensor_tensor(x3[:, a % 4, :], a_bank[:, 0:P], sumA[:, a % 2, 1:2], x2b[:, a % 2, :], ALU.mult,
                                       ALU.add).then_inc(a_x3, 1)

            def a_lg(a):
                dve.wait_ge(a_lg_mm, a + 1)
                mark("router logits", v.tensor_copy(lgR[:], a_bank[:, 0:E]))

            def a_lgmax(a):
                after("router logits")
                v.tensor_reduce(nmR[:], lgR[:], AX.X, ALU.max, negate=True).then_inc(a_lg_ready, 1)

            def a_route(a, step):
                if step == 0:
                    dve.wait_ge(a_ge_done, a + 1)
                    mark("route", v.reciprocal(suR[:, 1:2], suR[:, 0:1]))
                    return
                after("route")
                if step == 1:
                    mark("route", v.tensor_scalar(prR[:], peR[:], suR[:, 1:2], None, ALU.mult))
                elif step == 2:
                    mark("route", v.max(tpR[:], prR[:]))
                elif step == 3:
                    mark("two largest", v.tensor_scalar(suR[:, 2:3], tpR[:, 0:1], tpR[:, 1:2], 1e-20, ALU.add,
                                                        ALU.add))
                    mark("route", v.max_index(ixR[:], tpR[:], prR[:]))
                elif step == 4:
                    mark("route", v.tensor_copy(ifR[:], ixR[:]))
                    after("two largest")
                    mark("1 / two largest", v.reciprocal(suR[:, 3:4], suR[:, 2:3]))
                elif step == 5:
                    mark("route", v.tensor_scalar(mkR[:, 0, :], iota8[:], ifR[:, 0:1], None, ALU.is_equal))
                elif step == 6:
                    mark("route", v.scalar_tensor_tensor(mkR[:, 1, :], iota8[:], ifR[:, 1:2], mkR[:, 0, :],
                                                         ALU.is_equal, ALU.add))
                else:
                    after("1 / two largest")
                    v.scalar_tensor_tensor(wtR[:, a, :], prR[:], suR[:, 3:4], mkR[:, 1, :], ALU.mult,
                                           ALU.mult).then_inc(a_w_ready, 1)

            def m_gated(m, p):
                u, n_cols = m * NP + p, pair(p)[1]
                dve.wait_ge(m_tanh, u + 1)
                if u >= 1:
                    dve.wait_ge(m_hid, u)
                v.scalar_tensor_tensor(gg[:, 0:n_cols], th[:, 0:n_cols], 1.0, gate_bank[:, 0:n_cols], ALU.add,
                                       ALU.mult).then_inc(m_gg, 1)

            def m_hidden(m, p):
                u, n_cols = m * NP + p, pair(p)[1]
                dve.wait_ge(m_gg, u + 1)
                dve.wait_ge(m_up_mm, u + 1)
                if u >= 2:
                    b, q = divmod(u - 2, NP)
                    dve.wait_ge(m_y_mm, b * NE + pair(q)[0][-1] + 1)
                v.tensor_tensor(hid[:, u % 2, 0:n_cols], gg[:, 0:n_cols], up_bank[:, 0:n_cols],
                                ALU.mult).then_inc(m_hid, 1)

            def m_sum_(m):
                dve.wait_ge(m_y_sb, 3 * m + 3)
                if m >= 2:
                    dve.wait_ge(m_out, m - 1)
                v.tensor_reduce(ysum[:, m % 2, :], exM[:, m % 2], AX.X, ALU.add).then_inc(m_sum, 1)

            for s in range(STEPS):
                if on(s - 5):
                    m_gated(s - 5, 0)
                if on(s - 4):
                    a_sum(s - 4)
                if on(s - 2):
                    f_av_mul(s - 2, 1)
                if on(s - 4):
                    a_x3_(s - 4)
                if on(s - 2):
                    f_av_sum(s - 2, 1)
                    f_recip(s - 2)
                if on(s - 4):
                    a_bn(s - 4, 1)
                if on(s - 2):
                    f_o(s - 2)
                if on(s - 4):
                    a_aggr(s - 4, 1)
                if on(s - 5):
                    m_hidden(s - 5, 0)
                if on(s - 1):
                    f_qkv(s - 1)
                    f_qk_mul(s - 1, 0)
                if on(s - 5):
                    m_gated(s - 5, 1)
                if on(s - 2):
                    f_z(s - 2)
                if on(s - 1):
                    f_qk_sum(s - 1, 0)
                    f_qk_mul(s - 1, 1)
                if on(s - 7):
                    m_sum_(s - 7)
                if on(s - 5):
                    m_hidden(s - 5, 1)
                if on(s - 3):
                    a_max(s - 3)
                if on(s - 2):
                    f_lg(s - 2)
                if on(s - 4):
                    a_lg(s - 4)
                if on(s - 3):
                    a_negmax(s - 3)
                if on(s - 2):
                    f_lgmax(s - 2)
                if on(s - 3):
                    a_pick(s - 3)
                if on(s - 2):
                    f_gsum(s - 2)
                if on(s - 5):
                    m_gated(s - 5, 2)
                if on(s - 2):
                    f_wt(s - 2)
                if on(s - 1):
                    f_qk_sum(s - 1, 1)
                if on(s - 5):
                    m_hidden(s - 5, 2)
                if on(s - 1):
                    f_max(s - 1)
                if on(s - 4):
                    a_lgmax(s - 4)
                if on(s - 1):
                    f_sub(s - 1)
                if on(s - 4):
                    a_route(s - 4, 0)
                if on(s - 5):
                    m_gated(s - 5, 3)
                if on(s - 4):
                    a_route(s - 4, 1)
                if on(s - 5):
                    m_hidden(s - 5, 3)
                if on(s - 4):
                    a_route(s - 4, 2)
                    a_route(s - 4, 3)
                if on(s):
                    f_x1(s)
                if on(s - 4):
                    a_route(s - 4, 4)
                if on(s):
                    f_bn(s)
                if on(s - 4):
                    a_route(s - 4, 5)
                if on(s):
                    f_aggr(s)
                if on(s - 2):
                    f_x2_(s - 2)
                if on(s - 5):
                    m_gated(s - 5, 4)
                if on(s - 1):
                    f_sum(s - 1)
                if on(s - 2):
                    a_bn(s - 2, 0)
                if on(s - 4):
                    a_route(s - 4, 6)
                if on(s - 2):
                    a_aggr(s - 2, 0)
                if on(s - 1):
                    f_av_mul(s - 1, 0)
                if on(s - 5):
                    m_hidden(s - 5, 4)
                if on(s - 1):
                    f_av_sum(s - 1, 0)
                if on(s - 4):
                    a_route(s - 4, 7)

        @block.tensor
        def _(pe):
            t = nc.tensor

            def mm(out, lhsT, rhs, start=True, stop=True):
                return t.matmul(out, lhsT, rhs, start=start, stop=stop)

            def tr(out, src, k=P):
                return t.transpose(out, src, ident[0:k, 0:k])

            pe.wait_ge(in_mod0, 16)
            pe.wait_ge(silu_rows, 1)
            mm(bank[0][:, 0:3 * P], silu_b[:, 0, :], wmod[:, 0, 0:3 * P])
            mm(bank[1][:, 0:3 * P], silu_b[:, 0, :], wmod[:, 0, 3 * P:]).then_inc(mod0_mm, 1)
            pe.wait_ge(in_mod1, 16)
            mm(bank[2][:, 0:P], silu_b[:, 1, :], wmod[:, 1, 2 * P:3 * P])
            mm(bank[2][:, P:2 * P], silu_b[:, 1, :], wmod[:, 1, 5 * P:6 * P]).then_inc(mod1_mm, 1)
            for k, c in enumerate((0, 1, 3, 4)):
                last = mm(bank[3][:, k:k + 1], wmod[:, 1, c * P:(c + 1) * P], silu_b[:, 1, 0:1])
            last.then_inc(col_mm, 1)
            pe.wait_ge(consts, 1)
            lanes = lane_rows[:].rearrange("d h e -> d (h e)")
            mm(bank[4][:, 0:P], lanes, lanes).then_inc(lane_mm, 1)
            pe.wait_ge(in_tr, 80)
            tr(bank[5][:, 0:P], w0v[:])
            tr(bank[5][:, P:2 * P], w1v[:])
            tr(bank[5][0:64, 2 * P:3 * P], wdown[:]).then_inc(tr_mm, 1)
            pe.wait_ge(tr_sb, 1)
            pe.wait_ge(bcol_ready, 1)
            mm(bank[6][:, 0:2 * P], wdownT[:], wup[:])
            mm(bank[6][:, 2 * P:4 * P], bcols[0:64, 0, :], wup[:])
            mm(bank[7][:, 0:P], w1vT[:], w1o[:])
            mm(bank[7][:, P:2 * P], bcols[:, 1, :], w1o[:]).then_inc(fold_mm, 1)

            pe.wait_ge(mod1_sb, 1)
            for q in range(4):
                if q == 2:
                    pe.wait_ge(h0_dve, 1)
                else:
                    pe.wait_ge(h0_ready, min(q + 1, 3))
                if q >= 2:
                    pe.wait_ge(hT0_sb, q - 1)
                for j in range(4 * q, 4 * q + 4):
                    last = mm(bank[2][:, 0:P], h_str[:, j, :], h_str[:, j, :], start=(j == 0), stop=(j == NB - 1))
                if q == 3:
                    last.then_inc(gram_mm, 1)
                for j in range(4):
                    last = tr(bank[q % 2][:, j * P:(j + 1) * P], h_str[:, 4 * q + j, :])
                last.then_inc(hT0_mm, 1)
            pe.wait_ge(gram_sb, 1)
            pe.wait_ge(col_sb, 1)
            pe.wait_ge(in_w0, 48)
            mm(bank[3][:, 0:P], gram, w0k[:]).then_inc(gramk_mm, 1)
            pe.wait_ge(gramk_sb, 1)
            mm(bank[2][:, 0:P], w0q[:], gramk).then_inc(qk_mm, 1)
            pe.wait_ge(qkr_ready, 1)
            mm(bank[3][0:H, 0:H], head_cols[:], qk_r[:]).then_inc(hsc_mm, 1)
            pe.wait_ge(hT0_sb, 4)
            pe.wait_ge(hatt_ready, 1)
            mm(bank[2][0:H, 0:P], hatt[:], head_rows[:]).then_inc(hspr_mm, 1)
            pe.wait_ge(hspr_sb, 1)
            mm(bank[3][:, 0:P], head_rows[:], hspread[:]).then_inc(hmix_mm, 1)
            pe.wait_ge(hmix_sb, 1)
            mm(bank[2][:, 0:P], w0vT[:], hmix).then_inc(wva_mm, 1)
            pe.wait_ge(wva_sb, 1)
            pe.wait_ge(lane_sb, 1)
            for q in range(4):
                if q == 3:
                    pe.wait_ge(prep_dve, 1)
                for j in range(4):
                    last = mm(bank[4 + q][:, j * P:(j + 1) * P], hT_str[:, 4 * q + j, :], w0vA[:])
                last.then_inc(z0_mm, 1)
            pe.wait_ge(z0_sb, 4)
            pe.wait_ge(in_1, 96)

            def f_xt(f):
                if f >= 1:
                    pe.wait_ge(f_qkv_sb, f)
                tr(f1_bank[:, 0:P], mixed[:, f, :]).then_inc(f_xt_mm, 1)

            def f_wo(f):
                pe.wait_ge(f_xt_sb, f + 1)
                mm(f1_bank[:, 0:P], xT[:], w0oG[:]).then_inc(f_wo_mm, 1)

            def f_ht(f):
                pe.wait_ge(f_h_ready, f + 1)
                tr(f1_bank[:, 0:P], hF[:]).then_inc(f_ht_mm, 1)

            def f_qkv(f):
                pe.wait_ge(f_ht_sb, f + 1)
                if f == 0:
                    pe.wait_ge(mods_first, 1)
                mm(f1_bank[:, 0:3 * P], hFT[:], wqkv[:]).then_inc(f_qkv_mm, 1)

            def f_ot(f):
                pe.wait_ge(f_o_ready, f + 1)
                if f >= 1:
                    pe.wait_ge(f_e_sb, 2 * f)
                tr(f2_bank[:, 0:P], onF[:].rearrange("p h d -> p (h d)")).then_inc(f_ot_mm, 1)

            def f_y(f):
                pe.wait_ge(f_ot_sb, f + 1)
                mm(f2_bank[:, 0:P], oFT[:], wfo[:]).then_inc(f_y_mm, 1)

            def f_zt(f):
                pe.wait_ge(f_z_ready, f + 1)
                tr(f2_bank[:, 0:P], zF[:]).then_inc(f_zt_mm, 1)

            def f_logits(f):
                pe.wait_ge(f_zt_sb, f + 1)
                mm(f2_bank[:, 0:E], zFT[:], wfgG[:]).then_inc(f_lg_mm, 1)

            def f_experts(f, half):
                if half == 0:
                    pe.wait_ge(f_lg_ready, f + 1)
                    if f == 0:
                        pe.wait_ge(wfe_ready, 1)
                else:
                    pe.wait_ge(f_e_sb, 2 * f + 1)
                mm(f2_bank[:], zFT[:],
                   wfeG[:, 4 * half:4 * half + 4, :].rearrange("p e f -> p (e f)")).then_inc(f_e_mm, 1)

            def a_ht(a, k):
                pe.wait_ge((a_n_done, a_n2_done)[k], a + 1)
                if k == 0 and a >= 1:
                    pe.wait_ge(a_x3, a)
                if k == 1 and a + 1 < NB:
                    pe.wait_ge(a_v_sb, a + 2)
                tr(a_bank[:, 0:P], nA[:, k, :]).then_inc((a_ht_mm, a_h2_mm)[k], 1)

            def a_qkv(a):
                pe.wait_ge(a_ht_sb, a + 1)
                mm(a_bank[:, 0:P], w1q[:], hAT[:])
                mm(a_bank[:, P:2 * P], w1k[:], hAT[:])
                mm(a_bank[:, 2 * P:3 * P], hAT[:], w1vo[:]).then_inc(a_qkv_mm, 1)

            def bank_free(a, k, c):
                u = att_use[a, k, c] - 2
                if u >= 0:
                    b, kk, cc = att_user[u]
                    pe.wait_ge((a_sc_sb, a_pt_sb)[kk], chunks_before[b] + cc + 1)

            def a_scores(a):
                pe.wait_ge(a_qk_sb, a + 1)
                for c, (lo, w) in enumerate(chunks(a)):
                    bank_free(a, 0, c)
                    mm(att_bank[att_use[a, 0, c] % 2][:, 0:w], qT[:], kT[:, lo:lo + w]).then_inc(a_sc_mm, 1)

            def a_wt(a, c):
                if c < len(chunks(a)):
                    lo, w = chunks(a)[c]
                    if c == 0:
                        pe.wait_ge(a_p_ready, a + 1)
                    bank_free(a, 1, c)
                    for j in range(w // P):
                        last = tr(att_bank[att_use[a, 1, c] % 2][:, j * P:(j + 1) * P],
                                  W[:, a % 2, lo + j * P:lo + (j + 1) * P])
                    last.then_inc(a_pt_mm, 1)

            def a_av(a, c):
                if c < len(chunks(a)):
                    lo, w = chunks(a)[c]
                    pe.wait_ge(a_pt_sb, chunks_before[a] + c + 1)
                    if c == 0:
                        pe.wait_ge(a_v_sb, a + 1)
                        if a >= 1:
                            pe.wait_ge(a_lg_ready, a)
                    for b in range(lo // P, (lo + w) // P):
                        last = mm(a_bank[:, 0:P], PT[:, b * P:(b + 1) * P], vA[:, b, :], start=(b == 0), stop=(b == a))
                    if c == len(chunks(a)) - 1:
                        last.then_inc(a_o_mm, 1)

            def a_lg(a):
                pe.wait_ge(a_h2_sb, a + 1)
                mm(a_bank[:, 0:E], h2T[:, a % 2, :], w1r[:]).then_inc(a_lg_mm, 1)

            def m_gate(m, p):
                u = m * NP + p
                if u == 0:
                    pe.wait_ge(prep_pool, 1)
                    pe.wait_ge(a_h2_sb, 1)
                if u >= 1:
                    pe.wait_ge(m_gg, u)
                for i, e in enumerate(pair(p)[0]):
                    for c in range(2):
                        last = mm(gate_bank[:, i * HID + c * P:i * HID + (c + 1) * P],
                                  wgate[:, e, c * P:(c + 1) * P], h2T[:, m % 2, :])
                last.then_inc(m_gate_mm, 1)

            def m_up(m, p):
                u = m * NP + p
                if u >= 1:
                    pe.wait_ge(m_hid, u)
                for i, e in enumerate(pair(p)[0]):
                    for c in range(2):
                        last = mm(up_bank[:, i * HID + c * P:i * HID + (c + 1) * P],
                                  wups[:, e, c * P:(c + 1) * P], h2T[:, m % 2, :])
                last.then_inc(m_up_mm, 1)

            def m_down(m, e):
                u, i = m * NP + e // 2, e % 2
                pe.wait_ge(m_hid, u + 1)
                if e % 4 == 0 and u > 0:
                    pe.wait_ge(m_y_sb, 3 * m + e // 4)
                y = y_bank[:, (e % 4) * P:(e % 4 + 1) * P]
                for c in range(2):
                    last = mm(y, hid[:, u % 2, i * HID + c * P:i * HID + (c + 1) * P], wdnG[:, e, c, :],
                              start=(c == 0), stop=(c == 1))
                last.then_inc(m_y_mm, 1)

            for s in range(STEPS):
                if on(s - 6):
                    m_down(s - 6, 4)
                    m_down(s - 6, 5)
                    m_down(s - 6, 6)
                    m_down(s - 6, 7)
                if on(s - 4):
                    a_wt(s - 4, 0)
                if on(s - 6):
                    m_up(s - 6, 4)
                if on(s - 4):
                    a_wt(s - 4, 1)
                if on(s - 5):
                    m_gate(s - 5, 0)
                if on(s - 4):
                    a_av(s - 4, 0)
                    a_wt(s - 4, 2)
                    a_av(s - 4, 1)
                    a_wt(s - 4, 3)
                    a_av(s - 4, 2)
                    a_av(s - 4, 3)
                if on(s - 1):
                    f_ht(s - 1)
                if on(s - 5):
                    m_up(s - 5, 0)
                if on(s - 1):
                    f_qkv(s - 1)
                if on(s - 3):
                    a_ht(s - 3, 0)
                if on(s - 5):
                    m_gate(s - 5, 1)
                if on(s - 2):
                    f_ot(s - 2)
                if on(s - 3):
                    a_qkv(s - 3)
                if on(s - 2):
                    f_y(s - 2)
                if on(s - 5):
                    m_up(s - 5, 1)
                if on(s - 3):
                    a_scores(s - 3)
                if on(s - 6):
                    m_down(s - 6, 8)
                if on(s - 2):
                    f_zt(s - 2)
                if on(s - 4):
                    a_ht(s - 4, 1)
                if on(s - 5):
                    m_gate(s - 5, 2)
                    m_down(s - 5, 0)
                if on(s):
                    f_xt(s)
                if on(s - 4):
                    a_lg(s - 4)
                if on(s - 2):
                    f_logits(s - 2)
                if on(s - 5):
                    m_down(s - 5, 1)
                    m_up(s - 5, 2)
                if on(s - 2):
                    f_experts(s - 2, 0)
                if on(s - 5):
                    m_down(s - 5, 2)
                    m_gate(s - 5, 3)
                    m_down(s - 5, 3)
                    m_up(s - 5, 3)
                if on(s - 2):
                    f_experts(s - 2, 1)
                if on(s):
                    f_wo(s)
                if on(s - 5):
                    m_gate(s - 5, 4)


def kernel(**inputs):
    import numpy as np
    import concourse.bacc as bacc
    from concourse.bass_utils import run_bass_kernel_spmd

    nc = bacc.Bacc("TRN2", target_bir_lowering=False, num_devices=1)
    arrays, aps = {}, {}
    for name, a in inputs.items():
        a = np.ascontiguousarray(a)
        arrays[f"in_{name}"] = a
        aps[name] = nc.dram_tensor(f"in_{name}", a.shape, mybir.dt.from_np(a.dtype), kind="ExternalInput").ap()
    shape = inputs["L0_attn_x"].shape
    out = nc.dram_tensor("out_x", shape, F32, kind="ExternalOutput").ap()
    build(nc, aps, out)
    r = run_bass_kernel_spmd(nc, [arrays], core_ids=[0])
    return r.results[0]["out_x"]
```
